# Optimizing a Trainium2 kernel written in Bass

```python
import numpy as np
import jax
import jax.numpy as jnp

def _softmax(x, axis=-1):
    return jax.nn.softmax(x, axis=axis)

def _gelu(x):
    return jax.nn.gelu(x, approximate=True)

def _silu(x):
    return jax.nn.silu(x)

def _sigmoid(x):
    return jax.nn.sigmoid(x)

def _layernorm(x, axis=-1, eps=1e-05):
    m = jnp.mean(x, axis=axis, keepdims=True)
    v = jnp.var(x, axis=axis, keepdims=True)
    return (x - m) / jnp.sqrt(v + eps)

def _scatter_add(tgt, idx, src, axis=0):
    return tgt.at[idx].add(src)

def _segment_sum(src, seg, n):
    return jax.ops.segment_sum(src, seg, n)
kernel_name = 'mk_sandwich_d1_jaxref_r8_0cb057'

def setup_inputs(seed: int=0):
    np.random.seed(seed)
    _w = jnp.asarray

    def _L0_attn_setup():
        import jax, jax.numpy as jnp
        import numpy as np
        import math
        EMB = 256
        HEADS = 16
        HEAD_DIM = EMB // HEADS
        SCALE = math.sqrt(HEAD_DIM)

        def srms_norm(x, eps_min=1e-12):
            d = x.shape[-1]
            xf = x.astype(jnp.float32)
            norm = jnp.linalg.norm(xf * (1.0 / math.sqrt(d)), axis=-1, keepdims=True)
            norm = jnp.maximum(norm, eps_min)
            return (xf / norm).astype(x.dtype)
        key = jax.random.key(seed)
        ks = jax.random.split(key, 6)
        x = jax.random.normal(ks[0], (4, 512, EMB), dtype=jnp.float32)
        std = 1.0 / math.sqrt(EMB)
        Wq = jax.random.normal(ks[1], (EMB, EMB), dtype=jnp.float32) * std
        Wk = jax.random.normal(ks[2], (EMB, EMB), dtype=jnp.float32) * std
        Wv = jax.random.normal(ks[3], (EMB, EMB), dtype=jnp.float32) * std
        Wu = jax.random.normal(ks[4], (EMB, EMB), dtype=jnp.float32) * std
        Wo = jax.random.normal(ks[5], (EMB, EMB), dtype=jnp.float32) * std
        return {'x': x, 'Wq': Wq, 'Wk': Wk, 'Wv': Wv, 'Wu': Wu, 'Wo': Wo}
    _L0_attn_in = _L0_attn_setup()

    def _L0_ffn_setup():
        import jax, jax.numpy as jnp
        import numpy as np
        B, T = (1, 64)
        DIM = 256
        MOE_INTER = 176
        N_EXPERTS = 64
        TOPK = 6
        N_SHARED = 2
        SHARED_INTER = N_SHARED * MOE_INTER
        CAPACITY = 128
        ROUTE_SCALE = 1.0
        key = jax.random.key(seed)
        ks = jax.random.split(key, 8)

        def w(k, shape, fan_in):
            return jax.random.normal(k, shape, jnp.float32) * fan_in ** (-0.5)
        return {'x': jax.random.normal(ks[0], (B, T, DIM), jnp.float32), 'gate_w': w(ks[1], (N_EXPERTS, DIM), DIM), 'w1': w(ks[2], (N_EXPERTS, MOE_INTER, DIM), DIM), 'w2': w(ks[3], (N_EXPERTS, DIM, MOE_INTER), MOE_INTER), 'w3': w(ks[4], (N_EXPERTS, MOE_INTER, DIM), DIM), 'sw1': w(ks[5], (SHARED_INTER, DIM), DIM), 'sw2': w(ks[6], (DIM, SHARED_INTER), SHARED_INTER), 'sw3': w(ks[7], (SHARED_INTER, DIM), DIM)}
    _L0_ffn_in = _L0_ffn_setup()
    _d = {'L0_attn_x': _L0_attn_in['x'], 'L0_attn_Wq': _L0_attn_in['Wq'], 'L0_attn_Wk': _L0_attn_in['Wk'], 'L0_attn_Wv': _L0_attn_in['Wv'], 'L0_attn_Wu': _L0_attn_in['Wu'], 'L0_attn_Wo': _L0_attn_in['Wo'], 'L0_ffn_gate_w': _L0_ffn_in['gate_w'], 'L0_ffn_w1': _L0_ffn_in['w1'], 'L0_ffn_w2': _L0_ffn_in['w2'], 'L0_ffn_w3': _L0_ffn_in['w3'], 'L0_ffn_sw1': _L0_ffn_in['sw1'], 'L0_ffn_sw2': _L0_ffn_in['sw2'], 'L0_ffn_sw3': _L0_ffn_in['sw3']}
    _x0 = _d['L0_attn_x']
    _d['L0_attn_x'] = jax.random.normal(jax.random.fold_in(jax.random.key(seed), 1), (8, 512, 256), dtype=_x0.dtype)
    del _x0
    return _d

def reference(L0_attn_x, L0_attn_Wq, L0_attn_Wk, L0_attn_Wv, L0_attn_Wu, L0_attn_Wo, L0_ffn_gate_w, L0_ffn_w1, L0_ffn_w2, L0_ffn_w3, L0_ffn_sw1, L0_ffn_sw2, L0_ffn_sw3):

    def _L0_attn_ref(x, Wq, Wk, Wv, Wu, Wo):
        import jax, jax.numpy as jnp
        import numpy as np
        import math
        EMB = 256
        HEADS = 16
        HEAD_DIM = EMB // HEADS
        SCALE = math.sqrt(HEAD_DIM)

        def srms_norm(x, eps_min=1e-12):
            d = x.shape[-1]
            xf = x.astype(jnp.float32)
            norm = jnp.linalg.norm(xf * (1.0 / math.sqrt(d)), axis=-1, keepdims=True)
            norm = jnp.maximum(norm, eps_min)
            return (xf / norm).astype(x.dtype)
        B, L, D = x.shape
        H, dh = (HEADS, HEAD_DIM)
        q = (x @ Wq).reshape(B, L, H, dh).transpose(0, 2, 1, 3)
        k = (x @ Wk).reshape(B, L, H, dh).transpose(0, 2, 1, 3)
        v = (x @ Wv).reshape(B, L, H, dh).transpose(0, 2, 1, 3)
        u = (x @ Wu).reshape(B, L, H, dh).transpose(0, 2, 1, 3)
        q = jax.nn.relu(q) / SCALE
        k = jax.nn.relu(k) / SCALE
        u = jax.nn.silu(u)
        kv = jnp.einsum('bhlk,bhlv->bhkv', k, v)
        out = jnp.einsum('bhlk,bhkv->bhlv', q, kv)
        out = srms_norm(out) * u
        out = out.transpose(0, 2, 1, 3).reshape(B, L, D)
        return out @ Wo

    def _L0_ffn_ref(x, gate_w, w1, w2, w3, sw1, sw2, sw3):
        import jax, jax.numpy as jnp
        import numpy as np
        B, T = (1, 64)
        DIM = 256
        MOE_INTER = 176
        N_EXPERTS = 64
        TOPK = 6
        N_SHARED = 2
        SHARED_INTER = N_SHARED * MOE_INTER
        CAPACITY = 128
        ROUTE_SCALE = 1.0
        Bb, Tt, D = x.shape
        xf = x.reshape(-1, D)
        N = xf.shape[0]
        logits = xf @ gate_w.T
        scores = jax.nn.softmax(logits, axis=-1)
        gate_vals, idx = jax.lax.top_k(scores, TOPK)
        gate_vals = gate_vals * ROUTE_SCALE
        E = gate_w.shape[0]
        fe = idx.reshape(-1)
        ft = jnp.repeat(jnp.arange(N), TOPK)
        onehot = (fe[:, None] == jnp.arange(E)[None, :]).astype(jnp.int32)
        pos = jnp.take_along_axis(jnp.cumsum(onehot, axis=0) - 1, fe[:, None], axis=1)[:, 0]
        keep = pos < CAPACITY
        buf = jnp.full((E, CAPACITY), N, dtype=jnp.int32)
        buf = buf.at[fe, pos].set(ft.astype(jnp.int32), mode='drop')
        xpad = jnp.concatenate([xf, jnp.zeros((1, D), xf.dtype)], axis=0)
        xe = xpad[buf]
        h = jax.nn.silu(jnp.einsum('ecd,eid->eci', xe, w1)) * jnp.einsum('ecd,eid->eci', xe, w3)
        ye = jnp.einsum('eci,edi->ecd', h, w2)
        pc = jnp.minimum(pos, CAPACITY - 1)
        op = ye[fe, pc] * keep[:, None].astype(ye.dtype)
        routed = (op * gate_vals.reshape(-1)[:, None]).reshape(N, TOPK, D).sum(axis=1)
        z = jax.nn.silu(xf @ sw1.T) * (xf @ sw3.T) @ sw2.T
        return (routed + z).reshape(Bb, Tt, D)
    x = L0_attn_x
    x = x + _layernorm(_L0_attn_ref(_layernorm(x, axis=-1), L0_attn_Wq, L0_attn_Wk, L0_attn_Wv, L0_attn_Wu, L0_attn_Wo), axis=-1)
    x = x + _layernorm(_L0_ffn_ref(_layernorm(x, axis=-1), L0_ffn_gate_w, L0_ffn_w1, L0_ffn_w2, L0_ffn_w3, L0_ffn_sw1, L0_ffn_sw2, L0_ffn_sw3), axis=-1)
    return x

_drawn_inputs = setup_inputs


def setup_inputs(seed=0):
    import zlib

    import numpy as np

    out = dict(_drawn_inputs(seed))
    spreads = {}
    factors = {}
    for name, (base, spread) in spreads.items():
        noise = np.random.default_rng([zlib.crc32(name.encode()), seed]).standard_normal(out[name].shape)
        drawn = base * np.exp(spread * noise) if base else spread * noise
        out[name] = jnp.asarray(drawn.astype(out[name].dtype))
    for name, factor in factors.items():
        out[name] = (out[name] * factor).astype(out[name].dtype)
    return out
```

```python
from contextlib import ExitStack

import concourse.bass as bass
import numpy as np
from concourse import mybir

F32, F32R, F16, BF16 = mybir.dt.float32, mybir.dt.float32r, mybir.dt.float16, mybir.dt.bfloat16
I32, U32 = mybir.dt.int32, mybir.dt.uint32
ALU, ACT, AX = mybir.AluOpType, mybir.ActivationFunctionType, mybir.AxisListType

P = 128
B, L, D = 8, 512, 256
T = L // P
K = D // P
N = B * L
H, DH = 16, 16
E, F, CAP, TOPK = 64, 176, 128, 6
FS = 2 * F
FH = F // 2
EPS, EPS_NORM = 1e-5, 1e-12
ROW = D + E
CHUNKS = [(0, 128), (128, 128), (256, 96)]
HI, LO = 8, 16
GE = P // HI
G = E // GE
ACC_ROWS = 1 + N + P
PEEL = 3
WB = 4
BODY = 2 * WB
WORK = 17664


def build(nc, x, wq, wk, wv, wu, wo, gate_w, w13, w2, sw13, sw2, out):
    ctx = ExitStack()
    with ctx:
        def sb(name, shape, dt=F32):
            return ctx.enter_context(nc.sbuf_tensor(name, shape, dt))

        def sem(name):
            return ctx.enter_context(nc.semaphore(name))

        rows = nc.dram_tensor("token_rows", (1 + N, ROW), F32, kind="Internal").ap()
        sums = [nc.dram_tensor(f"sums{j}", (ACC_ROWS, D), F32, kind="Internal").ap() for j in range(2)]
        slot_table = nc.dram_tensor("slot_table", (E, CAP), F32, kind="Internal").ap()

        resid = sb("resid", [P, B, T, D])
        WCOLS = 5 * D
        w_hi, w_lo = sb("w_hi", [P, K, WCOLS], F32R), sb("w_lo", [P, K, WCOLS], F32R)
        s13_hi, s13_lo = sb("s13_hi", [P, K, 2 * FS], F32R), sb("s13_lo", [P, K, 2 * FS], F32R)
        s2_hi, s2_lo = sb("s2_hi", [P, 3, D], F32R), sb("s2_lo", [P, 3, D], F32R)
        g_hi, g_lo = sb("g_hi", [P, K, E], F32R), sb("g_lo", [P, K, E], F32R)
        xT_hi, xT_lo = sb("xT_hi", [P, K, L], F32R), sb("xT_lo", [P, K, L], F32R)
        oT_hi, oT_lo = sb("oT_hi", [P, K, L], F32R), sb("oT_lo", [P, K, L], F32R)
        x2T_hi, x2T_lo = sb("x2T_hi", [P, K, L], F32R), sb("x2T_lo", [P, K, L], F32R)
        hT_hi, hT_lo = sb("hT_hi", [P, 3, L], F32R), sb("hT_lo", [P, 3, L], F32R)
        onehot_hi = sb("onehot_hi", [P, T, G, HI, GE], F16)
        onehot_lo = sb("onehot_lo", [P, T, LO, E], F16)
        ident = sb("ident", [P, P])
        block_mask = sb("block_mask", [P, P])
        before = sb("before", [P, P], BF16)
        ones = sb("ones", [P, P], BF16)
        iota_hi = sb("iota_hi", [P, G, HI, GE], F16)
        iota_lo = sb("iota_lo", [P, LO, E], F16)
        token_code = sb("token_code", [P, B, T])
        slot_dump = sb("slot_dump", [P, 1])
        neg_half = sb("neg_half", [P, T * H])
        table = sb("table", [P, G, LO, GE])
        taken = sb("taken", [P, E], BF16)
        gather_rows, scatter_rows = sb("gather_rows", [P, E], U32), sb("scatter_rows", [P, E], U32)
        small = sb("small", [P, 1100])
        work = sb("work", [P, WORK])

        class Carve:
            def __init__(self, tensor):
                self.tensor, self.at = tensor, 0

            def take(self, *shape):
                n = int(np.prod(shape))
                view = self.tensor[:, self.at:self.at + n]
                self.at += n
                names = "abcd"[:len(shape)]
                if len(shape) > 1:
                    view = view.rearrange(f"p ({' '.join(names)}) -> p {' '.join(names)}",
                                          **dict(zip(names[1:], shape[1:])))
                return view

        s = Carve(small)
        stats1, mv1, ve1, r1 = s.take(T, 6), s.take(T, 2), s.take(T), s.take(T)
        stats2, mv2, ve2, r2 = s.take(T, 6), s.take(T, 2), s.take(T), s.take(T)
        stats3, mv3, ve3, r3 = s.take(T, 6), s.take(T, 2), s.take(T), s.take(T)
        power, norm = s.take(T * H), s.take(T * H)
        top, expsum, expinv, top8 = s.take(T), s.take(T), s.take(T), s.take(T, 8)
        padded = s.take(T, E + 2)
        replaced = s.take(T, E + 2)
        taken_now = s.take(E)
        code = s.take(E)

        a = Carve(work)
        u_sb, th, o_sb, sq = (a.take(T, D) for _ in range(4))
        q_sb, k_sb, v_sb = a.take(K, L), a.take(T, D), a.take(T, D)
        xn, on, y_sb, un = (a.take(T, D) for _ in range(4))
        xg = a.take(T, ROW)
        tu, hT = a.take(3, L), a.take(3, L)
        z_sb = a.take(T, D)
        kv_sb = a.take(K, P)
        logit = a.take(T, E)
        expd = a.take(T, E)
        penalty = a.take(T, E)
        assert a.at <= WORK
        posi, lo_i, hi_i = (sb(n, [P, T, E], I32) for n in ("posi", "lo_i", "hi_i"))
        lo_h, hi_h = sb("lo_h", [P, T, E], F16), sb("hi_h", [P, T, E], F16)
        sel = sb("sel", [P, T, E], BF16)
        r = Carve(work)
        r.at = 8 * T * D
        raw_w = r.take(K, WCOLS)
        raw_13 = r.take(K, 2 * FS)
        raw_2 = r.take(3, D)
        raw_g = r.take(K, E)
        zeros = r.take(D)
        assert r.at <= WORK

        m = Carve(work)
        w13_sb = m.take(WB, 2, K, 2 * F)
        w2_sb = m.take(WB, 2, 2, D)
        XS = 4
        xe = m.take(XS, ROW)
        xeT = m.take(2, K, P)
        silu_a, hid = m.take(2, F), m.take(2, F)
        hidT = m.take(2, 2, P)
        ye = m.take(4, D)
        gates = m.take(4, 1)
        assert m.at <= WORK
        rows_now = sb("rows_now", [P, XS], U32)
        dest_now = sb("dest_now", [P, 4], U32)

        c = Carve(work)
        s0, s1, total, fin = (c.take(2, T, D) for _ in range(4))

        bank = [ctx.enter_context(nc.psum_tensor(f"bank{j}", [P, 512], F32)) for j in range(8)]

        names = """dma_x dma_w dma_z dma_rows dma_table dma_table_back dma_zero_rows dma_zero0 dma_zero1
            pool_const pool_const2 dve_const act_w dve_w
            dve_mv1 pool_r1 dve_xn pe_trx act_xT dve_xT
            pe_q pe_kvp pe_u act_q act_k dve_v act_th dve_u pe_kv dve_kv
            pe_out act_o dve_power pool_norm pool_un dve_on pe_tro act_oT dve_oT pe_wo
            dve_mv2 pool_r2 dve_yn dve_x1 dve_mv3 pool_r3 dve_xn2 pe_trx2 act_x2T dve_x2T
            pe_gate dve_logit act_exp dve_scores dve_sel pe_pos dve_pos dve_onehot pe_table dve_table
            pe_up act_tu dve_h act_hT pool_hT pe_down act_z dve_link
            pe_code dve_index
            pool_rows_now pool_scatter_now pe_xeT act_xeT pe_eup act_silu dve_hid pe_hidT act_hidT pe_edown act_ye
            pool_gate dma_scatter0 dma_scatter1
            dve_total dve_mvc pool_rc dve_cn dve_fin dma_s0a dma_s0b dma_s1a dma_s1b dma_out0 dma_out1""".split()
        S = {n: sem(n) for n in names}
        dma_x = [sem(f"dma_x{b}") for b in range(B)]
        dma_w13 = [sem(f"dma_w13_{j}") for j in range(WB)]
        dma_w2 = [sem(f"dma_w2_{j}") for j in range(WB)]
        dma_xe = [sem(f"dma_xe{j}") for j in range(XS)]

        def wait_apart(engine, *waits):
            waits = [(S[n], v if isinstance(v, int) else engine.compute_val(v)) for n, v in waits]
            engine.wait_ge(S["pool_const"], 1)
            for semaphore, value in waits:
                engine.wait_ge(semaphore, value)

        def share(j, k, d):
            return j * (BODY // d) + k // d

        def tile_of(t):
            return slice(t * P, (t + 1) * P)

        def at(buffer, b):
            return buffer[:, b] if isinstance(b, int) else buffer[:, bass.ds(b, 1)].squeeze(1)

        def token_rows_of(tensor, b, width):
            first = 1 + b * L
            return tensor[bass.ds(first, L), 0:width].rearrange("(t p) d -> p t d", p=P)

        def steps(engine, body):
            for i in range(PEEL):
                body(i)
            with engine.Fori(PEEL, B - 1) as i:
                body(i)
            for i in range(B - 1, B + 2):
                body(i)

        def live(i, lag):
            if isinstance(i, int):
                return 0 <= i - lag < B, i == lag
            return True, False

        def expert_steps(engine, step, after=2):
            for k in range(BODY):
                step(0, k)
            with engine.Fori(1, E // BODY - 1) as j:
                for k in range(BODY):
                    step(j, k)
            for k in range(E - BODY, E + after):
                step(0, k)

        block = ctx.enter_context(nc.Block())

        @block.sync
        def _(sp):
            sp.dma_start(resid[:, 0], x[0].rearrange("(t p) d -> p t d", p=P)).then_inc(dma_x[0], 16)
            for j, w in enumerate((wq, wk, wv, wu, wo)):
                sp.dma_start(raw_w[:, :, j * D:(j + 1) * D], w.rearrange("(k p) n -> p k n", p=P)).then_inc(S["dma_w"], 16)
            sp.dma_start(resid[:, 1], x[1].rearrange("(t p) d -> p t d", p=P)).then_inc(dma_x[1], 16)
            sp.dma_start(raw_g, gate_w).then_inc(S["dma_w"], 16)
            sp.dma_start(raw_13, sw13).then_inc(S["dma_w"], 16)
            sp.dma_start(raw_2[:, 0:2, :], sw2[0:2 * P].rearrange("(c p) n -> p c n", p=P)).then_inc(S["dma_w"], 16)
            sp.dma_start(raw_2[0:FS - 2 * P, 2, :], sw2[2 * P:FS]).then_inc(S["dma_w"], 16)
            for b in range(2, B):
                sp.dma_start(resid[:, b], x[b].rearrange("(t p) d -> p t d", p=P)).then_inc(dma_x[b], 16)
            sp.wait_ge(S["pool_const"], 1)
            sp.dma_start(rows[0:1, :].rearrange("o (a b) -> o a b", a=2), zeros[0:1, :].rearrange("p (o d) -> p o d", o=1).to_broadcast([1, 2, D])[:, :, 0:ROW // 2]).then_inc(S["dma_zero_rows"], 16)
            sp.dma_start(sums[0][1 + N:ACC_ROWS, :], zeros).then_inc(S["dma_zero0"], 16)
            sp.dma_start(sums[1][1:ACC_ROWS, :].rearrange("(p r) d -> p r d", p=P),
                         zeros.rearrange("p (o d) -> p o d", o=1).to_broadcast([P, (N + P) // P, D])).then_inc(S["dma_zero1"], 16)

            def body(i):
                R, _ = live(i, 2)
                if R:
                    b = i - 2
                    sp.wait_ge(S["dve_scores"], b + 1)
                    sp.dma_start(token_rows_of(rows, b, ROW), xg).then_inc(S["dma_rows"], 16)
                    sp.wait_ge(S["act_z"], 2 * b + 2)
                    sp.dma_start(token_rows_of(sums[0], b, D), z_sb).then_inc(S["dma_z"], 16)

            steps(sp, body)

            sp.wait_ge(S["dve_index"], 1)
            for h in range(HI):
                sp.dma_start(slot_table[:, h * LO:(h + 1) * LO].rearrange("(g e) l -> e g l", e=GE),
                             sq[h * GE:(h + 1) * GE, 0, 0:G * LO].rearrange("p (g l) -> p g l", g=G)).then_inc(S["dma_table"], 16)
            sp.wait_ge(S["dma_table"], 16 * HI)
            sp.dma_start(sq[0:E, 1, 0:CAP], slot_table).then_inc(S["dma_table_back"], 16)

            def load_pair(pair, slot):
                sp.dma_start(w13_sb[:, slot], w13[:, bass.ds(2 * pair, 2)]).then_inc(dma_w13[slot], 16)
                sp.dma_start(w2_sb[0:FH, slot], w2[:, bass.ds(2 * pair, 2)]).then_inc(dma_w2[slot], 16)

            sp.wait_ge(S["dve_index"], 2)
            sp.wait_ge(S["dma_z"], 16 * B)
            for pair in range(WB):
                load_pair(pair, pair)
            with sp.Fori(1, E // BODY) as j:
                for slot in range(WB):
                    sp.wait_ge(S["pe_edown"], (j - 1) * BODY + 2 * slot + 2)
                    load_pair(j * WB + slot, slot)

            sp.wait_ge(S["act_ye"], E)
            sp.wait_ge(S["pe_edown"], E)
            for j in range(2):
                sp.wait_ge(S[f"dma_scatter{j}"], 16 * (E // 2))
            load = [("dma_s0a", "dma_s1a"), ("dma_s0b", "dma_s1b")]

            def load_sums(b, room):
                sp.dma_start(s0[:, room], token_rows_of(sums[0], b, D)).then_inc(S[load[room][0]], 16)
                sp.dma_start(s1[:, room], token_rows_of(sums[1], b, D)).then_inc(S[load[room][1]], 16)

            load_sums(0, 0)
            load_sums(1, 1)
            for b in range(B):
                if b + 2 < B:
                    sp.wait_ge(S["dve_total"], b + 1)
                    load_sums(b + 2, b % 2)
                sp.wait_ge(S["dve_fin"], b + 1)
                sp.dma_start(out[b].rearrange("(t p) d -> p t d", p=P), fin[:, b % 2]).then_inc(S[f"dma_out{b % 2}"], 16)
            sp.wait_ge(S["dma_out0"], 16 * (B // 2))
            sp.wait_ge(S["dma_out1"], 16 * (B // 2))
            sp.wait_ge(S["dma_zero0"], 16)

        @block.gpsimd
        def _(pool):
            pool.memset(zeros, 0.0).then_inc(S["pool_const"], 1)
            pool.memset(ident[:, :], 0.0)
            pool.memset(block_mask[:, :], 1.0)
            pool.memset(before[:, :], 1.0)
            pool.memset(ones[:, :], 1.0)
            pool.memset(neg_half[:, :], -0.5)
            pool.memset(taken[:, :], 0.0)
            pool.memset(table[:, :, :, :], 0.0)
            pool.memset(padded[:, :, E:E + 2], 2.0)
            pool.iota(iota_hi[:, :, :, :], pattern=[[0, G], [1, HI], [0, GE]], base=0, channel_multiplier=0, allow_small_or_imprecise_dtypes=True)
            pool.iota(iota_lo[:, :, :], pattern=[[1, LO], [0, E]], base=0, channel_multiplier=0, allow_small_or_imprecise_dtypes=True)
            pool.iota(token_code[:, :, :], pattern=[[L, B], [P, T]], base=-N // 2, channel_multiplier=1, allow_small_or_imprecise_dtypes=True)
            pool.iota(slot_dump[:, :], pattern=[[0, 1]], base=1 + N, channel_multiplier=1, allow_small_or_imprecise_dtypes=True).then_inc(S["pool_const"], 1)
            pool.wait_ge(S["pool_const"], 2)
            pool.affine_select(out=ident[:, :], in_=ident[:, :], compare_op=ALU.not_equal, fill=1.0, base=0,
                               pattern=[[-1, P]], channel_multiplier=1)
            pool.affine_select(out=before[:, :], in_=before[:, :], compare_op=ALU.is_ge, fill=0.0, base=-1,
                               pattern=[[1, P]], channel_multiplier=-1)
            blocks = block_mask[:, :].rearrange("p (h d) -> p h d", d=DH)
            pool.affine_select(out=blocks, in_=blocks, compare_op=ALU.is_ge, fill=0.0, base=0,
                               pattern=[[-DH, P // DH], [0, DH]], channel_multiplier=1).then_inc(S["pool_const"], 1)
            pool.wait_ge(S["pool_const"], 3)
            pool.affine_select(out=blocks, in_=blocks, compare_op=ALU.is_ge, fill=0.0, base=DH - 1,
                               pattern=[[DH, P // DH], [0, DH]], channel_multiplier=-1).then_inc(S["pool_const2"], 1)

            def inverse_root(out_, in_, ready, value, done):
                pool.wait_ge(S[ready], value)
                pool.tensor_tensor(out_, in_, neg_half[:, 0:in_.shape[1]], ALU.pow).then_inc(S[done], 1)

            inverse_root(r1, ve1, "dve_mv1", 1, "pool_r1")

            def body(i):
                Nx, _ = live(i, -1)
                Q, _ = live(i, 1)
                R, _ = live(i, 2)
                if Nx:
                    inverse_root(r1, ve1, "dve_mv1", i + 2, "pool_r1")
                if Q:
                    inverse_root(norm, power, "dve_power", i, "pool_norm")
                    pool.wait_ge(S["dve_u"], 2 * i)
                    pool.wait_ge(S["pool_norm"], i)
                    if not live(i, 1)[1]:
                        pool.wait_ge(S["dve_on"], i - 1)
                    pool.tensor_tensor(un.rearrange("p t (h d) -> p (t h) d", d=DH), u_sb.rearrange("p t (h d) -> p (t h) d", d=DH),
                                       norm.rearrange("p (n o) -> p n o", o=1).to_broadcast([P, T * H, DH]), ALU.mult).then_inc(S["pool_un"], 1)
                if R:
                    b = i - 2
                    if not live(i, 2)[1]:
                        pool.wait_ge(S["pe_down"], 2 * b)
                    for j, (_, w) in enumerate(CHUNKS):
                        pool.wait_ge(S["act_hT"], 3 * b + j + 1)
                        pool.tensor_tensor(hT_lo[0:w, j, :], hT[0:w, j, :], hT_hi[0:w, j, :].bitcast(F32), ALU.subtract).then_inc(S["pool_hT"], 1)
                if Q:
                    inverse_root(r2, ve2, "dve_mv2", i, "pool_r2")
                    inverse_root(r3, ve3, "dve_mv3", i, "pool_r3")

            steps(pool, body)

            pool.wait_ge(S["dve_index"], 2)
            pool.wait_ge(S["dma_rows"], 16 * B)
            pool.wait_ge(S["dma_zero_rows"], 16)
            pool.wait_ge(S["dma_zero0"], 16)
            pool.wait_ge(S["dma_zero1"], 16)
            pool.wait_ge(S["dma_z"], 16 * B)

            def gather(j, k, first):
                e = j * BODY + k
                if not first:
                    pool.wait_ge(dma_xe[k % XS], 16 * share(j, k, XS))
                pool.tensor_copy(rows_now[:, k % XS:k % XS + 1], gather_rows[:, bass.ds(e, 1)]).then_inc(S["pool_rows_now"], 1)
                free = [] if first else [("pe_xeT", e - XS + 1), ("pool_gate", e - XS + 1)]
                wait_apart(pool, *free, ("pool_rows_now", e + 1))
                pool.indirect_dma_start(out=xe[:, k % XS, :], out_offset=None, in_=rows,
                                        in_offset=bass.IndirectOffsetOnAxis(ap=rows_now[:, k % XS:k % XS + 1], axis=0)).then_inc(dma_xe[k % XS], 16)

            def keep_gate(j, k, first):
                e = j * BODY + k
                pool.wait_ge(dma_xe[k % XS], 16 * (share(j, k, XS) + 1))
                if not first:
                    pool.wait_ge(S["act_ye"], e - 3)
                pool.tensor_copy(gates[:, k % 4], xe[:, k % XS, bass.ds(D + e, 1)]).then_inc(S["pool_gate"], 1)

            def scatter(j, k, first):
                e = j * BODY + k
                if not first:
                    pool.wait_ge(S[f"dma_scatter{k % 2}"], 16 * share(j, k, 2))
                pool.tensor_copy(dest_now[:, k % 4:k % 4 + 1], scatter_rows[:, bass.ds(e, 1)]).then_inc(S["pool_scatter_now"], 1)
                wait_apart(pool, ("act_ye", e + 1), ("pool_scatter_now", e + 1))
                pool.indirect_dma_start(out=sums[k % 2], out_offset=bass.IndirectOffsetOnAxis(ap=dest_now[:, k % 4:k % 4 + 1], axis=0),
                                        in_=ye[:, k % 4, :], in_offset=None, compute_op=ALU.add).then_inc(S[f"dma_scatter{k % 2}"], 16)

            for e in range(3):
                gather(0, e, True)
                keep_gate(0, e, True)

            def experts(j, k):
                known = isinstance(j, int)
                if not known or k + 3 < E:
                    gather(j, k + 3, known and k + 3 < XS)
                    keep_gate(j, k + 3, known and k + 3 < 4)
                if not known or k >= 2:
                    scatter(j, k - 2, known and k < 4)

            expert_steps(pool, experts)

            for b in range(B):
                inverse_root(r1, ve1, "dve_mvc", b + 1, "pool_rc")

        @block.scalar
        def _(act):
            def hi_part(out_, in_, done):
                nc.scalar.activation(out_, in_, ACT.Copy).then_inc(S[done], 1)

            act.wait_ge(S["dma_w"], 16 * 9)
            hi_part(w_hi[:, :, :], raw_w, "act_w")
            hi_part(g_hi[:, :, :], raw_g, "act_w")
            hi_part(s13_hi[:, :, :], raw_13, "act_w")
            hi_part(s2_hi[:, 0:2, :], raw_2[:, 0:2, :], "act_w")
            hi_part(s2_hi[0:FS - 2 * P, 2, :], raw_2[0:FS - 2 * P, 2, :], "act_w")

            def transposed_hi(out_, banks, ready, value, done):
                for c_ in range(K):
                    act.wait_ge(S[ready], value + c_ + 1)
                    hi_part(out_[:, c_, :], bank[banks[c_]][:, :], done)

            transposed_hi(xT_hi, (2, 3), "pe_trx", 0, "act_xT")

            def body(i):
                Nx, _ = live(i, -1)
                Pr, Pfirst = live(i, 0)
                Q, Qfirst = live(i, 1)
                R, Rfirst = live(i, 2)
                if Q:
                    if not Qfirst:
                        act.wait_ge(S["dve_on"], i - 1)
                        act.wait_ge(S["dve_power"], i - 1)
                    for c_ in range(2):
                        act.wait_ge(S["pe_out"], 2 * (i - 1) + c_ + 1)
                        nc.scalar.activation(o_sb[:, 2 * c_:2 * c_ + 2, :].rearrange("p t d -> p (t d)"), bank[c_][:, :], ACT.Copy)
                        nc.scalar.activation(sq[:, 2 * c_:2 * c_ + 2, :].rearrange("p t d -> p (t d)"), bank[c_][:, :], ACT.Square).then_inc(S["act_o"], 1)
                if R:
                    if Rfirst:
                        for n in ("dma_zero_rows", "dma_zero0", "dma_zero1"):
                            act.wait_ge(S[n], 16)
                    act.wait_ge(S["dve_logit"], i - 1)
                    nc.scalar.activation(expd, logit, ACT.Exp).then_inc(S["act_exp"], 1)
                if Pr:
                    for c_ in range(K):
                        act.wait_ge(S["pe_q"], 2 * i + c_ + 1)
                        if not Pfirst:
                            act.wait_ge(S["pe_out"], 2 * i)
                        nc.scalar.activation(q_sb[:, c_, :], bank[c_][:, :], ACT.Relu, scale=0.25).then_inc(S["act_q"], 1)
                    for t in range(T):
                        act.wait_ge(S["pe_kvp"], 4 * i + t + 1)
                        if not Pfirst:
                            act.wait_ge(S["pe_kv"], i)
                        nc.scalar.activation(k_sb[:, t, :], bank[t % 2][:, 0:D], ACT.Relu, scale=0.25).then_inc(S["act_k"], 1)
                    for c_ in range(2):
                        act.wait_ge(S["pe_u"], 2 * i + c_ + 1)
                        if not Pfirst:
                            act.wait_ge(S["dve_u"], 2 * i)
                        nc.scalar.activation(th[:, 2 * c_:2 * c_ + 2, :].rearrange("p t d -> p (t d)"), bank[c_][:, :], ACT.Tanh, scale=0.5).then_inc(S["act_th"], 1)
                if R:
                    b = i - 2
                    for j, (_, w) in enumerate(CHUNKS):
                        act.wait_ge(S["pe_up"], 3 * b + j + 1)
                        if not Rfirst:
                            act.wait_ge(S["dve_h"], 3 * b)
                        nc.scalar.activation(tu[0:w, j, :], bank[(4, 6, 4)[j]][0:w, :], ACT.Tanh, scale=0.5).then_inc(S["act_tu"], 1)
                    for j, (_, w) in enumerate(CHUNKS):
                        act.wait_ge(S["dve_h"], 3 * b + j + 1)
                        if not Rfirst:
                            act.wait_ge(S["pe_down"], 2 * b)
                            act.wait_ge(S["pool_hT"], 3 * b)
                        hi_part(hT_hi[0:w, j, :], hT[0:w, j, :], "act_hT")
                if Q:
                    if not Qfirst:
                        act.wait_ge(S["pe_wo"], 2 * (i - 1))
                        act.wait_ge(S["dve_oT"], 2 * (i - 1))
                    transposed_hi(oT_hi, (0, 1), "pe_tro", 2 * (i - 1), "act_oT")
                if Nx:
                    if isinstance(i, int) and i < 0:
                        raise ValueError
                    act.wait_ge(S["pe_u"], 2 * i + 2)
                    transposed_hi(xT_hi, (2, 3), "pe_trx", 2 * (i + 1), "act_xT")
                if R:
                    b = i - 2
                    if not Rfirst:
                        act.wait_ge(S["dma_z"], 16 * b)
                    for c_ in range(2):
                        act.wait_ge(S["pe_down"], 2 * b + c_ + 1)
                        nc.scalar.activation(z_sb[:, 2 * c_:2 * c_ + 2, :].rearrange("p t d -> p (t d)"), bank[4 + c_][:, :], ACT.Copy).then_inc(S["act_z"], 1)
                if Q:
                    if not Qfirst:
                        act.wait_ge(S["pe_up"], 3 * (i - 1))
                        act.wait_ge(S["pe_gate"], i - 1)
                    transposed_hi(x2T_hi, (2, 3), "pe_trx2", 2 * (i - 1), "act_x2T")

            steps(act, body)

            def xeT_copy(j, k, first):
                e = j * BODY + k
                act.wait_ge(S["pe_xeT"], e + 1)
                if not first:
                    act.wait_ge(S["pe_eup"], e - 1)
                nc.scalar.activation(xeT[:, k % 2].rearrange("p k s -> p (k s)"), bank[k % 2][:, 0:D], ACT.Copy).then_inc(S["act_xeT"], 1)

            def silu(j, k, first):
                e = j * BODY + k
                act.wait_ge(S["pe_eup"], e + 1)
                if not first:
                    act.wait_ge(S["dve_hid"], e - 1)
                nc.scalar.activation(silu_a[:, k % 2], bank[2 + k % 2][:, 0:F], ACT.Silu).then_inc(S["act_silu"], 1)

            def hidT_copy(j, k, first):
                e = j * BODY + k
                act.wait_ge(S["pe_hidT"], e + 1)
                if not first:
                    act.wait_ge(S["pe_edown"], e - 1)
                nc.scalar.activation(hidT[0:FH, k % 2].rearrange("p c s -> p (c s)"), bank[4 + k % 2][0:FH, 0:2 * P], ACT.Copy).then_inc(S["act_hidT"], 1)

            def weigh(j, k, first):
                e = j * BODY + k
                act.wait_ge(S["pe_edown"], e + 1)
                act.wait_ge(S["pool_gate"], e + 1)
                if not first:
                    act.wait_ge(S[f"dma_scatter{k % 2}"], 16 * (share(j, k, 2) - 1))
                nc.scalar.activation(ye[:, k % 4], bank[6 + k % 2][:, 0:D], ACT.Copy, scale=gates[:, k % 4]).then_inc(S["act_ye"], 1)

            act.wait_ge(S["dve_index"], 2)
            xeT_copy(0, 0, True)

            def experts(j, k):
                known = isinstance(j, int)
                if not known or k < E:
                    silu(j, k, known and k < 2)
                if not known or k >= 2:
                    weigh(j, k - 2, known and k < 6)
                if not known or 1 <= k <= E:
                    hidT_copy(j, k - 1, known and k < 3)
                if not known or k + 1 < E:
                    xeT_copy(j, k + 1, known and k < 1)

            expert_steps(act, experts)

        @block.vector
        def _(dve):
            done = {"n": 0}

            def tiles(ap, c_):
                return ap[:, 2 * c_:2 * c_ + 2, :].rearrange("p t d -> p (t d)")

            def lo_part(out_, in_, hi, sem_name):
                nc.vector.tensor_tensor(out_, in_, hi.bitcast(F32), ALU.subtract).then_inc(S[sem_name], 1)

            dve.wait_ge(S["pool_const"], 2)
            nc.vector.scalar_tensor_tensor(token_code[:, :, :].rearrange("p b t -> p (b t)"), token_code[:, :, :].rearrange("p b t -> p (b t)"), 0.0,
                                           token_code[:, :, :].rearrange("p b t -> p (b t)"), ALU.is_ge, ALU.add).then_inc(S["dve_const"], 1)
            dve.wait_ge(S["dve_const"], 1)

            LINKS = {"A": 0}

            class Chain:
                per = 0

                def __init__(self, base):
                    self.base, self.n = base, 0

                def link(self, ins):
                    ins.then_inc(S["dve_link"], 1)
                    self.n += 1
                    dve.wait_ge(S["dve_link"], self.base + self.n)

                def link_apart(self, ins):
                    ins.then_inc(S["dve_link"], 1)
                    self.n += 1
                    wait_apart(dve, ("dve_link", self.base + self.n))

            def norm_stats(rows_, stats, mv, ve, chain, mv_done, *ready):
                wait_apart(dve, *ready)
                for t in range(T):
                    last = nc.vector.bn_stats(stats[:, t, :], rows_[t])
                chain.link_apart(last)
                for t in range(T):
                    last = nc.vector.bn_aggr(mv[:, t, :], stats[:, t, :])
                chain.link(last)
                nc.vector.tensor_scalar(ve, mv[:, :, 1], EPS, None, ALU.add).then_inc(S[mv_done], 1)

            c0 = Chain(0)
            dve.wait_ge(dma_x[0], 16)
            norm_stats([resid[:, 0, t, :] for t in range(T)], stats1, mv1, ve1, c0, "dve_mv1")
            dve.wait_ge(S["pool_r1"], 1)
            for t in range(T):
                last = nc.vector.tensor_scalar(xn[:, t, :], resid[:, 0, t, :], mv1[:, t, 0:1], r1[:, t:t + 1], ALU.subtract, ALU.mult)
            last.then_inc(S["dve_xn"], 1)
            dve.wait_ge(S["act_w"], 5)
            lo_part(w_lo[:, :, :], raw_w, w_hi[:, :, :], "dve_w")
            lo_part(g_lo[:, :, :], raw_g, g_hi[:, :, :], "dve_w")
            lo_part(s13_lo[:, :, :], raw_13, s13_hi[:, :, :], "dve_w")
            lo_part(s2_lo[:, 0:2, :], raw_2[:, 0:2, :], s2_hi[:, 0:2, :], "dve_w")
            lo_part(s2_lo[0:FS - 2 * P, 2, :], raw_2[0:FS - 2 * P, 2, :], s2_hi[0:FS - 2 * P, 2, :], "dve_w")
            base_links = c0.n

            def transposed_lo(out_, hi, banks, ready, value, sem_name):
                for c_ in range(K):
                    dve.wait_ge(S[ready], value + c_ + 1)
                    lo_part(out_[:, c_, :], bank[banks[c_]][:, :], hi[:, c_, :], sem_name)

            transposed_lo(xT_lo, xT_hi, (2, 3), "act_xT", 0, "dve_xT")
            PER_N, PER_Q, PER_R = 2, 5, 14

            def links_before(i):
                if not isinstance(i, int):
                    return base_links + PER_N * i + PER_Q * (i - 1) + PER_R * (i - 2)
                return base_links + sum(PER_N * live(j, -1)[0] + PER_Q * live(j, 1)[0] + PER_R * live(j, 2)[0] for j in range(i))

            def body(i):
                Nx, _ = live(i, -1)
                Pr, Pfirst = live(i, 0)
                Q, Qfirst = live(i, 1)
                R, Rfirst = live(i, 2)
                ch = Chain(links_before(i))
                before_n = 0
                if Nx:
                    if isinstance(i, int):
                        dve.wait_ge(dma_x[i + 1], 16)
                    xb = at(resid, i + 1)
                    norm_stats([xb[:, t, :] for t in range(T)], stats1, mv1, ve1, ch, "dve_mv1")
                    assert ch.n == PER_N
                if Q:
                    dve.wait_ge(S["act_o"], 2 * i)
                    if not Qfirst:
                        dve.wait_ge(S["pool_norm"], i - 1)
                    n0 = ch.n
                    ch.link(nc.vector.tensor_reduce(power, sq.rearrange("p t (h d) -> p (t h) d", d=DH), AX.X, ALU.add))
                    nc.vector.tensor_scalar(power, power, 4.0 / DH, 4.0 * EPS_NORM ** 2, ALU.mult, ALU.max).then_inc(S["dve_power"], 1)
                if R:
                    b = i - 2
                    n0 = ch.n
                    dve.wait_ge(S["pe_gate"], b + 1)
                    lg = bank[2][:, 0:T * E].rearrange("p (t e) -> p t e", t=T)
                    ch.link(nc.vector.tensor_reduce(top, lg, AX.X, ALU.max))
                    nc.vector.tensor_tensor(logit, lg, top.rearrange("p (t o) -> p t o", o=1).to_broadcast([P, T, E]), ALU.subtract).then_inc(S["dve_logit"], 1)
                    dve.wait_ge(S["act_exp"], b + 1)
                    ch.link(nc.vector.tensor_reduce(expsum, expd, AX.X, ALU.add))
                    ch.link(nc.vector.reciprocal(expinv, expsum))
                    ch.link(nc.vector.tensor_tensor(padded[:, :, 0:E], expd, expinv.rearrange("p (t o) -> p t o", o=1).to_broadcast([P, T, E]), ALU.mult))
                    nc.vector.tensor_copy(xg[:, :, D:ROW], padded[:, :, 0:E]).then_inc(S["dve_scores"], 1)
                    for t in range(T):
                        last = nc.vector.max(top8[:, t, :], padded[:, t, :])
                    ch.link_apart(last)
                    for t in range(T):
                        last = nc.vector.match_replace(replaced[:, t, :], top8[:, t, :], padded[:, t, :], -1.0)
                    ch.link(last)
                    if not Rfirst:
                        dve.wait_ge(S["pe_pos"], b)
                    nc.vector.tensor_scalar(sel[:, :, :], replaced[:, :, 0:E], 0.0, None, ALU.is_lt).then_inc(S["dve_sel"], 1)
                    ch.link(nc.vector.tensor_scalar(penalty, replaced[:, :, 0:E], 0.0, float(N), ALU.is_ge, ALU.mult))
                    r1_links = ch.n - n0
                if Pr:
                    for t in range(T):
                        dve.wait_ge(S["act_k"], 4 * i + t + 1)
                        if not Pfirst:
                            dve.wait_ge(S["pe_kv"], i)
                        nc.vector.tensor_copy(v_sb[:, t, :], bank[t % 2][:, D:2 * D]).then_inc(S["dve_v"], 1)

                def hidden(j):
                    w = CHUNKS[j][1]
                    ba, bb = ((4, 5), (6, 7), (4, 5))[j]
                    dve.wait_ge(S["act_tu"], 3 * b + j + 1)
                    if not Rfirst:
                        dve.wait_ge(S["pool_hT"], 3 * b)
                        dve.wait_ge(S["act_hT"], 3 * b)
                    ch.link(nc.vector.scalar_tensor_tensor(tu[0:w, j, :], tu[0:w, j, :], 1.0, bank[ba][0:w, :], ALU.add, ALU.mult))
                    nc.vector.scalar_tensor_tensor(hT[0:w, j, :], tu[0:w, j, :], 0.5, bank[bb][0:w, :], ALU.mult, ALU.mult).then_inc(S["dve_h"], 1)

                if R:
                    hidden(0)
                if Pr:
                    for c_ in range(2):
                        dve.wait_ge(S["act_th"], 2 * i + c_ + 1)
                        if not Pfirst:
                            dve.wait_ge(S["pool_un"], i)
                        nc.vector.scalar_tensor_tensor(tiles(u_sb, c_), tiles(th, c_), 1.0, bank[c_][:, :], ALU.add, ALU.mult).then_inc(S["dve_u"], 1)
                    dve.wait_ge(S["pe_kv"], i + 1)
                    if not Pfirst:
                        dve.wait_ge(S["pe_out"], 2 * i)
                    else:
                        dve.wait_ge(S["pool_const2"], 1)
                    nc.vector.tensor_tensor(kv_sb, bank[3][:, 0:K * P].rearrange("p (k n) -> p k n", k=K),
                                            block_mask[:, :].rearrange("p (o n) -> p o n", o=1).to_broadcast([P, K, P]), ALU.mult).then_inc(S["dve_kv"], 1)
                if R:
                    hidden(1)
                    hidden(2)
                if Q:
                    dve.wait_ge(S["pool_un"], i)
                    if not Qfirst:
                        dve.wait_ge(S["pe_tro"], 2 * (i - 1))
                    nc.vector.tensor_tensor(on, o_sb, un, ALU.mult).then_inc(S["dve_on"], 1)
                if Nx:
                    dve.wait_ge(S["pool_r1"], i + 2)
                    dve.wait_ge(S["pe_trx"], 2 * (i + 1))
                    if isinstance(i, int) and i == 0:
                        dve.wait_ge(S["dve_xn"], 1)
                    for t in range(T):
                        last = nc.vector.tensor_scalar(xn[:, t, :], xb[:, t, :], mv1[:, t, 0:1], r1[:, t:t + 1], ALU.subtract, ALU.mult)
                    last.then_inc(S["dve_xn"], 1)
                if R:
                    n0 = ch.n
                    dve.wait_ge(S["pe_pos"], b + 1)
                    nc.vector.tensor_tensor(posi[:, :, :], bank[2][:, 0:T * E].rearrange("p (t e) -> p t e", t=T), penalty, ALU.add).then_inc(S["dve_pos"], 1)
                    ch.link(nc.vector.tensor_reduce(taken_now, sel[:, :, :].rearrange("p t e -> p e t"), AX.X, ALU.add))
                    dve.wait_ge(S["dve_pos"], 2 * b + 1)
                    nc.vector.tensor_tensor(taken[:, :], taken[:, :], taken_now, ALU.add).then_inc(S["dve_pos"], 1)
                    nc.vector.tensor_scalar(lo_i[:, :, :], posi[:, :, :], LO - 1, None, ALU.bitwise_and)
                    ch.link(nc.vector.tensor_scalar(hi_i[:, :, :], posi[:, :, :], 4, None, ALU.logical_shift_right))
                    nc.vector.tensor_copy(lo_h[:, :, :], lo_i[:, :, :])
                    ch.link(nc.vector.tensor_copy(hi_h[:, :, :], hi_i[:, :, :]))
                    if not Rfirst:
                        dve.wait_ge(S["pe_table"], 2 * b)
                    for t in range(T):
                        nc.vector.tensor_tensor(onehot_lo[:, t], lo_h[:, t:t + 1, :].to_broadcast([P, LO, E]), iota_lo[:, :, :], ALU.is_equal)
                        last = nc.vector.tensor_tensor(onehot_hi[:, t], hi_h[:, t].rearrange("p (g o e) -> p g o e", g=G, o=1).to_broadcast([P, G, HI, GE]), iota_hi[:, :, :, :], ALU.is_equal)
                    ch.link(last)
                    code_b = at(token_code, b)
                    for t in range(T):
                        last = nc.vector.tensor_scalar(onehot_hi[:, t], onehot_hi[:, t], code_b[:, t:t + 1], None, ALU.mult)
                    last.then_inc(S["dve_onehot"], 1)
                if Q:
                    if not Qfirst:
                        dve.wait_ge(S["pe_wo"], 2 * (i - 1))
                    transposed_lo(oT_lo, oT_hi, (0, 1), "act_oT", 2 * (i - 1), "dve_oT")
                if Nx:
                    dve.wait_ge(S["pe_u"], 2 * i + 2)
                    transposed_lo(xT_lo, xT_hi, (2, 3), "act_xT", 2 * (i + 1), "dve_xT")
                if Q:
                    n0 = ch.n
                    bq = i - 1
                    x1 = at(resid, bq)
                    y = [bank[6 + t // 2][:, (t % 2) * D:(t % 2 + 1) * D] for t in range(T)]
                    norm_stats(y, stats2, mv2, ve2, ch, "dve_mv2", ("pe_wo", 2 * i))
                    dve.wait_ge(S["pool_r2"], i)
                    for t in range(T):
                        last = nc.vector.tensor_scalar(y_sb[:, t, :], y[t], mv2[:, t, 0:1], r2[:, t:t + 1], ALU.subtract, ALU.mult)
                    last.then_inc(S["dve_yn"], 1)
                    dve.wait_ge(S["dve_yn"], i)
                    nc.vector.tensor_tensor(x1, x1, y_sb, ALU.add).then_inc(S["dve_x1"], 1)
                    norm_stats([x1[:, t, :] for t in range(T)], stats3, mv3, ve3, ch, "dve_mv3", ("dve_x1", i))
                if R:
                    for c_ in range(2):
                        dve.wait_ge(S["pe_table"], 2 * b + c_ + 1)
                        tb = table[:, 2 * c_:2 * c_ + 2].rearrange("p g l e -> p (g l e)")
                        nc.vector.tensor_tensor(tb, tb, bank[c_][:, :], ALU.add).then_inc(S["dve_table"], 1)
                if Q:
                    dve.wait_ge(S["pool_r3"], i)
                    if not Qfirst:
                        dve.wait_ge(S["dma_rows"], 16 * (i - 1))
                    for t in range(T):
                        last = nc.vector.tensor_scalar(xg[:, t, 0:D], x1[:, t, :], mv3[:, t, 0:1], r3[:, t:t + 1], ALU.subtract, ALU.mult)
                    last.then_inc(S["dve_xn2"], 1)
                    if not Qfirst:
                        dve.wait_ge(S["pe_up"], 3 * (i - 1))
                        dve.wait_ge(S["pe_gate"], i - 1)
                    transposed_lo(x2T_lo, x2T_hi, (2, 3), "act_x2T", 2 * (i - 1), "dve_x2T")
                per = PER_N * Nx + PER_Q * Q + PER_R * R
                assert ch.n == per, (ch.n, per, Nx, Q, R)

            steps(dve, body)
            tail = Chain(links_before(B + 2))

            dve.wait_ge(S["dve_table"], 2 * B)
            own = work[:, 0:GE]
            dve.wait_ge(S["pe_down"], 2 * B)
            tail.link(nc.vector.tensor_copy(own, ident[:, 0:GE]))
            for h in range(1, HI):
                tail.link(nc.vector.tensor_tensor(own, own, ident[:, h * GE:(h + 1) * GE], ALU.add))
            masked = work[:, 1024:1024 + G * LO * GE].rearrange("p (n e) -> p n e", e=GE)
            tail.link(nc.vector.tensor_tensor(masked, table[:, :, :, :].rearrange("p g l e -> p (g l) e"),
                                              own.rearrange("p (o e) -> p o e", o=1).to_broadcast([P, G * LO, GE]), ALU.mult))
            nc.vector.tensor_reduce(sq[:, 0, 0:G * LO], masked, AX.X, ALU.add).then_inc(S["dve_index"], 1)

            dve.wait_ge(S["pe_code"], 1)
            cd = bank[0][:, 0:E]
            neg, used = logit[:, 0, :], logit[:, 1, :]
            nc.vector.tensor_scalar(neg, cd, 0.0, float(N // 2), ALU.is_lt, ALU.add)
            tail.link(nc.vector.tensor_scalar(used, cd, 0.0, None, ALU.not_equal))
            tail.link(nc.vector.tensor_tensor(code, cd, neg, ALU.add))
            tail.link(nc.vector.tensor_tensor(code, code, used, ALU.mult))
            tail.link(nc.vector.tensor_scalar(used, used, -1.0, 1.0, ALU.mult, ALU.add))
            nc.vector.tensor_copy(gather_rows[:, :], code)
            nc.vector.scalar_tensor_tensor(scatter_rows[:, :], used, slot_dump[:, 0:1], code, ALU.mult, ALU.add).then_inc(S["dve_index"], 1)

            def hidden_rows(j, k, first):
                e = j * BODY + k
                dve.wait_ge(S["act_silu"], e + 1)
                if not first:
                    dve.wait_ge(S["pe_hidT"], e - 1)
                nc.vector.tensor_tensor(hid[:, k % 2], silu_a[:, k % 2], bank[2 + k % 2][:, F:2 * F], ALU.mult).then_inc(S["dve_hid"], 1)

            expert_steps(dve, lambda j, k: hidden_rows(j, k, isinstance(j, int) and k < 2), after=0)

            base = tail.n
            for b in range(B):
                room = b % 2
                dve.wait_ge(S[("dma_s0a", "dma_s0b")[room]], 16 * (b // 2 + 1))
                dve.wait_ge(S[("dma_s1a", "dma_s1b")[room]], 16 * (b // 2 + 1))
                nc.vector.tensor_tensor(total[:, room], s0[:, room], s1[:, room], ALU.add).then_inc(S["dve_total"], 1)
                dve.wait_ge(S["dve_total"], b + 1)
                norm_stats([total[:, room, t, :] for t in range(T)], stats1, mv1, ve1, tail, "dve_mvc")
                dve.wait_ge(S["pool_rc"], b + 1)
                for t in range(T):
                    last = nc.vector.tensor_scalar(total[:, room, t, :], total[:, room, t, :], mv1[:, t, 0:1], r1[:, t:t + 1], ALU.subtract, ALU.mult)
                tail.link(last)
                if b >= 2:
                    dve.wait_ge(S[f"dma_out{room}"], 16 * (b // 2))
                nc.vector.tensor_tensor(fin[:, room], resid[:, b], total[:, room], ALU.add).then_inc(S["dve_fin"], 1)

        @block.tensor
        def _(pe):
            def product(out_, pairs, start=True, stop=True):
                for n, ((ah, al), (bh, bl)) in enumerate(pairs):
                    first, last_ = start and n == 0, stop and n == len(pairs) - 1
                    nc.tensor.matmul(out_, ah, bh, start=first, stop=False)
                    nc.tensor.matmul(out_, ah, bl, start=False, stop=False)
                    last = nc.tensor.matmul(out_, al, bh, start=False, stop=last_)
                return last

            def transposes(src, banks, done):
                for c_ in range(K):
                    for t in range(T):
                        last = nc.tensor.transpose(bank[banks[c_]][:, tile_of(t)], src[:, t, c_ * P:(c_ + 1) * P], ident[:, :])
                    last.then_inc(S[done], 1)

            def parts(hi, lo, *index):
                return hi[index], lo[index]

            pe.wait_ge(S["pool_const"], 3)
            pe.wait_ge(S["pool_const2"], 1)
            pe.wait_ge(S["dve_xn"], 1)
            transposes(xn, (2, 3), "pe_trx")
            pe.wait_ge(S["dve_w"], 5)
            pe.wait_ge(S["act_w"], 5)
            ALL = slice(None)

            def body(i):
                Nx, _ = live(i, -1)
                Pr, Pfirst = live(i, 0)
                Q, Qfirst = live(i, 1)
                R, Rfirst = live(i, 2)
                b = i - 2
                if Q:
                    pe.wait_ge(S["act_q"], 2 * i)
                    pe.wait_ge(S["dve_kv"], i)
                    pe.wait_ge(S["dve_u"], 2 * i)
                    if not Qfirst:
                        pe.wait_ge(S["act_oT"], 2 * (i - 1))
                        pe.wait_ge(S["dve_oT"], 2 * (i - 1))
                    if R and not Rfirst:
                        pe.wait_ge(S["dve_table"], 2 * b)
                    for t in range(T):
                        for c_ in range(K):
                            at_ = (t % 2) * D + c_ * P
                            last = nc.tensor.matmul(bank[t // 2][:, at_:at_ + P], q_sb[:, c_, tile_of(t)], kv_sb[:, c_, :], start=True, stop=True)
                        if t % 2:
                            last.then_inc(S["pe_out"], 1)
                if R:
                    pe.wait_ge(S["act_x2T"], 2 * b + 2)
                    pe.wait_ge(S["dve_x2T"], 2 * b + 2)
                    for t in range(T):
                        last = product(bank[2][:, t * E:(t + 1) * E],
                                       [(parts(x2T_hi, x2T_lo, ALL, k, tile_of(t)), parts(g_hi, g_lo, ALL, k, ALL)) for k in range(K)])
                    last.then_inc(S["pe_gate"], 1)
                if Pr:
                    pe.wait_ge(S["act_xT"], 2 * i + 2)
                    pe.wait_ge(S["dve_xT"], 2 * i + 2)
                    for c_ in range(K):
                        if Q:
                            pe.wait_ge(S["act_o"], 2 * (i - 1) + c_ + 1)
                        last = product(bank[c_][:, :], [(parts(w_hi, w_lo, ALL, k, slice(c_ * P, (c_ + 1) * P)), parts(xT_hi, xT_lo, ALL, k, ALL)) for k in range(K)])
                        last.then_inc(S["pe_q"], 1)
                    for t in range(T):
                        if t < 2:
                            pe.wait_ge(S["act_q"], 2 * i + t + 1)
                        else:
                            pe.wait_ge(S["act_k"], 4 * i + t - 1)
                            pe.wait_ge(S["dve_v"], 4 * i + t - 1)
                        last = product(bank[t % 2][:, :], [(parts(xT_hi, xT_lo, ALL, k, tile_of(t)), parts(w_hi, w_lo, ALL, k, slice(D, 3 * D))) for k in range(K)])
                        last.then_inc(S["pe_kvp"], 1)
                    for t in range(T):
                        if t % 2 == 0:
                            pe.wait_ge(S["act_k"], 4 * i + 3 + t // 2)
                            pe.wait_ge(S["dve_v"], 4 * i + 3 + t // 2)
                        last = product(bank[t // 2][:, (t % 2) * D:(t % 2 + 1) * D],
                                       [(parts(xT_hi, xT_lo, ALL, k, tile_of(t)), parts(w_hi, w_lo, ALL, k, slice(3 * D, 4 * D))) for k in range(K)])
                        if t % 2:
                            last.then_inc(S["pe_u"], 1)

                def up(j):
                    o, w = CHUNKS[j]
                    for half, bk in enumerate(((4, 5), (6, 7), (4, 5))[j]):
                        cols = slice(half * FS + o, half * FS + o + w)
                        last = product(bank[bk][0:w, :], [(parts(s13_hi, s13_lo, ALL, k, cols), parts(x2T_hi, x2T_lo, ALL, k, ALL)) for k in range(K)])
                    last.then_inc(S["pe_up"], 1)

                if R:
                    if not Rfirst:
                        pe.wait_ge(S["act_z"], 2 * b)
                    up(0)
                if Pr:
                    if Q and not Qfirst:
                        pe.wait_ge(S["act_x2T"], 2 * (i - 1))
                        pe.wait_ge(S["dve_x2T"], 2 * (i - 1))
                    pe.wait_ge(S["act_k"], 4 * i + 4)
                    pe.wait_ge(S["dve_v"], 4 * i + 4)
                    for c_ in range(K):
                        for t in range(T):
                            last = nc.tensor.matmul(bank[3][:, c_ * P:(c_ + 1) * P], k_sb[:, t, c_ * P:(c_ + 1) * P], v_sb[:, t, c_ * P:(c_ + 1) * P],
                                                    start=(t == 0), stop=(t == T - 1))
                    last.then_inc(S["pe_kv"], 1)
                if R:
                    pe.wait_ge(S["dve_yn"], i - 1)
                    up(1)
                    pe.wait_ge(S["dve_h"], 3 * b + 1)
                    up(2)
                    pe.wait_ge(S["dve_logit"], b + 1)
                    pe.wait_ge(S["dve_sel"], b + 1)
                    if not Rfirst:
                        pe.wait_ge(S["dve_pos"], 2 * b)
                    for t in range(T):
                        at_ = bank[2][:, t * E:(t + 1) * E]
                        nc.tensor.matmul(at_, before[:, :], sel[:, t, :], start=True, stop=False)
                        for t_ in range(t):
                            nc.tensor.matmul(at_, ones[:, :], sel[:, t_, :], start=False, stop=False)
                        last = nc.tensor.matmul(at_, ones[:, :], taken[:, :], start=False, stop=True)
                    last.then_inc(S["pe_pos"], 1)
                if Q:
                    pe.wait_ge(S["dve_on"], i)
                    if Pr:
                        pe.wait_ge(S["dve_u"], 2 * (i + 1))
                    else:
                        pe.wait_ge(S["act_o"], 2 * i)
                    transposes(on, (0, 1), "pe_tro")
                if Nx:
                    pe.wait_ge(S["dve_xn"], i + 2)
                    pe.wait_ge(S["dve_kv"], i + 1)
                    if R:
                        pe.wait_ge(S["dve_pos"], 2 * b + 1)
                    transposes(xn, (2, 3), "pe_trx")
                if Q:
                    pe.wait_ge(S["act_oT"], 2 * i)
                    pe.wait_ge(S["dve_oT"], 2 * i)
                    if R:
                        pe.wait_ge(S["dve_h"], 3 * b + 2)
                    for t in range(T):
                        last = product(bank[6 + t // 2][:, (t % 2) * D:(t % 2 + 1) * D],
                                       [(parts(oT_hi, oT_lo, ALL, k, tile_of(t)), parts(w_hi, w_lo, ALL, k, slice(4 * D, 5 * D))) for k in range(K)])
                        if t % 2:
                            last.then_inc(S["pe_wo"], 1)
                if R:
                    pe.wait_ge(S["dve_h"], 3 * b + 3)
                    pe.wait_ge(S["act_hT"], 3 * b + 3)
                    pe.wait_ge(S["pool_hT"], 3 * b + 3)
                    for t in range(T):
                        last = product(bank[4 + t // 2][:, (t % 2) * D:(t % 2 + 1) * D],
                                       [((hT_hi[0:w, j, tile_of(t)], hT_lo[0:w, j, tile_of(t)]), (s2_hi[0:w, j, :], s2_lo[0:w, j, :]))
                                        for j, (_, w) in enumerate(CHUNKS)])
                        if t % 2:
                            last.then_inc(S["pe_down"], 1)
                    pe.wait_ge(S["dve_onehot"], b + 1)
                    if not Q:
                        pe.wait_ge(S["dve_table"], 2 * b)
                    for g in range(G):
                        for t in range(T):
                            last = nc.tensor.matmul(bank[g // 2][:, (g % 2) * D:(g % 2 + 1) * D],
                                                    onehot_hi[:, t, g].rearrange("p h e -> p (h e)"), onehot_lo[:, t, :, g * GE:(g + 1) * GE],
                                                    start=(t == 0), stop=(t == T - 1))
                        if g % 2:
                            last.then_inc(S["pe_table"], 1)
                if Q:
                    pe.wait_ge(S["dve_xn2"], i)
                    if Nx:
                        pe.wait_ge(S["act_xT"], 2 * (i + 2))
                        pe.wait_ge(S["dve_xT"], 2 * (i + 2))
                    else:
                        pe.wait_ge(S["dve_pos"], 2 * b + 1)
                        pe.wait_ge(S["dve_kv"], B)
                    transposes(xg, (2, 3), "pe_trx2")

            steps(pe, body)

            pe.wait_ge(S["dma_table_back"], 16)
            nc.tensor.transpose(bank[0][:, 0:E], sq[0:E, 1, 0:CAP], ident[0:E, 0:E]).then_inc(S["pe_code"], 1)

            def tokens_T(j, k, first):
                e = j * BODY + k
                pe.wait_ge(dma_xe[k % XS], 16 * (share(j, k, XS) + 1))
                if not first:
                    pe.wait_ge(S["act_xeT"], e - 1)
                for c_ in range(K):
                    last = nc.tensor.transpose(bank[k % 2][:, c_ * P:(c_ + 1) * P], xe[:, k % XS, c_ * P:(c_ + 1) * P], ident[:, :])
                last.then_inc(S["pe_xeT"], 1)

            def expert_up(j, k, first):
                e = j * BODY + k
                slot = (k // 2) % WB
                pe.wait_ge(dma_w13[slot], 16 * (share(j, k, BODY) + 1))
                pe.wait_ge(S["act_xeT"], e + 1)
                if not first:
                    pe.wait_ge(S["dve_hid"], e - 1)
                for c_ in range(K):
                    last = nc.tensor.matmul(bank[2 + k % 2][:, 0:2 * F], xeT[:, k % 2, c_, :], w13_sb[:, slot, k % 2, c_, :], start=(c_ == 0), stop=(c_ == K - 1))
                last.then_inc(S["pe_eup"], 1)

            def hidden_T(j, k, first):
                e = j * BODY + k
                pe.wait_ge(S["dve_hid"], e + 1)
                if not first:
                    pe.wait_ge(S["act_hidT"], e - 1)
                for c_ in range(2):
                    last = nc.tensor.transpose(bank[4 + k % 2][0:FH, c_ * P:(c_ + 1) * P], hid[:, k % 2, c_ * FH:(c_ + 1) * FH], ident[:, :])
                last.then_inc(S["pe_hidT"], 1)

            def expert_down(j, k, first):
                e = j * BODY + k
                slot = (k // 2) % WB
                pe.wait_ge(dma_w2[slot], 16 * (share(j, k, BODY) + 1))
                pe.wait_ge(S["act_hidT"], e + 1)
                if not first:
                    pe.wait_ge(S["act_ye"], e - 1)
                for c_ in range(2):
                    last = nc.tensor.matmul(bank[6 + k % 2][:, 0:D], hidT[0:FH, k % 2, c_, :], w2_sb[0:FH, slot, k % 2, c_, :], start=(c_ == 0), stop=(c_ == 1))
                last.then_inc(S["pe_edown"], 1)

            pe.wait_ge(S["dve_index"], 2)
            tokens_T(0, 0, True)

            def experts(j, k):
                known = isinstance(j, int)
                if not known or k < E:
                    expert_up(j, k, known and k < 2)
                if not known or k >= 2:
                    expert_down(j, k - 2, known and k < 4)
                if not known or 1 <= k <= E:
                    hidden_T(j, k - 1, known and k < 3)
                if not known or k + 1 < E:
                    tokens_T(j, k + 1, known and k < 1)

            expert_steps(pe, experts)


def kernel(L0_attn_x, L0_attn_Wq, L0_attn_Wk, L0_attn_Wv, L0_attn_Wu, L0_attn_Wo, L0_ffn_gate_w, L0_ffn_w1, L0_ffn_w2,
           L0_ffn_w3, L0_ffn_sw1, L0_ffn_sw2, L0_ffn_sw3):
    import concourse.bacc as bacc
    from concourse.bass_utils import run_bass_kernel_spmd

    def features_first(w):
        return np.asarray(w).T.reshape(K, P, -1).transpose(1, 0, 2)

    w1, w2, w3 = (np.asarray(w) for w in (L0_ffn_w1, L0_ffn_w2, L0_ffn_w3))
    both = np.concatenate([w1, w3], axis=1)
    arrays = {
        "x": L0_attn_x, "wq": L0_attn_Wq, "wk": L0_attn_Wk, "wv": L0_attn_Wv, "wu": L0_attn_Wu, "wo": L0_attn_Wo,
        "gate_w": features_first(L0_ffn_gate_w),
        "w13": both.transpose(2, 0, 1).reshape(K, P, E, 2 * F).transpose(1, 2, 0, 3),
        "w2": w2.transpose(2, 0, 1).reshape(2, FH, E, D).transpose(1, 2, 0, 3),
        "sw13": features_first(np.concatenate([np.asarray(L0_ffn_sw1), np.asarray(L0_ffn_sw3)], axis=0)),
        "sw2": np.asarray(L0_ffn_sw2).T,
    }
    arrays = {n: np.ascontiguousarray(a) for n, a in arrays.items()}
    nc = bacc.Bacc("TRN2", target_bir_lowering=False, num_devices=1)
    aps = [nc.dram_tensor(n, a.shape, mybir.dt.from_np(a.dtype), kind="ExternalInput").ap() for n, a in arrays.items()]
    result = nc.dram_tensor("result", (B, L, D), F32, kind="ExternalOutput").ap()
    build(nc, *aps, result)
    r = run_bass_kernel_spmd(nc, [arrays], core_ids=[0])
    return r.results[0]["result"]
```

```python
from contextlib import ExitStack

import concourse.bass as bass
import numpy as np
from concourse import mybir

F32, F32R, F16, BF16 = mybir.dt.float32, mybir.dt.float32r, mybir.dt.float16, mybir.dt.bfloat16
I32, U32 = mybir.dt.int32, mybir.dt.uint32
ALU, ACT, AX = mybir.AluOpType, mybir.ActivationFunctionType, mybir.AxisListType

P = 128
B, L, D = 8, 512, 256
T = L // P
K = D // P
N = B * L
H, DH = 16, 16
E, F, CAP, TOPK = 64, 176, 128, 6
FS = 2 * F
FH = F // 2
EPS, EPS_NORM = 1e-5, 1e-12
ROW = D + E
CHUNKS = [(0, 128), (128, 128), (256, 96)]
HI, LO = 8, 16
GE = P // HI
G = E // GE
ACC_ROWS = 1 + N + P
PEEL = 3
WB = 4
AHEAD = 4
BODY = 2 * WB
EARLY = 2 * 2 * (K * 2 * F + 2 * D)
WORK = EARLY + 13312


def build(nc, x, wq, wk, wv, wu, wo, gate_w, w13, w2, sw13, sw2, out):
    ctx = ExitStack()
    with ctx:
        def sb(name, shape, dt=F32):
            return ctx.enter_context(nc.sbuf_tensor(name, shape, dt))

        def sem(name):
            return ctx.enter_context(nc.semaphore(name))

        rows = nc.dram_tensor("token_rows", (1 + N, ROW), F32, kind="Internal").ap()
        sums = [nc.dram_tensor(f"sums{j}", (ACC_ROWS, D), F32, kind="Internal").ap() for j in range(2)]
        slot_table = nc.dram_tensor("slot_table", (E, CAP), F32, kind="Internal").ap()

        resid = sb("resid", [P, B, T, D])
        WCOLS = 5 * D
        w_hi, w_lo = sb("w_hi", [P, K, WCOLS], F32R), sb("w_lo", [P, K, WCOLS], F32R)
        s13_hi, s13_lo = sb("s13_hi", [P, K, 2 * FS], F32R), sb("s13_lo", [P, K, 2 * FS], F32R)
        s2_hi, s2_lo = sb("s2_hi", [P, 3, D], F32R), sb("s2_lo", [P, 3, D], F32R)
        g_hi, g_lo = sb("g_hi", [P, K, E], F32R), sb("g_lo", [P, K, E], F32R)
        xT_hi, xT_lo = sb("xT_hi", [P, K, L], F32R), sb("xT_lo", [P, K, L], F32R)
        oT_hi, oT_lo = sb("oT_hi", [P, K, L], F32R), sb("oT_lo", [P, K, L], F32R)
        x2T_hi, x2T_lo = sb("x2T_hi", [P, K, L], F32R), sb("x2T_lo", [P, K, L], F32R)
        hT_hi, hT_lo = sb("hT_hi", [P, 3, L], F32R), sb("hT_lo", [P, 3, L], F32R)
        onehot_hi = sb("onehot_hi", [P, T, G, HI, GE], F16)
        onehot_lo = sb("onehot_lo", [P, T, LO, E], F16)
        ident = sb("ident", [P, P])
        block_mask = sb("block_mask", [P, P])
        before = sb("before", [P, P], BF16)
        ones = sb("ones", [P, P], BF16)
        iota_hi = sb("iota_hi", [P, G, HI, GE], F16)
        iota_lo = sb("iota_lo", [P, LO, E], F16)
        token_code = sb("token_code", [P, B, T])
        slot_dump = sb("slot_dump", [P, 1])
        own = sb("own", [P, GE])
        neg_half = sb("neg_half", [P, T * H])
        table = sb("table", [P, G, LO, GE])
        taken = sb("taken", [P, E], BF16)
        gather_rows, scatter_rows = sb("gather_rows", [P, E], U32), sb("scatter_rows", [P, E], U32)
        small = sb("small", [P, 1010])
        work = sb("work", [P, WORK])

        class Carve:
            def __init__(self, tensor):
                self.tensor, self.at = tensor, 0

            def take(self, *shape):
                n = int(np.prod(shape))
                view = self.tensor[:, self.at:self.at + n]
                self.at += n
                names = "abcd"[:len(shape)]
                if len(shape) > 1:
                    view = view.rearrange(f"p ({' '.join(names)}) -> p {' '.join(names)}",
                                          **dict(zip(names[1:], shape[1:])))
                return view

        s = Carve(small)
        stats1, mv1, ve1, r1 = s.take(T, 6), s.take(T, 2), s.take(T), s.take(T)
        stats2, mv2, ve2, r2 = s.take(T, 6), s.take(T, 2), s.take(T), s.take(T)
        stats3, mv3, ve3, r3 = s.take(T, 6), s.take(T, 2), s.take(T), s.take(T)
        statsc, mvc, vec, rc = s.take(T, 6), s.take(2, T, 2), s.take(2, T), s.take(2, T)
        power, norm = s.take(T * H), s.take(T * H)
        top, expsum, expinv, top8 = s.take(T), s.take(T), s.take(T), s.take(T, 8)
        padded = s.take(T, E + 2)
        replaced = s.take(T, E + 2)
        taken_now = s.take(E)
        code = s.take(E)

        a = Carve(work)
        th, k_sb, v_sb, xn = (a.take(T, D) for _ in range(4))
        a.take(EARLY - a.at)
        u_sb, o_sb, sq = (a.take(T, D) for _ in range(3))
        q_sb = a.take(K, L)
        on, y_sb, un = (a.take(T, D) for _ in range(3))
        xg = a.take(T, ROW)
        tu, hT = a.take(3, L), a.take(3, L)
        z_sb = a.take(T, D)
        kv_sb = a.take(K, P)
        logit, penalty = (a.take(T, E) for _ in range(2))
        assert a.at <= WORK
        posi, lo_i, hi_i = (sb(n, [P, T, E], I32) for n in ("posi", "lo_i", "hi_i"))
        lo_h, hi_h = sb("lo_h", [P, T, E], F16), sb("hi_h", [P, T, E], F16)
        sel = sb("sel", [P, T, E], BF16)
        r = Carve(work)
        r.at = EARLY + 4 * T * D
        raw_w = r.take(K, WCOLS)
        raw_13 = r.take(K, 2 * FS)
        raw_2 = r.take(3, D)
        raw_g = r.take(K, E)
        zeros = r.take(D)
        assert r.at <= WORK

        m = Carve(work)
        w13_sb, w2_sb = [None] * WB, [None] * WB
        for room in range(WB):
            w13_sb[room], w2_sb[room] = m.take(2, K, 2 * F), m.take(2, 2, D)
            assert room != 1 or m.at == EARLY
        XS = 8
        xe = m.take(XS, ROW)
        xeT = m.take(2, K, P)
        silu_a, hid = m.take(2, F), m.take(2, F)
        hidT = m.take(2, 2, P)
        ye = m.take(4, D)
        assert m.at <= WORK
        rows_now = sb("rows_now", [P, XS], U32)
        dest_now = sb("dest_now", [P, 4], U32)

        CS = 3
        c = Carve(work)
        s0, s1, total, fin = (c.take(CS, T, D) for _ in range(4))
        assert c.at <= WORK

        bank = [ctx.enter_context(nc.psum_tensor(f"bank{j}", [P, 512], F32)) for j in range(8)]

        names = """dma_wg dma_w13 dma_w2 dma_z dma_rows dma_table dma_table_back dma_zero_rows dma_zero0 dma_zero1
            pool_const pool_const2 dve_const act_w dve_w
            dve_mv1 pool_r1 dve_xn pe_trx act_xT dve_xT
            pe_q pe_kvp pe_u act_q act_kv act_th dve_u pe_kv dve_kv
            pe_out act_o act_sq dve_power pool_norm pool_un dve_on pe_tro act_oT dve_oT pe_wo
            dve_mv2 pool_r2 dve_yn dve_x1 dve_mv3 pool_r3 dve_xn2 pe_trx2 act_x2T dve_x2T
            pe_gate dve_logit act_exp dve_scores dve_sel pe_pos dve_pos dve_onehot pe_table dve_table
            pe_up act_tu dve_h act_hT pool_hT pe_down act_z dve_link
            pe_code dve_index
            pe_xeT act_xeT pe_eup act_silu dve_hid pe_hidT act_hidT pe_edown act_ye
            dma_scatter0 dma_scatter1
            dve_total dve_mvc pool_rc dve_cn pool_fin dve_rows_now dve_dest_now""".split()
        S = {n: sem(n) for n in names}
        dma_x = [sem(f"dma_x{b}") for b in range(B)]
        dma_w = [sem(f"dma_w{n}") for n in ("q", "k", "v", "u", "o")]
        dma_w13 = [sem(f"dma_w13_{j}") for j in range(WB)]
        dma_w2 = [sem(f"dma_w2_{j}") for j in range(WB)]
        dma_s = [sem(f"dma_s{j}") for j in range(CS)]
        dma_out = [sem(f"dma_out{j}") for j in range(CS)]
        dma_xe = [sem(f"dma_xe{j}") for j in range(XS)]

        def wait_apart(engine, *waits):
            waits = [(S[n], v if isinstance(v, int) else engine.compute_val(v)) for n, v in waits]
            engine.wait_ge(S["pool_const"], 1)
            for semaphore, value in waits:
                engine.wait_ge(semaphore, value)

        def share(j, k, d):
            return j * (BODY // d) + k // d

        def tile_of(t):
            return slice(t * P, (t + 1) * P)

        def at(buffer, b):
            return buffer[:, b] if isinstance(b, int) else buffer[:, bass.ds(b, 1)].squeeze(1)

        def token_rows_of(tensor, b, width):
            first = 1 + b * L
            return tensor[bass.ds(first, L), 0:width].rearrange("(t p) d -> p t d", p=P)

        def steps(engine, body):
            for i in range(PEEL):
                body(i)
            with engine.Fori(PEEL, B - 1) as i:
                body(i)
            for i in range(B - 1, B + 2):
                body(i)

        def live(i, lag):
            if isinstance(i, int):
                return 0 <= i - lag < B, i == lag
            return True, False

        def expert_steps(engine, step, after=2):
            for k in range(BODY):
                step(0, k)
            with engine.Fori(1, E // BODY - 1) as j:
                for k in range(BODY):
                    step(j, k)
            for k in range(E - BODY, E + after):
                step(0, k)

        block = ctx.enter_context(nc.Block())

        @block.sync
        def _(sp):
            sp.dma_start(resid[:, 0], x[0].rearrange("(t p) d -> p t d", p=P)).then_inc(dma_x[0], 16)
            for j, w in enumerate((wq, wk, wv, wu, wo)):
                sp.dma_start(raw_w[:, :, j * D:(j + 1) * D], w.rearrange("(k p) n -> p k n", p=P)).then_inc(dma_w[j], 16)
            sp.dma_start(resid[:, 1], x[1].rearrange("(t p) d -> p t d", p=P)).then_inc(dma_x[1], 16)
            sp.dma_start(raw_g, gate_w).then_inc(S["dma_wg"], 16)
            sp.dma_start(raw_13, sw13).then_inc(S["dma_w13"], 16)
            sp.dma_start(raw_2[:, 0:2, :], sw2[0:2 * P].rearrange("(c p) n -> p c n", p=P)).then_inc(S["dma_w2"], 16)
            sp.dma_start(raw_2[0:FS - 2 * P, 2, :], sw2[2 * P:FS]).then_inc(S["dma_w2"], 16)
            for b in range(2, B):
                sp.dma_start(resid[:, b], x[b].rearrange("(t p) d -> p t d", p=P)).then_inc(dma_x[b], 16)
            sp.wait_ge(S["pool_const"], 1)
            sp.dma_start(rows[0:1, :].rearrange("o (a b) -> o a b", a=2), zeros[0:1, :].rearrange("p (o d) -> p o d", o=1).to_broadcast([1, 2, D])[:, :, 0:ROW // 2]).then_inc(S["dma_zero_rows"], 16)
            sp.dma_start(sums[0][1 + N:ACC_ROWS, :], zeros).then_inc(S["dma_zero0"], 16)
            sp.dma_start(sums[1][1:ACC_ROWS, :].rearrange("(p r) d -> p r d", p=P),
                         zeros.rearrange("p (o d) -> p o d", o=1).to_broadcast([P, (N + P) // P, D])).then_inc(S["dma_zero1"], 16)

            def load_pair(pair, slot):
                sp.dma_start(w13_sb[slot], w13[:, bass.ds(2 * pair, 2)]).then_inc(dma_w13[slot], 16)
                sp.dma_start(w2_sb[slot][0:FH], w2[:, bass.ds(2 * pair, 2)]).then_inc(dma_w2[slot], 16)

            def body(i):
                R, _ = live(i, 2)
                if isinstance(i, int) and i == B:
                    sp.wait_ge(S["dve_u"], 2 * B)
                    sp.wait_ge(S["pe_kv"], B)
                    sp.wait_ge(S["pe_trx"], 2 * B)
                    load_pair(0, 0)
                    load_pair(1, 1)
                if R:
                    b = i - 2
                    sp.wait_ge(S["dve_scores"], b + 1)
                    sp.dma_start(token_rows_of(rows, b, ROW), xg).then_inc(S["dma_rows"], 16)
                    sp.wait_ge(S["act_z"], 2 * b + 2)
                    sp.dma_start(token_rows_of(sums[0], b, D), z_sb).then_inc(S["dma_z"], 16)

            steps(sp, body)

            sp.wait_ge(S["dve_index"], 1)
            for h in range(HI):
                sp.dma_start(slot_table[:, h * LO:(h + 1) * LO].rearrange("(g e) l -> e g l", e=GE),
                             sq[h * GE:(h + 1) * GE, 0, 0:G * LO].rearrange("p (g l) -> p g l", g=G)).then_inc(S["dma_table"], 16)
            sp.wait_ge(S["dma_table"], 16 * HI)
            sp.dma_start(sq[0:E, 1, 0:CAP], slot_table).then_inc(S["dma_table_back"], 16)

            sp.wait_ge(S["dve_index"], 2)
            sp.wait_ge(S["dma_z"], 16 * B)
            for pair in range(2, WB):
                load_pair(pair, pair)
            with sp.Fori(1, E // BODY) as j:
                for slot in range(WB):
                    sp.wait_ge(S["pe_edown"], (j - 1) * BODY + 2 * slot + 2)
                    load_pair(j * WB + slot, slot)

            sp.wait_ge(S["act_ye"], E)
            sp.wait_ge(S["pe_edown"], E)
            for j in range(2):
                sp.wait_ge(S[f"dma_scatter{j}"], 16 * (E // 2))
            def load_sums(b):
                sp.dma_start(s0[:, b % CS], token_rows_of(sums[0], b, D)).then_inc(dma_s[b % CS], 16)
                sp.dma_start(s1[:, b % CS], token_rows_of(sums[1], b, D)).then_inc(dma_s[b % CS], 16)

            for b in range(CS):
                load_sums(b)
            for b in range(B):
                if b + CS < B:
                    sp.wait_ge(S["dve_total"], b + 1)
                    load_sums(b + CS)
                sp.wait_ge(S["pool_fin"], b + 1)
                sp.dma_start(out[b].rearrange("(t p) d -> p t d", p=P), fin[:, b % CS]).then_inc(dma_out[b % CS], 16)
            for room in range(CS):
                sp.wait_ge(dma_out[room], 16 * len(range(room, B, CS)))
            sp.wait_ge(S["dma_zero0"], 16)

        @block.gpsimd
        def _(pool):
            pool.memset(zeros, 0.0).then_inc(S["pool_const"], 1)
            pool.memset(ident[:, :], 0.0)
            pool.memset(block_mask[:, :], 1.0)
            pool.memset(before[:, :], 1.0)
            pool.memset(ones[:, :], 1.0)
            pool.memset(neg_half[:, :], -0.5)
            pool.memset(taken[:, :], 0.0)
            pool.memset(table[:, :, :, :], 0.0)
            pool.memset(padded[:, :, E:E + 2], 2.0)
            pool.iota(iota_hi[:, :, :, :], pattern=[[0, G], [1, HI], [0, GE]], base=0, channel_multiplier=0, allow_small_or_imprecise_dtypes=True)
            pool.iota(iota_lo[:, :, :], pattern=[[1, LO], [0, E]], base=0, channel_multiplier=0, allow_small_or_imprecise_dtypes=True)
            pool.iota(token_code[:, :, :], pattern=[[L, B], [P, T]], base=-N // 2, channel_multiplier=1, allow_small_or_imprecise_dtypes=True)
            pool.iota(slot_dump[:, :], pattern=[[0, 1]], base=1 + N, channel_multiplier=1, allow_small_or_imprecise_dtypes=True).then_inc(S["pool_const"], 1)
            pool.wait_ge(S["pool_const"], 2)
            pool.affine_select(out=ident[:, :], in_=ident[:, :], compare_op=ALU.not_equal, fill=1.0, base=0,
                               pattern=[[-1, P]], channel_multiplier=1)
            pool.affine_select(out=before[:, :], in_=before[:, :], compare_op=ALU.is_ge, fill=0.0, base=-1,
                               pattern=[[1, P]], channel_multiplier=-1)
            blocks = block_mask[:, :].rearrange("p (h d) -> p h d", d=DH)
            pool.affine_select(out=blocks, in_=blocks, compare_op=ALU.is_ge, fill=0.0, base=0,
                               pattern=[[-DH, P // DH], [0, DH]], channel_multiplier=1).then_inc(S["pool_const"], 1)
            pool.wait_ge(S["pool_const"], 3)
            pool.affine_select(out=blocks, in_=blocks, compare_op=ALU.is_ge, fill=0.0, base=DH - 1,
                               pattern=[[DH, P // DH], [0, DH]], channel_multiplier=-1).then_inc(S["pool_const2"], 1)

            def inverse_root(out_, in_, ready, value, done):
                pool.wait_ge(S[ready], value)
                pool.tensor_tensor(out_, in_, neg_half[:, 0:in_.shape[1]], ALU.pow).then_inc(S[done], 1)

            inverse_root(r1, ve1, "dve_mv1", 1, "pool_r1")

            def body(i):
                Nx, _ = live(i, -1)
                Q, _ = live(i, 1)
                R, _ = live(i, 2)
                if Q:
                    inverse_root(norm, power, "dve_power", i, "pool_norm")
                if Nx:
                    inverse_root(r1, ve1, "dve_mv1", i + 2, "pool_r1")
                if Q:
                    pool.wait_ge(S["dve_u"], 2 * i)
                    pool.wait_ge(S["pool_norm"], i)
                    if not live(i, 1)[1]:
                        pool.wait_ge(S["dve_on"], i - 1)
                    pool.tensor_tensor(un.rearrange("p t (h d) -> p (t h) d", d=DH), u_sb.rearrange("p t (h d) -> p (t h) d", d=DH),
                                       norm.rearrange("p (n o) -> p n o", o=1).to_broadcast([P, T * H, DH]), ALU.mult).then_inc(S["pool_un"], 1)
                if R:
                    b = i - 2
                    if not live(i, 2)[1]:
                        pool.wait_ge(S["pe_down"], 2 * b)
                    for j, (_, w) in enumerate(CHUNKS):
                        pool.wait_ge(S["act_hT"], 3 * b + j + 1)
                        pool.tensor_tensor(hT_lo[0:w, j, :], hT[0:w, j, :], hT_hi[0:w, j, :].bitcast(F32), ALU.subtract).then_inc(S["pool_hT"], 1)
                if Q:
                    inverse_root(r2, ve2, "dve_mv2", i, "pool_r2")
                    inverse_root(r3, ve3, "dve_mv3", i, "pool_r3")

            steps(pool, body)

            pool.wait_ge(S["dve_index"], 2)
            pool.wait_ge(S["dma_rows"], 16 * B)
            pool.wait_ge(S["dma_zero_rows"], 16)
            pool.wait_ge(S["dma_zero0"], 16)
            pool.wait_ge(S["dma_zero1"], 16)
            pool.wait_ge(S["dma_z"], 16 * B)

            def gather(j, k):
                e = j * BODY + k
                wait_apart(pool, ("dve_rows_now", e + 1))
                pool.indirect_dma_start(out=xe[:, k % XS, :], out_offset=None, in_=rows,
                                        in_offset=bass.IndirectOffsetOnAxis(ap=rows_now[:, k % XS:k % XS + 1], axis=0)).then_inc(dma_xe[k % XS], 16)

            def scatter(j, k, first):
                e = j * BODY + k
                landed = [] if first else [(f"dma_scatter{k % 2}", 16 * share(j, k, 2))]
                wait_apart(pool, ("act_ye", e + 1), ("dve_dest_now", e + 1), *landed)
                pool.indirect_dma_start(out=sums[k % 2], out_offset=bass.IndirectOffsetOnAxis(ap=dest_now[:, k % 4:k % 4 + 1], axis=0),
                                        in_=ye[:, k % 4, :], in_offset=None, compute_op=ALU.add).then_inc(S[f"dma_scatter{k % 2}"], 16)

            for e in range(AHEAD):
                gather(0, e)

            def experts(j, k):
                known = isinstance(j, int)
                if not known or k + AHEAD < E:
                    gather(j, k + AHEAD)
                if not known or k >= 2:
                    scatter(j, k - 2, known and k < 4)

            expert_steps(pool, experts)

            for b in range(B):
                inverse_root(rc[:, b % 2], vec[:, b % 2], "dve_mvc", b + 1, "pool_rc")
                pool.wait_ge(S["dve_cn"], b + 1)
                if b >= CS:
                    pool.wait_ge(dma_out[b % CS], 16 * (b // CS))
                pool.tensor_tensor(fin[:, b % CS], resid[:, b], total[:, b % CS], ALU.add).then_inc(S["pool_fin"], 1)

        @block.scalar
        def _(act):
            def hi_part(out_, in_, done):
                nc.scalar.activation(out_, in_, ACT.Copy).then_inc(S[done], 1)

            def weights_hi(n):
                act.wait_ge(dma_w[n], 16)
                hi_part(w_hi[:, :, n * D:(n + 1) * D], raw_w[:, :, n * D:(n + 1) * D], "act_w")

            def transposed_hi(out_, banks, ready, value, done):
                for c_ in range(K):
                    act.wait_ge(S[ready], value + c_ + 1)
                    hi_part(out_[:, c_, :], bank[banks[c_]][:, :], done)

            for n in range(4):
                weights_hi(n)
            transposed_hi(xT_hi, (2, 3), "pe_trx", 0, "act_xT")
            weights_hi(4)
            act.wait_ge(S["dma_wg"], 16)
            hi_part(g_hi[:, :, :], raw_g, "act_w")
            act.wait_ge(S["dma_w13"], 16)
            hi_part(s13_hi[:, :, :], raw_13, "act_w")
            act.wait_ge(S["dma_w2"], 32)
            hi_part(s2_hi[:, 0:2, :], raw_2[:, 0:2, :], "act_w")
            hi_part(s2_hi[0:FS - 2 * P, 2, :], raw_2[0:FS - 2 * P, 2, :], "act_w")

            def half(ap, c_):
                return ap[:, 2 * c_:2 * c_ + 2, :].rearrange("p t d -> p (t d)")

            def body(i):
                Nx, _ = live(i, -1)
                Pr, Pfirst = live(i, 0)
                Q, Qfirst = live(i, 1)
                R, Rfirst = live(i, 2)
                b = i - 2
                if Q:
                    if not Qfirst:
                        act.wait_ge(S["dve_on"], i - 1)
                        act.wait_ge(S["dve_power"], i - 1)
                    for c_ in range(2):
                        act.wait_ge(S["pe_out"], 2 * (i - 1) + c_ + 1)
                        nc.scalar.activation(half(sq, c_), bank[c_][:, :], ACT.Square).then_inc(S["act_sq"], 1)
                        nc.scalar.activation(half(o_sb, c_), bank[c_][:, :], ACT.Copy).then_inc(S["act_o"], 1)
                if Pr:
                    for c_ in range(K):
                        act.wait_ge(S["pe_q"], 2 * i + c_ + 1)
                        if not Pfirst:
                            act.wait_ge(S["pe_out"], 2 * i)
                        nc.scalar.activation(q_sb[:, c_, :], bank[c_][:, :], ACT.Relu, scale=0.25).then_inc(S["act_q"], 1)

                def keys_values(t):
                    act.wait_ge(S["pe_kvp"], 4 * i + t + 1)
                    if not Pfirst:
                        act.wait_ge(S["pe_kv"], i)
                    nc.scalar.activation(k_sb[:, t, :], bank[t % 2][:, 0:D], ACT.Relu, scale=0.25)
                    nc.scalar.activation(v_sb[:, t, :], bank[t % 2][:, D:2 * D], ACT.Copy).then_inc(S["act_kv"], 1)

                if Pr:
                    keys_values(0)
                    keys_values(1)
                if R:
                    if not Rfirst:
                        act.wait_ge(S["pe_up"], 3 * b)
                        act.wait_ge(S["pe_gate"], b)
                    transposed_hi(x2T_hi, (2, 3), "pe_trx2", 2 * b, "act_x2T")
                if Pr:
                    keys_values(2)
                    keys_values(3)
                if R:
                    if Rfirst:
                        for n in ("dma_zero_rows", "dma_zero0", "dma_zero1"):
                            act.wait_ge(S[n], 16)
                    act.wait_ge(S["dve_logit"], i - 1)
                    nc.scalar.activation(logit, logit, ACT.Exp).then_inc(S["act_exp"], 1)
                if Pr:
                    for c_ in range(2):
                        act.wait_ge(S["pe_u"], 2 * i + c_ + 1)
                        if not Pfirst:
                            act.wait_ge(S["dve_u"], 2 * i)
                        nc.scalar.activation(half(th, c_), bank[c_][:, :], ACT.Tanh, scale=0.5).then_inc(S["act_th"], 1)

                def up_tanh(j):
                    w = CHUNKS[j][1]
                    act.wait_ge(S["pe_up"], 3 * b + j + 1)
                    if not Rfirst:
                        act.wait_ge(S["dve_h"], 3 * b)
                    nc.scalar.activation(tu[0:w, j, :], bank[(4, 6, 4)[j]][0:w, :], ACT.Tanh, scale=0.5).then_inc(S["act_tu"], 1)

                def up_hi(j):
                    w = CHUNKS[j][1]
                    act.wait_ge(S["dve_h"], 3 * b + j + 1)
                    if not Rfirst:
                        act.wait_ge(S["pe_down"], 2 * b)
                        act.wait_ge(S["pool_hT"], 3 * b)
                    hi_part(hT_hi[0:w, j, :], hT[0:w, j, :], "act_hT")

                if R:
                    up_tanh(0)
                    up_tanh(1)
                if Q:
                    if not Qfirst:
                        act.wait_ge(S["pe_wo"], 2 * (i - 1))
                        act.wait_ge(S["dve_oT"], 2 * (i - 1))
                    transposed_hi(oT_hi, (0, 1), "pe_tro", 2 * (i - 1), "act_oT")
                if R:
                    up_hi(0)
                if Nx:
                    act.wait_ge(S["pe_u"], 2 * i + 2)
                    transposed_hi(xT_hi, (2, 3), "pe_trx", 2 * (i + 1), "act_xT")
                if R:
                    up_hi(1)
                    up_tanh(2)
                    up_hi(2)
                    if not Rfirst:
                        act.wait_ge(S["dma_z"], 16 * b)
                    for c_ in range(2):
                        act.wait_ge(S["pe_down"], 2 * b + c_ + 1)
                        nc.scalar.activation(half(z_sb, c_), bank[4 + c_][:, :], ACT.Copy).then_inc(S["act_z"], 1)

            steps(act, body)

            def xeT_copy(j, k, first):
                e = j * BODY + k
                act.wait_ge(S["pe_xeT"], e + 1)
                if not first:
                    act.wait_ge(S["pe_eup"], e - 1)
                nc.scalar.activation(xeT[:, k % 2].rearrange("p k s -> p (k s)"), bank[k % 2][:, 0:D], ACT.Copy).then_inc(S["act_xeT"], 1)

            def silu(j, k, first):
                e = j * BODY + k
                act.wait_ge(S["pe_eup"], e + 1)
                if not first:
                    act.wait_ge(S["dve_hid"], e - 1)
                nc.scalar.activation(silu_a[:, k % 2], bank[2 + k % 2][:, 0:F], ACT.Silu).then_inc(S["act_silu"], 1)

            def hidT_copy(j, k, first):
                e = j * BODY + k
                act.wait_ge(S["pe_hidT"], e + 1)
                if not first:
                    act.wait_ge(S["pe_edown"], e - 1)
                nc.scalar.activation(hidT[0:FH, k % 2].rearrange("p c s -> p (c s)"), bank[4 + k % 2][0:FH, 0:2 * P], ACT.Copy).then_inc(S["act_hidT"], 1)

            def weigh(j, k, first):
                e = j * BODY + k
                act.wait_ge(S["pe_edown"], e + 1)
                if not first:
                    act.wait_ge(S[f"dma_scatter{k % 2}"], 16 * (share(j, k, 2) - 1))
                nc.scalar.activation(ye[:, k % 4], bank[6 + k % 2][:, 0:D], ACT.Copy, scale=xe[:, k % XS, bass.ds(D + e, 1)]).then_inc(S["act_ye"], 1)

            act.wait_ge(S["dve_index"], 2)
            xeT_copy(0, 0, True)

            def experts(j, k):
                known = isinstance(j, int)
                if not known or k + 1 < E:
                    xeT_copy(j, k + 1, known and k < 1)
                if not known or k < E:
                    silu(j, k, known and k < 2)
                if not known or 1 <= k <= E:
                    hidT_copy(j, k - 1, known and k < 3)
                if not known or k >= 2:
                    weigh(j, k - 2, known and k < 6)

            expert_steps(act, experts)

        @block.vector
        def _(dve):
            done = {"n": 0}

            def tiles(ap, c_):
                return ap[:, 2 * c_:2 * c_ + 2, :].rearrange("p t d -> p (t d)")

            def lo_part(out_, in_, hi, sem_name):
                nc.vector.tensor_tensor(out_, in_, hi.bitcast(F32), ALU.subtract).then_inc(S[sem_name], 1)

            dve.wait_ge(S["pool_const"], 2)
            nc.vector.scalar_tensor_tensor(token_code[:, :, :].rearrange("p b t -> p (b t)"), token_code[:, :, :].rearrange("p b t -> p (b t)"), 0.0,
                                           token_code[:, :, :].rearrange("p b t -> p (b t)"), ALU.is_ge, ALU.add).then_inc(S["dve_const"], 1)
            dve.wait_ge(S["dve_const"], 1)

            LINKS = {"A": 0}

            class Chain:
                per = 0

                def __init__(self, base):
                    self.base, self.n = base, 0

                def link(self, ins):
                    ins.then_inc(S["dve_link"], 1)
                    self.n += 1
                    dve.wait_ge(S["dve_link"], self.base + self.n)

                def link_apart(self, ins):
                    ins.then_inc(S["dve_link"], 1)
                    self.n += 1
                    wait_apart(dve, ("dve_link", self.base + self.n))

            def norm_stats(rows_, stats, mv, ve, chain, mv_done, *ready):
                wait_apart(dve, *ready)
                for t in range(T):
                    last = nc.vector.bn_stats(stats[:, t, :], rows_[t])
                chain.link_apart(last)
                for t in range(T):
                    last = nc.vector.bn_aggr(mv[:, t, :], stats[:, t, :])
                chain.link(last)
                nc.vector.tensor_scalar(ve, mv[:, :, 1], EPS, None, ALU.add).then_inc(S[mv_done], 1)

            c0 = Chain(0)
            dve.wait_ge(S["pool_const"], 3)
            nc.vector.tensor_reduce(own[:, :], ident[:, :].rearrange("p (h e) -> p e h", e=GE), AX.X, ALU.add)
            dve.wait_ge(dma_x[0], 16)
            norm_stats([resid[:, 0, t, :] for t in range(T)], stats1, mv1, ve1, c0, "dve_mv1")
            dve.wait_ge(S["pool_r1"], 1)
            for t in range(T):
                last = nc.vector.tensor_scalar(xn[:, t, :], resid[:, 0, t, :], mv1[:, t, 0:1], r1[:, t:t + 1], ALU.subtract, ALU.mult)
            last.then_inc(S["dve_xn"], 1)

            def weights_lo(n):
                dve.wait_ge(S["act_w"], n + 1)
                lo_part(w_lo[:, :, n * D:(n + 1) * D], raw_w[:, :, n * D:(n + 1) * D], w_hi[:, :, n * D:(n + 1) * D], "dve_w")

            base_links = c0.n

            def transposed_lo(out_, hi, banks, ready, value, sem_name):
                for c_ in range(K):
                    dve.wait_ge(S[ready], value + c_ + 1)
                    lo_part(out_[:, c_, :], bank[banks[c_]][:, :], hi[:, c_, :], sem_name)

            for n in range(4):
                weights_lo(n)
            transposed_lo(xT_lo, xT_hi, (2, 3), "act_xT", 0, "dve_xT")
            PER_N, PER_Q, PER_R = 2, 5, 14

            def links_before(i):
                if not isinstance(i, int):
                    return base_links + PER_N * i + PER_Q * (i - 1) + PER_R * (i - 2)
                return base_links + sum(PER_N * live(j, -1)[0] + PER_Q * live(j, 1)[0] + PER_R * live(j, 2)[0] for j in range(i))

            def late_weights():
                weights_lo(4)
                dve.wait_ge(S["act_w"], 9)
                lo_part(g_lo[:, :, :], raw_g, g_hi[:, :, :], "dve_w")
                lo_part(s13_lo[:, :, :], raw_13, s13_hi[:, :, :], "dve_w")
                lo_part(s2_lo[:, 0:2, :], raw_2[:, 0:2, :], s2_hi[:, 0:2, :], "dve_w")
                lo_part(s2_lo[0:FS - 2 * P, 2, :], raw_2[0:FS - 2 * P, 2, :], s2_hi[0:FS - 2 * P, 2, :], "dve_w")

            def body(i):
                Nx, _ = live(i, -1)
                Pr, Pfirst = live(i, 0)
                Q, Qfirst = live(i, 1)
                R, Rfirst = live(i, 2)
                ch = Chain(links_before(i))
                b = i - 2
                if Q:
                    dve.wait_ge(S["act_sq"], 2 * i)
                    if not Qfirst:
                        dve.wait_ge(S["pool_norm"], i - 1)
                    ch.link(nc.vector.tensor_reduce(power, sq.rearrange("p t (h d) -> p (t h) d", d=DH), AX.X, ALU.add))
                    nc.vector.tensor_scalar(power, power, 4.0 / DH, 4.0 * EPS_NORM ** 2, ALU.mult, ALU.max).then_inc(S["dve_power"], 1)
                if R:
                    x1 = at(resid, b)
                    dve.wait_ge(S["pool_r3"], b + 1)
                    if not Rfirst:
                        dve.wait_ge(S["dma_rows"], 16 * b)
                    for t in range(T):
                        last = nc.vector.tensor_scalar(xg[:, t, 0:D], x1[:, t, :], mv3[:, t, 0:1], r3[:, t:t + 1], ALU.subtract, ALU.mult)
                    last.then_inc(S["dve_xn2"], 1)
                if Nx:
                    if isinstance(i, int):
                        dve.wait_ge(dma_x[i + 1], 16)
                    xb = at(resid, i + 1)
                    norm_stats([xb[:, t, :] for t in range(T)], stats1, mv1, ve1, ch, "dve_mv1")
                if R:
                    if not Rfirst:
                        dve.wait_ge(S["pe_up"], 3 * b)
                        dve.wait_ge(S["pe_gate"], b)
                    transposed_lo(x2T_lo, x2T_hi, (2, 3), "act_x2T", 2 * b, "dve_x2T")
                    dve.wait_ge(S["pe_gate"], b + 1)
                    lg = bank[2][:, 0:T * E].rearrange("p (t e) -> p t e", t=T)
                    ch.link(nc.vector.tensor_reduce(top, lg, AX.X, ALU.max))
                    nc.vector.tensor_tensor(logit, lg, top.rearrange("p (t o) -> p t o", o=1).to_broadcast([P, T, E]), ALU.subtract).then_inc(S["dve_logit"], 1)
                if R:
                    dve.wait_ge(S["act_exp"], b + 1)
                    ch.link(nc.vector.tensor_reduce(expsum, logit, AX.X, ALU.add))
                    ch.link(nc.vector.reciprocal(expinv, expsum))
                    ch.link(nc.vector.tensor_tensor(padded[:, :, 0:E], logit, expinv.rearrange("p (t o) -> p t o", o=1).to_broadcast([P, T, E]), ALU.mult))
                    nc.vector.tensor_copy(xg[:, :, D:ROW], padded[:, :, 0:E]).then_inc(S["dve_scores"], 1)
                    for t in range(T):
                        last = nc.vector.max(top8[:, t, :], padded[:, t, :])
                    ch.link_apart(last)
                    for t in range(T):
                        last = nc.vector.match_replace(replaced[:, t, :], top8[:, t, :], padded[:, t, :], -1.0)
                    ch.link(last)
                    if not Rfirst:
                        dve.wait_ge(S["pe_pos"], b)
                    nc.vector.tensor_scalar(sel[:, :, :], replaced[:, :, 0:E], 0.0, None, ALU.is_lt).then_inc(S["dve_sel"], 1)
                    ch.link(nc.vector.tensor_scalar(penalty, replaced[:, :, 0:E], 0.0, float(N), ALU.is_ge, ALU.mult))
                if Nx:
                    dve.wait_ge(S["pool_r1"], i + 2)
                    dve.wait_ge(S["pe_trx"], 2 * (i + 1))
                    for t in range(T):
                        last = nc.vector.tensor_scalar(xn[:, t, :], xb[:, t, :], mv1[:, t, 0:1], r1[:, t:t + 1], ALU.subtract, ALU.mult)
                    last.then_inc(S["dve_xn"], 1)
                if Pfirst:
                    late_weights()
                if Pr:
                    for c_ in range(2):
                        dve.wait_ge(S["act_th"], 2 * i + c_ + 1)
                        if not Pfirst:
                            dve.wait_ge(S["pool_un"], i)
                        nc.vector.scalar_tensor_tensor(tiles(u_sb, c_), tiles(th, c_), 1.0, bank[c_][:, :], ALU.add, ALU.mult).then_inc(S["dve_u"], 1)
                if Q:
                    dve.wait_ge(S["pool_un"], i)
                    dve.wait_ge(S["act_o"], 2 * i)
                    if not Qfirst:
                        dve.wait_ge(S["pe_tro"], 2 * (i - 1))
                    nc.vector.tensor_tensor(on, o_sb, un, ALU.mult).then_inc(S["dve_on"], 1)

                def hidden(j):
                    w = CHUNKS[j][1]
                    ba, bb = ((4, 5), (6, 7), (4, 5))[j]
                    dve.wait_ge(S["act_tu"], 3 * b + j + 1)
                    if not Rfirst:
                        dve.wait_ge(S["pool_hT"], 3 * b)
                        dve.wait_ge(S["act_hT"], 3 * b)
                    ch.link(nc.vector.scalar_tensor_tensor(tu[0:w, j, :], tu[0:w, j, :], 1.0, bank[ba][0:w, :], ALU.add, ALU.mult))
                    nc.vector.scalar_tensor_tensor(hT[0:w, j, :], tu[0:w, j, :], 0.5, bank[bb][0:w, :], ALU.mult, ALU.mult).then_inc(S["dve_h"], 1)

                if R:
                    hidden(0)
                if Pr:
                    dve.wait_ge(S["pe_kv"], i + 1)
                    if not Pfirst:
                        dve.wait_ge(S["pe_out"], 2 * i)
                    else:
                        dve.wait_ge(S["pool_const2"], 1)
                    nc.vector.tensor_tensor(kv_sb, bank[3][:, 0:K * P].rearrange("p (k n) -> p k n", k=K),
                                            block_mask[:, :].rearrange("p (o n) -> p o n", o=1).to_broadcast([P, K, P]), ALU.mult).then_inc(S["dve_kv"], 1)
                if R:
                    dve.wait_ge(S["pe_pos"], b + 1)
                    nc.vector.tensor_tensor(posi[:, :, :], bank[2][:, 0:T * E].rearrange("p (t e) -> p t e", t=T), penalty, ALU.add).then_inc(S["dve_pos"], 1)
                    ch.link(nc.vector.tensor_reduce(taken_now, sel[:, :, :].rearrange("p t e -> p e t"), AX.X, ALU.add))
                    dve.wait_ge(S["dve_pos"], 2 * b + 1)
                    nc.vector.tensor_tensor(taken[:, :], taken[:, :], taken_now, ALU.add).then_inc(S["dve_pos"], 1)
                    nc.vector.tensor_scalar(lo_i[:, :, :], posi[:, :, :], LO - 1, None, ALU.bitwise_and)
                    ch.link(nc.vector.tensor_scalar(hi_i[:, :, :], posi[:, :, :], 4, None, ALU.logical_shift_right))
                    nc.vector.tensor_copy(lo_h[:, :, :], lo_i[:, :, :])
                    ch.link(nc.vector.tensor_copy(hi_h[:, :, :], hi_i[:, :, :]))
                    hidden(1)
                if Q:
                    if not Qfirst:
                        dve.wait_ge(S["pe_wo"], 2 * (i - 1))
                    transposed_lo(oT_lo, oT_hi, (0, 1), "act_oT", 2 * (i - 1), "dve_oT")
                if Nx:
                    dve.wait_ge(S["pe_u"], 2 * i + 2)
                    transposed_lo(xT_lo, xT_hi, (2, 3), "act_xT", 2 * (i + 1), "dve_xT")
                if R:
                    if not Rfirst:
                        dve.wait_ge(S["pe_table"], 2 * b)
                    for t in range(T):
                        nc.vector.tensor_tensor(onehot_lo[:, t], lo_h[:, t:t + 1, :].to_broadcast([P, LO, E]), iota_lo[:, :, :], ALU.is_equal)
                        last = nc.vector.tensor_tensor(onehot_hi[:, t], hi_h[:, t].rearrange("p (g o e) -> p g o e", g=G, o=1).to_broadcast([P, G, HI, GE]), iota_hi[:, :, :, :], ALU.is_equal)
                    ch.link(last)
                    code_b = at(token_code, b)
                    for t in range(T):
                        last = nc.vector.tensor_scalar(onehot_hi[:, t], onehot_hi[:, t], code_b[:, t:t + 1], None, ALU.mult)
                    last.then_inc(S["dve_onehot"], 1)
                    hidden(2)
                if Q:
                    x1 = at(resid, i - 1)
                    y = [bank[6 + t // 2][:, (t % 2) * D:(t % 2 + 1) * D] for t in range(T)]
                    norm_stats(y, stats2, mv2, ve2, ch, "dve_mv2", ("pe_wo", 2 * i))
                if R:
                    for c_ in range(2):
                        dve.wait_ge(S["pe_table"], 2 * b + c_ + 1)
                        tb = table[:, 2 * c_:2 * c_ + 2].rearrange("p g l e -> p (g l e)")
                        nc.vector.tensor_tensor(tb, tb, bank[c_][:, :], ALU.add).then_inc(S["dve_table"], 1)
                if Q:
                    dve.wait_ge(S["pool_r2"], i)
                    for t in range(T):
                        last = nc.vector.tensor_scalar(y_sb[:, t, :], y[t], mv2[:, t, 0:1], r2[:, t:t + 1], ALU.subtract, ALU.mult)
                    last.then_inc(S["dve_yn"], 1)
                    dve.wait_ge(S["dve_yn"], i)
                    nc.vector.tensor_tensor(x1, x1, y_sb, ALU.add).then_inc(S["dve_x1"], 1)
                    norm_stats([x1[:, t, :] for t in range(T)], stats3, mv3, ve3, ch, "dve_mv3", ("dve_x1", i))
                assert ch.n == PER_N * Nx + PER_Q * Q + PER_R * R

            steps(dve, body)
            tail = Chain(links_before(B + 2))

            dve.wait_ge(S["dve_table"], 2 * B)
            masked = o_sb.rearrange("p t d -> p (t d)").rearrange("p (n e) -> p n e", e=GE)
            tail.link(nc.vector.tensor_tensor(masked, table[:, :, :, :].rearrange("p g l e -> p (g l) e"),
                                              own[:, :].rearrange("p (o e) -> p o e", o=1).to_broadcast([P, G * LO, GE]), ALU.mult))
            nc.vector.tensor_reduce(sq[:, 0, 0:G * LO], masked, AX.X, ALU.add).then_inc(S["dve_index"], 1)

            dve.wait_ge(S["pe_code"], 1)
            cd = bank[0][:, 0:E]
            neg, used = logit[:, 0, :], logit[:, 1, :]
            nc.vector.tensor_scalar(neg, cd, 0.0, float(N // 2), ALU.is_lt, ALU.add)
            tail.link(nc.vector.tensor_scalar(used, cd, 0.0, None, ALU.not_equal))
            tail.link(nc.vector.tensor_tensor(code, cd, neg, ALU.add))
            tail.link(nc.vector.tensor_tensor(code, code, used, ALU.mult))
            tail.link(nc.vector.tensor_scalar(used, used, -1.0, 1.0, ALU.mult, ALU.add))
            nc.vector.tensor_copy(gather_rows[:, :], code)
            nc.vector.scalar_tensor_tensor(scatter_rows[:, :], used, slot_dump[:, 0:1], code, ALU.mult, ALU.add).then_inc(S["dve_index"], 1)

            def rows_list(j, k, first):
                e = j * BODY + k
                if not first:
                    dve.wait_ge(dma_xe[k % XS], 16 * share(j, k, XS))
                    dve.wait_ge(S["act_ye"], e - XS + 1)
                nc.vector.tensor_copy(rows_now[:, k % XS:k % XS + 1], gather_rows[:, bass.ds(e, 1)]).then_inc(S["dve_rows_now"], 1)

            def dest_list(j, k, first):
                e = j * BODY + k
                if not first:
                    dve.wait_ge(S[f"dma_scatter{k % 2}"], 16 * (share(j, k, 2) - 1))
                nc.vector.tensor_copy(dest_now[:, k % 4:k % 4 + 1], scatter_rows[:, bass.ds(e, 1)]).then_inc(S["dve_dest_now"], 1)

            def hidden_rows(j, k, first):
                e = j * BODY + k
                dve.wait_ge(S["act_silu"], e + 1)
                if not first:
                    dve.wait_ge(S["pe_hidT"], e - 1)
                nc.vector.tensor_tensor(hid[:, k % 2], silu_a[:, k % 2], bank[2 + k % 2][:, F:2 * F], ALU.mult).then_inc(S["dve_hid"], 1)

            for n in ("dma_z", "dma_rows"):
                dve.wait_ge(S[n], 16 * B)
            dve.wait_ge(S["dve_index"], 2)
            for e in range(AHEAD):
                rows_list(0, e, True)

            def experts(j, k):
                known = isinstance(j, int)
                if not known or k + AHEAD < E:
                    rows_list(j, k + AHEAD, known and k + AHEAD < XS)
                if not known or k < E:
                    dest_list(j, k, known and k < 4)
                hidden_rows(j, k, known and k < 2)

            expert_steps(dve, experts, after=0)

            def sum_and_stats(b):
                room = b % CS
                dve.wait_ge(dma_s[room], 32 * (b // CS + 1))
                if b >= CS:
                    dve.wait_ge(S["pool_fin"], b - CS + 1)
                nc.vector.tensor_tensor(total[:, room], s0[:, room], s1[:, room], ALU.add).then_inc(S["dve_total"], 1)
                norm_stats([total[:, room, t, :] for t in range(T)], statsc, mvc[:, b % 2], vec[:, b % 2], tail, "dve_mvc", ("dve_total", b + 1))

            sum_and_stats(0)
            for b in range(B):
                if b + 1 < B:
                    sum_and_stats(b + 1)
                dve.wait_ge(S["pool_rc"], b + 1)
                room = b % CS
                for t in range(T):
                    last = nc.vector.tensor_scalar(total[:, room, t, :], total[:, room, t, :], mvc[:, b % 2, t, 0:1], rc[:, b % 2, t:t + 1], ALU.subtract, ALU.mult)
                last.then_inc(S["dve_cn"], 1)

        @block.tensor
        def _(pe):
            def product(out_, pairs, start=True, stop=True):
                for n, ((ah, al), (bh, bl)) in enumerate(pairs):
                    first, last_ = start and n == 0, stop and n == len(pairs) - 1
                    nc.tensor.matmul(out_, ah, bh, start=first, stop=False)
                    nc.tensor.matmul(out_, ah, bl, start=False, stop=False)
                    last = nc.tensor.matmul(out_, al, bh, start=False, stop=last_)
                return last

            def transposes(src, banks, done):
                for c_ in range(K):
                    for t in range(T):
                        last = nc.tensor.transpose(bank[banks[c_]][:, tile_of(t)], src[:, t, c_ * P:(c_ + 1) * P], ident[:, :])
                    last.then_inc(S[done], 1)

            def parts(hi, lo, *index):
                return hi[index], lo[index]

            pe.wait_ge(S["pool_const"], 3)
            pe.wait_ge(S["pool_const2"], 1)
            pe.wait_ge(S["dve_xn"], 1)
            transposes(xn, (2, 3), "pe_trx")
            ALL = slice(None)

            def body(i):
                Nx, _ = live(i, -1)
                Pr, Pfirst = live(i, 0)
                Q, Qfirst = live(i, 1)
                R, Rfirst = live(i, 2)
                b = i - 2
                if Q:
                    pe.wait_ge(S["act_q"], 2 * i)
                    pe.wait_ge(S["dve_kv"], i)
                    pe.wait_ge(S["dve_u"], 2 * i)
                    if not Qfirst:
                        pe.wait_ge(S["act_oT"], 2 * (i - 1))
                        pe.wait_ge(S["dve_oT"], 2 * (i - 1))
                    if R and not Rfirst:
                        pe.wait_ge(S["dve_table"], 2 * b)
                    for t in range(T):
                        for c_ in range(K):
                            at_ = (t % 2) * D + c_ * P
                            last = nc.tensor.matmul(bank[t // 2][:, at_:at_ + P], q_sb[:, c_, tile_of(t)], kv_sb[:, c_, :], start=True, stop=True)
                        if t % 2:
                            last.then_inc(S["pe_out"], 1)
                if Pr:
                    pe.wait_ge(S["act_xT"], 2 * i + 2)
                    pe.wait_ge(S["dve_xT"], 2 * i + 2)
                    for c_ in range(K):
                        if Q:
                            pe.wait_ge(S["act_o"], 2 * (i - 1) + c_ + 1)
                        if Pfirst:
                            pe.wait_ge(S["dve_w"], 1)
                        last = product(bank[c_][:, :], [(parts(w_hi, w_lo, ALL, k, slice(c_ * P, (c_ + 1) * P)), parts(xT_hi, xT_lo, ALL, k, ALL)) for k in range(K)])
                        last.then_inc(S["pe_q"], 1)

                def keys_values(t):
                    if t < 2:
                        pe.wait_ge(S["act_q"], 2 * i + t + 1)
                    else:
                        pe.wait_ge(S["act_kv"], 4 * i + t - 1)
                    if Pfirst:
                        pe.wait_ge(S["dve_w"], 3)
                    last = product(bank[t % 2][:, :], [(parts(xT_hi, xT_lo, ALL, k, tile_of(t)), parts(w_hi, w_lo, ALL, k, slice(D, 3 * D))) for k in range(K)])
                    last.then_inc(S["pe_kvp"], 1)

                if Pr:
                    keys_values(0)
                    keys_values(1)
                if R:
                    pe.wait_ge(S["dve_xn2"], b + 1)
                    if not Pr:
                        pe.wait_ge(S["dve_pos"], 2 * b)
                        pe.wait_ge(S["dve_kv"], B)
                    transposes(xg, (2, 3), "pe_trx2")
                if Pr:
                    keys_values(2)
                    keys_values(3)
                if R:
                    if Rfirst:
                        pe.wait_ge(S["dve_w"], 9)
                    pe.wait_ge(S["act_x2T"], 2 * b + 2)
                    pe.wait_ge(S["dve_x2T"], 2 * b + 2)
                    for t in range(T):
                        last = product(bank[2][:, t * E:(t + 1) * E],
                                       [(parts(x2T_hi, x2T_lo, ALL, k, tile_of(t)), parts(g_hi, g_lo, ALL, k, ALL)) for k in range(K)])
                    last.then_inc(S["pe_gate"], 1)
                if Pr:
                    if Pfirst:
                        pe.wait_ge(S["dve_w"], 4)
                    for t in range(T):
                        if t % 2 == 0:
                            pe.wait_ge(S["act_kv"], 4 * i + 3 + t // 2)
                        last = product(bank[t // 2][:, (t % 2) * D:(t % 2 + 1) * D],
                                       [(parts(xT_hi, xT_lo, ALL, k, tile_of(t)), parts(w_hi, w_lo, ALL, k, slice(3 * D, 4 * D))) for k in range(K)])
                        if t % 2:
                            last.then_inc(S["pe_u"], 1)

                def up(j):
                    o, w = CHUNKS[j]
                    for half, bk in enumerate(((4, 5), (6, 7), (4, 5))[j]):
                        cols = slice(half * FS + o, half * FS + o + w)
                        last = product(bank[bk][0:w, :], [(parts(s13_hi, s13_lo, ALL, k, cols), parts(x2T_hi, x2T_lo, ALL, k, ALL)) for k in range(K)])
                    last.then_inc(S["pe_up"], 1)

                if R:
                    if not Rfirst:
                        pe.wait_ge(S["act_z"], 2 * b)
                    up(0)
                    pe.wait_ge(S["dve_yn"], i - 1)
                    up(1)
                if Pr:
                    pe.wait_ge(S["act_kv"], 4 * i + 4)
                    for c_ in range(K):
                        for t in range(T):
                            last = nc.tensor.matmul(bank[3][:, c_ * P:(c_ + 1) * P], k_sb[:, t, c_ * P:(c_ + 1) * P], v_sb[:, t, c_ * P:(c_ + 1) * P],
                                                    start=(t == 0), stop=(t == T - 1))
                    last.then_inc(S["pe_kv"], 1)
                if R:
                    pe.wait_ge(S["dve_logit"], b + 1)
                    pe.wait_ge(S["dve_sel"], b + 1)
                    if not Rfirst:
                        pe.wait_ge(S["dve_pos"], 2 * b)
                    for t in range(T):
                        at_ = bank[2][:, t * E:(t + 1) * E]
                        nc.tensor.matmul(at_, before[:, :], sel[:, t, :], start=True, stop=False)
                        for t_ in range(t):
                            nc.tensor.matmul(at_, ones[:, :], sel[:, t_, :], start=False, stop=False)
                        last = nc.tensor.matmul(at_, ones[:, :], taken[:, :], start=False, stop=True)
                    last.then_inc(S["pe_pos"], 1)
                if Q:
                    pe.wait_ge(S["dve_on"], i)
                    if Pr:
                        pe.wait_ge(S["dve_u"], 2 * (i + 1))
                    else:
                        pe.wait_ge(S["act_o"], 2 * i)
                    transposes(on, (0, 1), "pe_tro")
                if Nx:
                    pe.wait_ge(S["dve_xn"], i + 2)
                    pe.wait_ge(S["dve_kv"], i + 1)
                    if R:
                        pe.wait_ge(S["dve_pos"], 2 * b + 1)
                    transposes(xn, (2, 3), "pe_trx")
                if R:
                    pe.wait_ge(S["dve_h"], 3 * b + 1)
                    up(2)
                if Q:
                    pe.wait_ge(S["act_oT"], 2 * i)
                    pe.wait_ge(S["dve_oT"], 2 * i)
                    if Qfirst:
                        pe.wait_ge(S["dve_w"], 5)
                    if R:
                        pe.wait_ge(S["dve_h"], 3 * b + 2)
                    for t in range(T):
                        last = product(bank[6 + t // 2][:, (t % 2) * D:(t % 2 + 1) * D],
                                       [(parts(oT_hi, oT_lo, ALL, k, tile_of(t)), parts(w_hi, w_lo, ALL, k, slice(4 * D, 5 * D))) for k in range(K)])
                        if t % 2:
                            last.then_inc(S["pe_wo"], 1)
                if R:
                    pe.wait_ge(S["dve_onehot"], b + 1)
                    if not Q:
                        pe.wait_ge(S["dve_table"], 2 * b)
                    for g in range(G):
                        for t in range(T):
                            last = nc.tensor.matmul(bank[g // 2][:, (g % 2) * D:(g % 2 + 1) * D],
                                                    onehot_hi[:, t, g].rearrange("p h e -> p (h e)"), onehot_lo[:, t, :, g * GE:(g + 1) * GE],
                                                    start=(t == 0), stop=(t == T - 1))
                        if g % 2:
                            last.then_inc(S["pe_table"], 1)
                    pe.wait_ge(S["dve_h"], 3 * b + 3)
                    pe.wait_ge(S["act_hT"], 3 * b + 3)
                    pe.wait_ge(S["pool_hT"], 3 * b + 3)
                    for t in range(T):
                        last = product(bank[4 + t // 2][:, (t % 2) * D:(t % 2 + 1) * D],
                                       [((hT_hi[0:w, j, tile_of(t)], hT_lo[0:w, j, tile_of(t)]), (s2_hi[0:w, j, :], s2_lo[0:w, j, :]))
                                        for j, (_, w) in enumerate(CHUNKS)])
                        if t % 2:
                            last.then_inc(S["pe_down"], 1)

            steps(pe, body)

            pe.wait_ge(S["dma_table_back"], 16)
            nc.tensor.transpose(bank[0][:, 0:E], sq[0:E, 1, 0:CAP], ident[0:E, 0:E]).then_inc(S["pe_code"], 1)

            def tokens_T(j, k, first):
                e = j * BODY + k
                pe.wait_ge(dma_xe[k % XS], 16 * (share(j, k, XS) + 1))
                if not first:
                    pe.wait_ge(S["act_xeT"], e - 1)
                for c_ in range(K):
                    last = nc.tensor.transpose(bank[k % 2][:, c_ * P:(c_ + 1) * P], xe[:, k % XS, c_ * P:(c_ + 1) * P], ident[:, :])
                last.then_inc(S["pe_xeT"], 1)

            def expert_up(j, k, first):
                e = j * BODY + k
                slot = (k // 2) % WB
                pe.wait_ge(dma_w13[slot], 16 * (share(j, k, BODY) + 1))
                pe.wait_ge(S["act_xeT"], e + 1)
                if not first:
                    pe.wait_ge(S["dve_hid"], e - 1)
                for c_ in range(K):
                    last = nc.tensor.matmul(bank[2 + k % 2][:, 0:2 * F], xeT[:, k % 2, c_, :], w13_sb[slot][:, k % 2, c_, :], start=(c_ == 0), stop=(c_ == K - 1))
                last.then_inc(S["pe_eup"], 1)

            def hidden_T(j, k, first):
                e = j * BODY + k
                pe.wait_ge(S["dve_hid"], e + 1)
                if not first:
                    pe.wait_ge(S["act_hidT"], e - 1)
                for c_ in range(2):
                    last = nc.tensor.transpose(bank[4 + k % 2][0:FH, c_ * P:(c_ + 1) * P], hid[:, k % 2, c_ * FH:(c_ + 1) * FH], ident[:, :])
                last.then_inc(S["pe_hidT"], 1)

            def expert_down(j, k, first):
                e = j * BODY + k
                slot = (k // 2) % WB
                pe.wait_ge(dma_w2[slot], 16 * (share(j, k, BODY) + 1))
                pe.wait_ge(S["act_hidT"], e + 1)
                if not first:
                    pe.wait_ge(S["act_ye"], e - 1)
                for c_ in range(2):
                    last = nc.tensor.matmul(bank[6 + k % 2][:, 0:D], hidT[0:FH, k % 2, c_, :], w2_sb[slot][0:FH, k % 2, c_, :], start=(c_ == 0), stop=(c_ == 1))
                last.then_inc(S["pe_edown"], 1)

            pe.wait_ge(S["dve_index"], 2)
            tokens_T(0, 0, True)

            def experts(j, k):
                known = isinstance(j, int)
                if not known or k + 1 < E:
                    tokens_T(j, k + 1, known and k < 1)
                if not known or k < E:
                    expert_up(j, k, known and k < 2)
                if not known or 1 <= k <= E:
                    hidden_T(j, k - 1, known and k < 3)
                if not known or k >= 2:
                    expert_down(j, k - 2, known and k < 4)

            expert_steps(pe, experts)


def kernel(L0_attn_x, L0_attn_Wq, L0_attn_Wk, L0_attn_Wv, L0_attn_Wu, L0_attn_Wo, L0_ffn_gate_w, L0_ffn_w1, L0_ffn_w2,
           L0_ffn_w3, L0_ffn_sw1, L0_ffn_sw2, L0_ffn_sw3):
    import concourse.bacc as bacc
    from concourse.bass_utils import run_bass_kernel_spmd

    def features_first(w):
        return np.asarray(w).T.reshape(K, P, -1).transpose(1, 0, 2)

    w1, w2, w3 = (np.asarray(w) for w in (L0_ffn_w1, L0_ffn_w2, L0_ffn_w3))
    both = np.concatenate([w1, w3], axis=1)
    arrays = {
        "x": L0_attn_x, "wq": L0_attn_Wq, "wk": L0_attn_Wk, "wv": L0_attn_Wv, "wu": L0_attn_Wu, "wo": L0_attn_Wo,
        "gate_w": features_first(L0_ffn_gate_w),
        "w13": both.transpose(2, 0, 1).reshape(K, P, E, 2 * F).transpose(1, 2, 0, 3),
        "w2": w2.transpose(2, 0, 1).reshape(2, FH, E, D).transpose(1, 2, 0, 3),
        "sw13": features_first(np.concatenate([np.asarray(L0_ffn_sw1), np.asarray(L0_ffn_sw3)], axis=0)),
        "sw2": np.asarray(L0_ffn_sw2).T,
    }
    arrays = {n: np.ascontiguousarray(a) for n, a in arrays.items()}
    nc = bacc.Bacc("TRN2", target_bir_lowering=False, num_devices=1)
    aps = [nc.dram_tensor(n, a.shape, mybir.dt.from_np(a.dtype), kind="ExternalInput").ap() for n, a in arrays.items()]
    result = nc.dram_tensor("result", (B, L, D), F32, kind="ExternalOutput").ap()
    build(nc, *aps, result)
    r = run_bass_kernel_spmd(nc, [arrays], core_ids=[0])
    return r.results[0]["result"]
```

```python
from contextlib import ExitStack

import concourse.bass as bass
import numpy as np
from concourse import mybir

F32, F32R, F16, BF16 = mybir.dt.float32, mybir.dt.float32r, mybir.dt.float16, mybir.dt.bfloat16
I32, U32 = mybir.dt.int32, mybir.dt.uint32
ALU, ACT, AX = mybir.AluOpType, mybir.ActivationFunctionType, mybir.AxisListType

P = 128
B, L, D = 8, 512, 256
T = L // P
K = D // P
N = B * L
H, DH = 16, 16
E, F, CAP, TOPK = 64, 176, 128, 6
FS = 2 * F
FH = F // 2
EPS, EPS_NORM = 1e-5, 1e-12
ROW = D + E
CHUNKS = [(0, 128), (128, 128), (256, 96)]
HI, LO = 16, 8
GE = P // HI
G = E // GE
ACC_ROWS = 1 + N + P
PEEL = 3
WB = 4
AHEAD = 4
BODY = 2 * WB
EARLY = 2 * 2 * (K * 2 * F + 2 * D)
WORK = EARLY + 13312


def build(nc, x, wq, wk, wv, wu, wo, gate_w, w13, w2, sw13, sw2, out):
    ctx = ExitStack()
    with ctx:
        def sb(name, shape, dt=F32):
            return ctx.enter_context(nc.sbuf_tensor(name, shape, dt))

        def sem(name):
            return ctx.enter_context(nc.semaphore(name))

        rows = nc.dram_tensor("token_rows", (1 + N, ROW), F32, kind="Internal").ap()
        sums = [nc.dram_tensor(f"sums{j}", (ACC_ROWS, D), F32, kind="Internal").ap() for j in range(2)]

        resid = sb("resid", [P, B, T, D])
        WCOLS = 5 * D
        w_hi, w_lo = sb("w_hi", [P, K, WCOLS], F32R), sb("w_lo", [P, K, WCOLS], F32R)
        s13_hi, s13_lo = sb("s13_hi", [P, K, 2 * FS], F32R), sb("s13_lo", [P, K, 2 * FS], F32R)
        s2_hi, s2_lo = sb("s2_hi", [P, 3, D], F32R), sb("s2_lo", [P, 3, D], F32R)
        gate = sb("gate", [P, K, E])
        xT_hi, xT_lo = sb("xT_hi", [P, K, L], F32R), sb("xT_lo", [P, K, L], F32R)
        oT_hi, oT_lo = sb("oT_hi", [P, K, L], F32R), sb("oT_lo", [P, K, L], F32R)
        x2T_hi, x2T_lo = sb("x2T_hi", [P, K, L], F32R), sb("x2T_lo", [P, K, L], F32R)
        hT_hi, hT_lo = sb("hT_hi", [P, 3, L], F32R), sb("hT_lo", [P, 3, L], F32R)
        onehot_hi = sb("onehot_hi", [P, T, G, HI, GE], F16)
        onehot_lo = sb("onehot_lo", [P, T, LO, E], F16)
        ident = sb("ident", [P, P])
        block_mask = sb("block_mask", [P, P])
        before = sb("before", [P, P], BF16)
        ones = sb("ones", [P, P], BF16)
        iota_hi = sb("iota_hi", [P, G, HI, GE], F16)
        iota_lo = sb("iota_lo", [P, LO, E], F16)
        token_code = sb("token_code", [P, B, T])
        slot_dump = sb("slot_dump", [P, 1])
        own_hi = sb("own_hi", [P, HI])
        own = sb("own", [P, GE])
        neg_half = sb("neg_half", [P, T * H])
        table = sb("table", [P, G, LO, GE])
        taken = sb("taken", [P, E], BF16)
        gather_rows, scatter_rows = sb("gather_rows", [P, E], U32), sb("scatter_rows", [P, E], U32)
        small = sb("small", [P, 1100])
        root_bits = sb("root_bits", [P, T * H], I32)
        work = sb("work", [P, WORK])

        class Carve:
            def __init__(self, tensor):
                self.tensor, self.at = tensor, 0

            def take(self, *shape):
                n = int(np.prod(shape))
                view = self.tensor[:, self.at:self.at + n]
                self.at += n
                names = "abcd"[:len(shape)]
                if len(shape) > 1:
                    view = view.rearrange(f"p ({' '.join(names)}) -> p {' '.join(names)}",
                                          **dict(zip(names[1:], shape[1:])))
                return view

        s = Carve(small)
        stats1, mv1, ve1, nm1, r1, shift1 = s.take(T, 6), s.take(T, 2), s.take(T), s.take(T), s.take(T), s.take(T)
        stats2, mv2, ve2, nm2, r2, shift2 = s.take(T, 6), s.take(T, 2), s.take(T), s.take(T), s.take(T), s.take(T)
        stats3, mv3, ve3, nm3, r3, shift3 = s.take(T, 6), s.take(T, 2), s.take(T), s.take(T), s.take(T), s.take(T)
        statsc, mvc, vec, nmc, rc, shiftc = s.take(T, 6), s.take(T, 2), s.take(2, T), s.take(2, T), s.take(2, T), s.take(2, T)
        power, norm = s.take(T * H), s.take(T * H)
        root_work = s.take(T * H)
        top, expsum, expinv, top8 = s.take(T), s.take(T), s.take(T), s.take(T, 8)
        padded = s.take(T, E + 2)
        replaced = s.take(T, E + 2)
        taken_now = s.take(E)
        code = s.take(E)

        a = Carve(work)
        th, k_sb, v_sb, xn = (a.take(T, D) for _ in range(4))
        a.take(EARLY - a.at)
        u_sb, o_sb, sq = (a.take(T, D) for _ in range(3))
        q_sb = a.take(K, L)
        kv_sb = a.take(K, P)
        raw_at = a.at
        on, y_sb, un = (a.take(T, D) for _ in range(3))
        x2T = y_sb.rearrange("p t d -> p (t d)").rearrange("p (k l) -> p k l", k=K)
        slot_codes = un.rearrange("p t d -> p (t d)").rearrange("p (g h l) -> p g h l", g=G, h=HI)
        logit, penalty = (a.take(T, E) for _ in range(2))
        xg = a.take(T, ROW)
        tu, hT = a.take(3, L), a.take(3, L)
        z_sb = a.take(T, D)
        zeros = z_sb[:, 0, :]
        assert a.at <= WORK
        posi, lo_i, hi_i = (sb(n, [P, T, E], I32) for n in ("posi", "lo_i", "hi_i"))
        lo_h, hi_h = sb("lo_h", [P, T, E], F16), sb("hi_h", [P, T, E], F16)
        sel = sb("sel", [P, T, E], BF16)
        r = Carve(work)
        r.at = raw_at
        raw_w = r.take(K, WCOLS)
        raw_13 = r.take(K, 2 * FS)
        raw_2 = r.take(3, D)
        assert r.at <= WORK - T * D

        m = Carve(work)
        w13_sb, w2_sb = [None] * WB, [None] * WB
        for room in range(WB):
            w13_sb[room], w2_sb[room] = m.take(2, K, 2 * F), m.take(2, 2, D)
            assert room != 1 or m.at == EARLY
        XS = 8
        xe = m.take(XS, ROW)
        xeT = m.take(2, K, P)
        silu_a, hid = m.take(2, F), m.take(2, F)
        hidT = m.take(2, 2, P)
        ye = m.take(4, D)
        assert m.at <= WORK
        rows_now = sb("rows_now", [P, XS], U32)
        dest_now = sb("dest_now", [P, 4], U32)

        CT = T // 2
        CN, CS = B * T // CT, 6
        c = Carve(work)
        s0, s1, total, fin = (c.take(CS, CT, D) for _ in range(4))
        assert CS * CT * D <= EARLY and c.at <= WORK

        bank = [ctx.enter_context(nc.psum_tensor(f"bank{j}", [P, 512], F32)) for j in range(8)]

        names = """dma_wg dma_w13 dma_w2 dma_z dma_rows dma_zero_rows dma_zero0 dma_zero1
            pool_const pool_const2 dve_const act_w dve_w
            dve_mv1 pool_r1 act_xn pe_trx act_xT dve_xT
            pe_q pe_kvp pe_u act_q act_kv act_th dve_u pe_kv dve_kv
            pe_out act_o act_sq dve_power dve_norm pool_un dve_on pe_tro act_oT dve_oT pe_wo
            dve_mv2 pool_r2 act_yn pool_x1 pool_root1 pool_root2 pool_root3 pool_rootc dve_mv3 pool_r3 act_xn2 pe_trx2 act_x2 act_x2T dve_x2T pool_x2T
            pe_gate dve_logit act_exp dve_scores dve_sel pe_pos dve_pos dve_onehot pe_table dve_table
            pe_up act_tu dve_h act_hT pool_hT pe_down act_z dve_link
            dve_slots pe_code dve_index
            pe_xeT act_xeT pe_eup act_silu dve_hid pe_hidT act_hidT pe_edown act_ye
            dma_scatter0 dma_scatter1
            dve_total dve_mvc pool_rc act_cn pool_fin dve_fin dve_rows_now dve_dest_now""".split()
        S = {n: sem(n) for n in names}
        dma_x = [sem(f"dma_x{b}") for b in range(B)]
        dma_w = [sem(f"dma_w{n}") for n in ("q", "k", "v", "u", "o")]
        dma_w13 = [sem(f"dma_w13_{j}") for j in range(WB)]
        dma_w2 = [sem(f"dma_w2_{j}") for j in range(WB)]
        dma_s = [sem(f"dma_s{j}") for j in range(CS)]
        dma_out = [sem(f"dma_out{j}") for j in range(CS)]
        dma_xe = [sem(f"dma_xe{j}") for j in range(XS)]

        def wait_apart(engine, *waits):
            waits = [(S[n], v if isinstance(v, int) else engine.compute_val(v)) for n, v in waits]
            engine.wait_ge(S["pool_const"], 1)
            for semaphore, value in waits:
                engine.wait_ge(semaphore, value)

        def share(j, k, d):
            return j * (BODY // d) + k // d

        def tile_of(t):
            return slice(t * P, (t + 1) * P)

        def at(buffer, b):
            return buffer[:, b] if isinstance(b, int) else buffer[:, bass.ds(b, 1)].squeeze(1)

        def token_rows_of(tensor, b, width):
            first = 1 + b * L
            return tensor[bass.ds(first, L), 0:width].rearrange("(t p) d -> p t d", p=P)

        def steps(engine, body):
            for i in range(PEEL):
                body(i)
            with engine.Fori(PEEL, B - 1) as i:
                body(i)
            for i in range(B - 1, B + 2):
                body(i)

        def live(i, lag):
            if isinstance(i, int):
                return 0 <= i - lag < B, i == lag
            return True, False

        def ending(i):
            return isinstance(i, int) and i == B, isinstance(i, int) and i == B + 1

        def deferred(i):
            return isinstance(i, int) and i == B - 1

        def up_banks(j, b):
            last = isinstance(b, int) and b == B - 1
            return (4, 5) if (j % 2 == 0) != last else (6, 7)

        def expert_steps(engine, step, after=2):
            for k in range(BODY):
                step(0, k)
            with engine.Fori(1, E // BODY - 1) as j:
                for k in range(BODY):
                    step(j, k)
            for k in range(E - BODY, E + after):
                step(0, k)

        block = ctx.enter_context(nc.Block())

        @block.sync
        def _(sp):
            sp.dma_start(resid[:, 0], x[0].rearrange("(t p) d -> p t d", p=P)).then_inc(dma_x[0], 16)
            for j, w in enumerate((wq, wk, wv, wu, wo)):
                sp.dma_start(raw_w[:, :, j * D:(j + 1) * D], w.rearrange("(k p) n -> p k n", p=P)).then_inc(dma_w[j], 16)
            sp.dma_start(resid[:, 1], x[1].rearrange("(t p) d -> p t d", p=P)).then_inc(dma_x[1], 16)
            sp.dma_start(gate[:, :, :], gate_w).then_inc(S["dma_wg"], 16)
            sp.dma_start(raw_13, sw13).then_inc(S["dma_w13"], 16)
            sp.dma_start(raw_2[:, 0:2, :], sw2[0:2 * P].rearrange("(c p) n -> p c n", p=P)).then_inc(S["dma_w2"], 16)
            sp.dma_start(raw_2[0:FS - 2 * P, 2, :], sw2[2 * P:FS]).then_inc(S["dma_w2"], 16)
            for b in range(2, B):
                sp.dma_start(resid[:, b], x[b].rearrange("(t p) d -> p t d", p=P)).then_inc(dma_x[b], 16)
            sp.wait_ge(S["pool_const"], 1)
            sp.dma_start(rows[0:1, :].rearrange("o (a b) -> o a b", a=2), zeros[0:1, :].rearrange("p (o d) -> p o d", o=1).to_broadcast([1, 2, D])[:, :, 0:ROW // 2]).then_inc(S["dma_zero_rows"], 16)
            sp.dma_start(sums[0][1 + N:ACC_ROWS, :], zeros).then_inc(S["dma_zero0"], 16)
            sp.dma_start(sums[1][1:ACC_ROWS, :].rearrange("(p r) d -> p r d", p=P),
                         zeros.rearrange("p (o d) -> p o d", o=1).to_broadcast([P, (N + P) // P, D])).then_inc(S["dma_zero1"], 16)

            def load_pair(pair, slot):
                sp.dma_start(w13_sb[slot], w13[:, bass.ds(2 * pair, 2)]).then_inc(dma_w13[slot], 16)
                sp.dma_start(w2_sb[slot][0:FH], w2[:, bass.ds(2 * pair, 2)]).then_inc(dma_w2[slot], 16)

            def shared_rows_out(b):
                sp.wait_ge(S["act_z"], 2 * b + 2)
                sp.dma_start(token_rows_of(sums[0], b, D), z_sb).then_inc(S["dma_z"], 16)

            def body(i):
                R, _ = live(i, 2)
                if isinstance(i, int) and i == B:
                    sp.wait_ge(S["dve_u"], 2 * B)
                    sp.wait_ge(S["pe_kv"], B)
                    sp.wait_ge(S["pe_trx"], 2 * B)
                    load_pair(0, 0)
                    load_pair(1, 1)
                if R:
                    b = i - 2
                    sp.wait_ge(S["act_xn2"], b + 1)
                    sp.wait_ge(S["dve_scores"], b + 1)
                    sp.dma_start(token_rows_of(rows, b, ROW), xg).then_inc(S["dma_rows"], 16)
                    if not ending(i)[1]:
                        shared_rows_out(b)
                if ending(i)[0]:
                    sp.wait_ge(S["pe_tro"], 2 * B)
                    load_pair(2, 2)
                    load_pair(3, 3)

            steps(sp, body)

            shared_rows_out(B - 1)
            with sp.Fori(1, E // BODY) as j:
                for slot in range(WB):
                    sp.wait_ge(S["pe_edown"], (j - 1) * BODY + 2 * slot + 2)
                    load_pair(j * WB + slot, slot)

            def load_sum(j, n):
                sp.dma_start((s0, s1)[j][:, n % CS], sums[j][1 + n * CT * P:1 + (n + 1) * CT * P, :].rearrange("(t p) d -> p t d", p=P)).then_inc(dma_s[n % CS], 16)

            sp.wait_ge(S["dma_scatter0"], 16 * (E // 2))
            sp.wait_ge(S["pe_edown"], E - 2 * WB + 4)
            for n in range(CS):
                load_sum(0, n)
            sp.wait_ge(S["act_ye"], E)
            sp.wait_ge(S["pe_edown"], E)
            sp.wait_ge(S["dma_scatter1"], 16 * (E // 2))
            for n in range(CS):
                load_sum(1, n)
            for n in range(CN):
                if n + CS < CN:
                    sp.wait_ge(S["dve_total"], n + 1)
                    load_sum(0, n + CS)
                    load_sum(1, n + CS)
                sp.wait_ge(S["pool_fin"], n + 1)
                sp.wait_ge(S["dve_fin"], n + 1)
                first = n % (T // CT) * CT * P
                sp.dma_start(out[n * CT // T, first:first + CT * P].rearrange("(t p) d -> p t d", p=P), fin[:, n % CS]).then_inc(dma_out[n % CS], 16)
            for room in range(CS):
                sp.wait_ge(dma_out[room], 16 * len(range(room, CN, CS)))
            sp.wait_ge(S["dma_zero0"], 16)

        @block.gpsimd
        def _(pool):
            pool.memset(neg_half[:, :], -0.5)
            pool.memset(zeros, 0.0).then_inc(S["pool_const"], 1)
            pool.memset(ident[:, :], 0.0)
            pool.memset(block_mask[:, :], 1.0)
            pool.memset(before[:, :], 1.0)
            pool.memset(ones[:, :], 1.0)
            pool.memset(taken[:, :], 0.0)
            pool.memset(table[:, :, :, :], 0.0)
            pool.memset(padded[:, :, E:E + 2], 2.0).then_inc(S["pool_const"], 1)
            pool.wait_ge(S["pool_const"], 2)
            pool.affine_select(out=ident[:, :], in_=ident[:, :], compare_op=ALU.not_equal, fill=1.0, base=0,
                               pattern=[[-1, P]], channel_multiplier=1)
            pool.affine_select(out=before[:, :], in_=before[:, :], compare_op=ALU.is_ge, fill=0.0, base=-1,
                               pattern=[[1, P]], channel_multiplier=-1)
            blocks = block_mask[:, :].rearrange("p (h d) -> p h d", d=DH)
            pool.affine_select(out=blocks, in_=blocks, compare_op=ALU.is_ge, fill=0.0, base=0,
                               pattern=[[-DH, P // DH], [0, DH]], channel_multiplier=1).then_inc(S["pool_const"], 1)
            pool.wait_ge(S["pool_const"], 3)
            pool.affine_select(out=blocks, in_=blocks, compare_op=ALU.is_ge, fill=0.0, base=DH - 1,
                               pattern=[[DH, P // DH], [0, DH]], channel_multiplier=-1).then_inc(S["pool_const2"], 1)

            def inverse_root(out_, in_, ready, value, done):
                pool.wait_ge(S[ready], value)
                pool.tensor_tensor(out_, in_, neg_half[:, 0:in_.shape[1]], ALU.pow).then_inc(S[done], 1)

            def norm_factors(r, shift, ve, nm, ready, root, done, value, used=None, uses=1):
                if used is not None:
                    pool.wait_ge(S[used], uses * (value - 1))
                inverse_root(r, ve, ready, value, root)
                pool.wait_ge(S[root], value)
                pool.tensor_tensor(shift, nm, r, ALU.mult).then_inc(S[done], 1)

            norm_factors(r1, shift1, ve1, nm1, "dve_mv1", "pool_root1", "pool_r1", 1)
            pool.iota(iota_hi[:, :, :, :], pattern=[[0, G], [1, HI], [0, GE]], base=0, channel_multiplier=0, allow_small_or_imprecise_dtypes=True)
            pool.iota(iota_lo[:, :, :], pattern=[[1, LO], [0, E]], base=0, channel_multiplier=0, allow_small_or_imprecise_dtypes=True)
            pool.iota(token_code[:, :, :], pattern=[[L, B], [P, T]], base=-N // 2, channel_multiplier=1, allow_small_or_imprecise_dtypes=True)
            pool.iota(slot_dump[:, :], pattern=[[0, 1]], base=1 + N, channel_multiplier=1, allow_small_or_imprecise_dtypes=True).then_inc(S["pool_const2"], 1)

            def hidden_lo(b, j):
                w = CHUNKS[j][1]
                pool.wait_ge(S["act_hT"], 3 * b + j + 1)
                pool.tensor_tensor(hT_lo[0:w, j, :], hT[0:w, j, :], hT_hi[0:w, j, :].bitcast(F32), ALU.subtract).then_inc(S["pool_hT"], 1)

            def body(i):
                Nx, _ = live(i, -1)
                Q, _ = live(i, 1)
                R, _ = live(i, 2)

                if Q:
                    pool.wait_ge(S["dve_u"], 2 * i)
                    pool.wait_ge(S["dve_norm"], i)
                    if not live(i, 1)[1]:
                        pool.wait_ge(S["dve_on"], i - 1)
                    pool.tensor_tensor(un.rearrange("p t (h d) -> p (t h) d", d=DH), u_sb.rearrange("p t (h d) -> p (t h) d", d=DH),
                                       norm.rearrange("p (n o) -> p n o", o=1).to_broadcast([P, T * H, DH]), ALU.mult).then_inc(S["pool_un"], 1)
                if Nx:
                    norm_factors(r1, shift1, ve1, nm1, "dve_mv1", "pool_root1", "pool_r1", i + 2, "act_xn")

                def residual_factors(i):
                    norm_factors(r3, shift3, ve3, nm3, "dve_mv3", "pool_root3", "pool_r3", i, None if live(i, 1)[1] else "act_xn2")

                if ending(i)[0]:
                    residual_factors(i - 1)

                def hidden_parts():
                    if not live(i, 2)[1]:
                        pool.wait_ge(S["pe_down"], 2 * (i - 2))
                    for j in range(1 if ending(i)[1] else 2 if ending(i)[0] else len(CHUNKS)):
                        hidden_lo(i - 2, j)

                if ending(i)[1]:
                    pool.wait_ge(S["pe_up"], 3 * (i - 2))
                    for c_ in range(K):
                        pool.wait_ge(S["act_x2T"], 2 * (i - 2) + c_ + 1)
                        pool.tensor_tensor(x2T_lo[:, c_, :], x2T[:, c_, :], x2T_hi[:, c_, :].bitcast(F32), ALU.subtract).then_inc(S["pool_x2T"], 1)
                    hidden_lo(i - 3, 2)
                if R and not ending(i)[0]:
                    hidden_parts()
                if Q:
                    first = live(i, 1)[1]
                    norm_factors(r2, shift2, ve2, nm2, "dve_mv2", "pool_root2", "pool_r2", i, None if first else "act_yn", 2)
                    x1 = at(resid, i - 1)
                    for h in range(2):
                        pool.wait_ge(S["act_yn"], 2 * (i - 1) + h + 1)
                        two = slice(2 * h, 2 * h + 2)
                        pool.tensor_tensor(x1[:, two], x1[:, two], y_sb[:, two], ALU.add).then_inc(S["pool_x1"], 1)
                    if not deferred(i):
                        residual_factors(i)
                if ending(i)[0]:
                    hidden_parts()

            steps(pool, body)

            pool.wait_ge(S["dve_index"], 1)
            pool.wait_ge(S["dma_rows"], 16 * B)
            pool.wait_ge(S["dma_zero_rows"], 16)

            def gather(j, k):
                e = j * BODY + k
                wait_apart(pool, ("dve_rows_now", e + 1))
                pool.indirect_dma_start(out=xe[:, k % XS, :], out_offset=None, in_=rows,
                                        in_offset=bass.IndirectOffsetOnAxis(ap=rows_now[:, k % XS:k % XS + 1], axis=0)).then_inc(dma_xe[k % XS], 16)

            def scatter(j, k, first):
                e = j * BODY + k
                landed = [] if first else [(f"dma_scatter{k % 2}", 16 * share(j, k, 2))]
                wait_apart(pool, ("act_ye", e + 1), ("dve_dest_now", e + 1), *landed)
                pool.indirect_dma_start(out=sums[k % 2], out_offset=bass.IndirectOffsetOnAxis(ap=dest_now[:, k % 4:k % 4 + 1], axis=0),
                                        in_=ye[:, k % 4, :], in_offset=None, compute_op=ALU.add).then_inc(S[f"dma_scatter{k % 2}"], 16)

            for e in range(AHEAD):
                gather(0, e)
            for j in range(1, len(CHUNKS)):
                hidden_lo(B - 1, j)

            def experts(j, k):
                known = isinstance(j, int)
                if not known or k + AHEAD < E:
                    gather(j, k + AHEAD)
                if known and k == 2:
                    pool.wait_ge(S["dma_zero0"], 16)
                    pool.wait_ge(S["dma_zero1"], 16)
                    pool.wait_ge(S["dma_z"], 16 * B)
                if not known or k >= 2:
                    scatter(j, k - 2, known and k < 4)

            expert_steps(pool, experts)

            def factors(n):
                r_ = n % 2
                if n >= 2:
                    pool.wait_ge(S["act_cn"], n - 1)
                norm_factors(rc[:, r_, 0:CT], shiftc[:, r_, 0:CT], vec[:, r_, 0:CT], nmc[:, r_, 0:CT], "dve_mvc", "pool_rootc", "pool_rc", n + 1)

            factors(0)
            for n in range(CN):
                if n + 1 < CN:
                    factors(n + 1)
                pool.wait_ge(S["act_cn"], n + 1)
                if n >= CS:
                    pool.wait_ge(dma_out[n % CS], 16 * (n // CS))
                pool.tensor_tensor(fin[:, n % CS, 0], resid[:, n * CT // T, n * CT % T], total[:, n % CS, 0], ALU.add).then_inc(S["pool_fin"], 1)

        @block.scalar
        def _(act):
            def hi_part(out_, in_, done):
                nc.scalar.activation(out_, in_, ACT.Copy).then_inc(S[done], 1)

            def weights_hi(n):
                act.wait_ge(dma_w[n], 16)
                hi_part(w_hi[:, :, n * D:(n + 1) * D], raw_w[:, :, n * D:(n + 1) * D], "act_w")

            def transposed_hi(out_, banks, ready, value, done):
                for c_ in range(K):
                    act.wait_ge(S[ready], value + c_ + 1)
                    hi_part(out_[:, c_, :], bank[banks[c_]][:, :], done)

            def normed(out_, rows_, r, shift, done):
                for t in range(len(rows_)):
                    last = nc.scalar.activation(out_[:, t, 0:D], rows_[t], ACT.Identity, bias=shift[:, t:t + 1], scale=r[:, t:t + 1])
                last.then_inc(S[done], 1)

            def tiles_of(x_):
                return [x_[:, t, :] for t in range(x_.shape[1])]

            for n in range(3):
                weights_hi(n)
            act.wait_ge(S["pool_r1"], 1)
            normed(xn, tiles_of(resid[:, 0]), r1, shift1, "act_xn")
            weights_hi(3)
            transposed_hi(xT_hi, (2, 3), "pe_trx", 0, "act_xT")
            weights_hi(4)
            act.wait_ge(S["dma_w13"], 16)
            hi_part(s13_hi[:, :, :], raw_13, "act_w")
            act.wait_ge(S["dma_w2"], 32)
            hi_part(s2_hi[:, 0:2, :], raw_2[:, 0:2, :], "act_w")
            hi_part(s2_hi[0:FS - 2 * P, 2, :], raw_2[0:FS - 2 * P, 2, :], "act_w")

            def half(ap, c_):
                return ap[:, 2 * c_:2 * c_ + 2, :].rearrange("p t d -> p (t d)")

            def shared_rows(b, first=False):
                if not first:
                    act.wait_ge(S["dma_z"], 16 * b)
                for c_ in range(2):
                    act.wait_ge(S["pe_down"], 2 * b + c_ + 1)
                    nc.scalar.activation(half(z_sb, c_), bank[4 + c_][:, :], ACT.Copy).then_inc(S["act_z"], 1)

            def body(i):
                Nx, _ = live(i, -1)
                Pr, Pfirst = live(i, 0)
                Q, Qfirst = live(i, 1)
                R, Rfirst = live(i, 2)
                flush, final = ending(i)
                b = i - 2
                y_banks = (0, 1) if flush else (6, 7)
                gate_bank = 7 if flush else 0 if final else 2
                def squares(i):
                    if not live(i, 1)[1]:
                        act.wait_ge(S["dve_on"], i - 1)
                        act.wait_ge(S["dve_power"], i - 1)
                    for c_ in range(2):
                        act.wait_ge(S["pe_out"], 2 * (i - 1) + c_ + 1)
                        nc.scalar.activation(half(sq, c_), bank[c_][:, :], ACT.Square).then_inc(S["act_sq"], 1)
                    for c_ in range(2):
                        nc.scalar.activation(half(o_sb, c_), bank[c_][:, :], ACT.Copy).then_inc(S["act_o"], 1)

                if Q and not flush:
                    squares(i)
                if Pr:
                    for c_ in range(K):
                        act.wait_ge(S["pe_q"], 2 * i + c_ + 1)
                        if not Pfirst:
                            act.wait_ge(S["pe_out"], 2 * i)
                        nc.scalar.activation(q_sb[:, c_, :], bank[2 + c_][:, :], ACT.Relu, scale=0.25).then_inc(S["act_q"], 1)
                def rows_for_experts(b_):
                    act.wait_ge(S["pool_r3"], b_ + 1)
                    if not Rfirst:
                        act.wait_ge(S["dma_rows"], 16 * b_)
                    normed(xg, tiles_of(at(resid, b_)), r3, shift3, "act_xn2")


                def keys_values(t):
                    act.wait_ge(S["pe_kvp"], 4 * i + t + 1)
                    if not Pfirst:
                        act.wait_ge(S["pe_kv"], i)
                    nc.scalar.activation(k_sb[:, t, :], bank[t % 2][:, 0:D], ACT.Relu, scale=0.25)
                    nc.scalar.activation(v_sb[:, t, :], bank[t % 2][:, D:2 * D], ACT.Copy).then_inc(S["act_kv"], 1)

                def next_rows():
                    act.wait_ge(S["pool_r1"], i + 2)
                    act.wait_ge(S["pe_trx"], 2 * (i + 1))
                    normed(xn, tiles_of(at(resid, i + 1)), r1, shift1, "act_xn")

                if Pr:
                    keys_values(0)
                    keys_values(1)
                if Nx and Pfirst:
                    next_rows()
                if R and not final and not flush:
                    rows_for_experts(b)
                if Pr:
                    keys_values(2)
                    keys_values(3)
                def output_hi():
                    if not Qfirst:
                        act.wait_ge(S["pe_wo"], 2 * (i - 1))
                        act.wait_ge(S["dve_oT"], 2 * (i - 1))
                    transposed_hi(oT_hi, (0, 1), "pe_tro", 2 * (i - 1), "act_oT")

                if flush:
                    output_hi()
                    rows_for_experts(b)
                if R:
                    if not Rfirst:
                        act.wait_ge(S["pe_gate"], b)
                        if not final:
                            act.wait_ge(S["pe_up"], 3 * b)
                    for c_ in range(K):
                        act.wait_ge(S["pe_trx2"], 2 * b + c_ + 1)
                        nc.scalar.activation(x2T[:, c_, :], bank[2 + c_][:, :], ACT.Copy).then_inc(S["act_x2"], 1)
                        if not (flush or final):
                            hi_part(x2T_hi[:, c_, :], bank[2 + c_][:, :], "act_x2T")
                    if final:
                        act.wait_ge(S["pe_up"], 3 * b)
                    if flush or final:
                        transposed_hi(x2T_hi, (2, 3), "pe_trx2", 2 * b, "act_x2T")
                def output_rows():
                    act.wait_ge(S["pool_r2"], i)
                    if not Qfirst:
                        act.wait_ge(S["pool_x1"], 2 * (i - 1))
                    if R:
                        act.wait_ge(S["pe_gate"], b + 1)
                    for h in range(2):
                        two = slice(2 * h, 2 * h + 2)
                        normed(y_sb[:, two], [bank[y_banks[h]][:, t * D:(t + 1) * D] for t in range(2)], r2[:, two], shift2[:, two], "act_yn")

                def up_tanh(j, b=b):
                    w = CHUNKS[j][1]
                    act.wait_ge(S["pe_up"], 3 * b + j + 1)
                    if not Rfirst:
                        act.wait_ge(S["dve_h"], 3 * b)
                    nc.scalar.activation(tu[0:w, j, :], bank[up_banks(j, b)[0]][0:w, :], ACT.Tanh, scale=0.5).then_inc(S["act_tu"], 1)

                def up_hi(j, b=b):
                    w = CHUNKS[j][1]
                    act.wait_ge(S["dve_h"], 3 * b + j + 1)
                    if not Rfirst:
                        act.wait_ge(S["pe_down"], 2 * b)
                        act.wait_ge(S["pool_hT"], 3 * b)
                    hi_part(hT_hi[0:w, j, :], hT[0:w, j, :], "act_hT")

                if flush:
                    output_rows()
                if final:
                    up_tanh(2, b - 1)
                if R:
                    if Rfirst:
                        for n in ("dma_zero_rows", "dma_zero0", "dma_zero1"):
                            act.wait_ge(S[n], 16)
                    act.wait_ge(S["dve_logit"], i - 1)
                    nc.scalar.activation(logit, logit, ACT.Exp).then_inc(S["act_exp"], 1)
                if Pr:
                    for c_ in range(2):
                        act.wait_ge(S["pe_u"], 2 * i + c_ + 1)
                        if not Pfirst:
                            act.wait_ge(S["dve_u"], 2 * i)
                        nc.scalar.activation(half(th, c_), bank[c_][:, :], ACT.Tanh, scale=0.5).then_inc(S["act_th"], 1)

                if final:
                    up_hi(2, b - 1)
                    shared_rows(b - 1)
                if R:
                    up_tanh(0)
                if Nx and not Pfirst:
                    next_rows()
                if R:
                    up_tanh(1)
                if Q and not flush:
                    output_hi()
                if flush:
                    rows_for_experts(b + 1)
                if R:
                    up_hi(0)
                if Nx:
                    act.wait_ge(S["pe_u"], 2 * i + 2)
                    transposed_hi(xT_hi, (2, 3), "pe_trx", 2 * (i + 1), "act_xT")
                if R:
                    up_hi(1)
                    if not flush:
                        up_tanh(2)
                        up_hi(2)
                if deferred(i):
                    squares(i + 1)
                if Q and not flush:
                    output_rows()
                if R and not flush and not final:
                    shared_rows(b, Rfirst)
            steps(act, body)

            def xeT_copy(j, k, first):
                e = j * BODY + k
                act.wait_ge(S["pe_xeT"], e + 1)
                if not first:
                    act.wait_ge(S["pe_eup"], e - 1)
                nc.scalar.activation(xeT[:, k % 2].rearrange("p k s -> p (k s)"), bank[k % 2][:, 0:D], ACT.Copy).then_inc(S["act_xeT"], 1)

            def silu(j, k, first):
                e = j * BODY + k
                act.wait_ge(S["pe_eup"], e + 1)
                if not first:
                    act.wait_ge(S["dve_hid"], e - 1)
                nc.scalar.activation(silu_a[:, k % 2], bank[2 + k % 2][:, 0:F], ACT.Silu).then_inc(S["act_silu"], 1)

            def hidT_copy(j, k, first):
                e = j * BODY + k
                act.wait_ge(S["pe_hidT"], e + 1)
                if not first:
                    act.wait_ge(S["pe_edown"], e - 1)
                nc.scalar.activation(hidT[0:FH, k % 2].rearrange("p c s -> p (c s)"), bank[4 + k % 2][0:FH, 0:2 * P], ACT.Copy).then_inc(S["act_hidT"], 1)

            def weigh(j, k, first):
                e = j * BODY + k
                act.wait_ge(S["pe_edown"], e + 1)
                if not first:
                    act.wait_ge(S[f"dma_scatter{k % 2}"], 16 * (share(j, k, 2) - 1))
                nc.scalar.activation(ye[:, k % 4], bank[6 + k % 2][:, 0:D], ACT.Copy, scale=xe[:, k % XS, bass.ds(D + e, 1)]).then_inc(S["act_ye"], 1)

            act.wait_ge(S["dve_index"], 1)
            xeT_copy(0, 0, True)

            def experts(j, k):
                known = isinstance(j, int)
                if not known or k + 1 < E:
                    xeT_copy(j, k + 1, known and k < 1)
                if not known or k < E:
                    silu(j, k, known and k < 2)
                if known and k == 0:
                    shared_rows(B - 1)
                if not known or 1 <= k <= E:
                    hidT_copy(j, k - 1, known and k < 3)
                if not known or k >= 2:
                    weigh(j, k - 2, known and k < 6)

            expert_steps(act, experts)

            for n in range(CN):
                act.wait_ge(S["pool_rc"], n + 1)
                normed(total[:, n % CS], tiles_of(total[:, n % CS]), rc[:, n % 2], shiftc[:, n % 2], "act_cn")

        @block.vector
        def _(dve):
            done = {"n": 0}

            def tiles(ap, c_):
                return ap[:, 2 * c_:2 * c_ + 2, :].rearrange("p t d -> p (t d)")

            def lo_part(out_, in_, hi, sem_name):
                nc.vector.tensor_tensor(out_, in_, hi.bitcast(F32), ALU.subtract).then_inc(S[sem_name], 1)

            class Chain:
                per = 0

                def __init__(self, base):
                    self.base, self.n = base, 0

                def link(self, ins):
                    ins.then_inc(S["dve_link"], 1)
                    self.n += 1
                    dve.wait_ge(S["dve_link"], self.base + self.n)

                def link_apart(self, ins):
                    ins.then_inc(S["dve_link"], 1)
                    self.n += 1
                    wait_apart(dve, ("dve_link", self.base + self.n))

            def norm_stats(rows_, stats, mv, ve, nm, chain, mv_done, *ready):
                wait_apart(dve, *ready)
                for t in range(len(rows_)):
                    last = nc.vector.bn_stats(stats[:, t, :], rows_[t])
                chain.link_apart(last)
                for t in range(len(rows_)):
                    last = nc.vector.bn_aggr(mv[:, t, :], stats[:, t, :])
                chain.link(last)
                nc.vector.tensor_scalar(ve, mv[:, :, 1], EPS, None, ALU.add)
                nc.vector.tensor_scalar(nm, mv[:, :, 0], -1.0, None, ALU.mult).then_inc(S[mv_done], 1)

            c0 = Chain(0)
            dve.wait_ge(dma_x[0], 16)
            norm_stats([resid[:, 0, t, :] for t in range(T)], stats1, mv1, ve1, nm1, c0, "dve_mv1")
            dve.wait_ge(S["pool_const"], 3)
            nc.vector.tensor_reduce(own[:, :], ident[:, :].rearrange("p (h e) -> p e h", e=GE), AX.X, ALU.add)
            nc.vector.tensor_reduce(own_hi[:, :], ident[:, :].rearrange("p (h e) -> p h e", e=GE), AX.X, ALU.add)

            def weights_lo(n):
                dve.wait_ge(S["act_w"], n + 1)
                lo_part(w_lo[:, :, n * D:(n + 1) * D], raw_w[:, :, n * D:(n + 1) * D], w_hi[:, :, n * D:(n + 1) * D], "dve_w")

            base_links = c0.n

            def transposed_lo(out_, hi, banks, ready, value, sem_name):
                for c_ in range(K):
                    dve.wait_ge(S[ready], value + c_ + 1)
                    lo_part(out_[:, c_, :], bank[banks[c_]][:, :], hi[:, c_, :], sem_name)

            for n in range(4):
                weights_lo(n)
            transposed_lo(xT_lo, xT_hi, (2, 3), "act_xT", 0, "dve_xT")
            PER_N, PER_Q, PER_R = 2, 5 + 10, 14
            MOVED = {B - 1: 11 - 2 - 1, B: 2 + 2 - 11 - 1, B + 1: 1}
            SLOTS = 2 + 4

            def links_before(i):
                if not isinstance(i, int):
                    return base_links + PER_N * i + PER_Q * (i - 1) + PER_R * (i - 2)
                return base_links + sum(PER_N * live(j, -1)[0] + PER_Q * live(j, 1)[0] + PER_R * live(j, 2)[0] + MOVED.get(j, 0) for j in range(i))

            def inverse_root(out_, in_, chain, done):
                y, w = out_, root_work
                chain.link(nc.vector.tensor_scalar(root_bits[:, :], in_.bitcast(I32), 1, None, ALU.logical_shift_right))
                chain.link(nc.vector.tensor_scalar(y.bitcast(I32), root_bits[:, :], -1.0, float(0x5F375A00), ALU.mult, ALU.add))
                for round_ in range(3):
                    chain.link(nc.vector.scalar_tensor_tensor(w, in_, -0.5, y, ALU.mult, ALU.mult))
                    chain.link(nc.vector.tensor_tensor(w, w, y, ALU.mult))
                    last = nc.vector.scalar_tensor_tensor(y, w, 1.5, y, ALU.add, ALU.mult)
                    if round_ < 2:
                        chain.link(last)
                last.then_inc(S[done], 1)

            def late_weights():
                weights_lo(4)
                dve.wait_ge(S["act_w"], 8)
                lo_part(s13_lo[:, :, :], raw_13, s13_hi[:, :, :], "dve_w")
                lo_part(s2_lo[:, 0:2, :], raw_2[:, 0:2, :], s2_hi[:, 0:2, :], "dve_w")
                lo_part(s2_lo[0:FS - 2 * P, 2, :], raw_2[0:FS - 2 * P, 2, :], s2_hi[0:FS - 2 * P, 2, :], "dve_w")

            def token_codes():
                dve.wait_ge(S["pool_const2"], 2)
                nc.vector.scalar_tensor_tensor(token_code[:, :, :].rearrange("p b t -> p (b t)"), token_code[:, :, :].rearrange("p b t -> p (b t)"), 0.0,
                                               token_code[:, :, :].rearrange("p b t -> p (b t)"), ALU.is_ge, ALU.add).then_inc(S["dve_const"], 1)
                dve.wait_ge(S["dve_const"], 1)

            def index(ch):
                dve.wait_ge(S["pe_code"], 1)
                cd = bank[0][:, 0:E]
                neg, used = logit[:, 0, :], logit[:, 1, :]
                nc.vector.tensor_scalar(neg, cd, 0.0, float(N // 2), ALU.is_lt, ALU.add)
                ch.link(nc.vector.tensor_scalar(used, cd, 0.0, None, ALU.not_equal))
                ch.link(nc.vector.tensor_tensor(code, cd, neg, ALU.add))
                ch.link(nc.vector.tensor_tensor(code, code, used, ALU.mult))
                ch.link(nc.vector.tensor_scalar(used, used, -1.0, 1.0, ALU.mult, ALU.add))
                nc.vector.tensor_copy(gather_rows[:, :], code)
                nc.vector.scalar_tensor_tensor(scatter_rows[:, :], used, slot_dump[:, 0:1], code, ALU.mult, ALU.add).then_inc(S["dve_index"], 1)

            def rows_list(j, k, first):
                e = j * BODY + k
                if not first:
                    dve.wait_ge(dma_xe[k % XS], 16 * share(j, k, XS))
                    dve.wait_ge(S["act_ye"], e - XS + 1)
                nc.vector.tensor_copy(rows_now[:, k % XS:k % XS + 1], gather_rows[:, bass.ds(e, 1)]).then_inc(S["dve_rows_now"], 1)

            def body(i):
                Nx, _ = live(i, -1)
                Pr, Pfirst = live(i, 0)
                Q, Qfirst = live(i, 1)
                R, Rfirst = live(i, 2)
                flush, final = ending(i)
                ch = Chain(links_before(i))
                b = i - 2
                y_banks = (0, 1) if flush else (6, 7)
                gate_bank = 7 if flush else 0 if final else 2

                def add_table(b_, bank_):
                    dve.wait_ge(S["pe_table"], b_ + 1)
                    tb = table[:, :].rearrange("p g l e -> p (g l e)")
                    nc.vector.tensor_tensor(tb, tb, bank[bank_][:, :], ALU.add).then_inc(S["dve_table"], 1)

                def heads_norm(i):
                    dve.wait_ge(S["act_sq"], 2 * i)
                    ch.link(nc.vector.tensor_reduce(power, sq.rearrange("p t (h d) -> p (t h) d", d=DH), AX.X, ALU.add))
                    nc.vector.tensor_scalar(power, power, 4.0 / DH, 4.0 * EPS_NORM ** 2, ALU.mult, ALU.max).then_inc(S["dve_power"], 1)
                    dve.wait_ge(S["dve_power"], i)
                    if not live(i, 1)[1]:
                        dve.wait_ge(S["pool_un"], i - 1)
                    inverse_root(norm, power, ch, "dve_norm")

                if Q and not flush:
                    heads_norm(i)

                def output():
                    dve.wait_ge(S["pool_un"], i)
                    dve.wait_ge(S["act_o"], 2 * i)
                    if not Qfirst:
                        dve.wait_ge(S["pe_tro"], 2 * (i - 1))
                    nc.vector.tensor_tensor(on, o_sb, un, ALU.mult).then_inc(S["dve_on"], 1)


                def output_lo():
                    if not Qfirst:
                        dve.wait_ge(S["pe_wo"], 2 * (i - 1))
                    transposed_lo(oT_lo, oT_hi, (0, 1), "act_oT", 2 * (i - 1), "dve_oT")

                def output_stats():
                    y = [bank[y_banks[t // 2]][:, (t % 2) * D:(t % 2 + 1) * D] for t in range(T)]
                    norm_stats(y, stats2, mv2, ve2, nm2, ch, "dve_mv2", ("pe_wo", 2 * i), *([] if Qfirst else [("pool_r2", i - 1)]))

                def residual_stats(i):
                    x1 = at(resid, i - 1)
                    norm_stats([x1[:, t, :] for t in range(T)], stats3, mv3, ve3, nm3, ch, "dve_mv3", ("pool_x1", 2 * i), *([] if live(i, 1)[1] else [("pool_r3", i - 1)]))

                def rows_lo():
                    if not Rfirst:
                        dve.wait_ge(S["pe_up"], 3 * b)
                        dve.wait_ge(S["pe_gate"], b)
                    transposed_lo(x2T_lo, x2T_hi, (2, 3), "act_x2T", 2 * b, "dve_x2T")

                def hidden(j, b=b):
                    w = CHUNKS[j][1]
                    ba, bb = up_banks(j, b)
                    dve.wait_ge(S["act_tu"], 3 * b + j + 1)
                    if not Rfirst:
                        dve.wait_ge(S["pool_hT"], 3 * b)
                        dve.wait_ge(S["act_hT"], 3 * b)
                    ch.link(nc.vector.scalar_tensor_tensor(tu[0:w, j, :], tu[0:w, j, :], 1.0, bank[ba][0:w, :], ALU.add, ALU.mult))
                    nc.vector.scalar_tensor_tensor(hT[0:w, j, :], tu[0:w, j, :], 0.5, bank[bb][0:w, :], ALU.mult, ALU.mult).then_inc(S["dve_h"], 1)

                def onehots(b_, tiles_=range(T)):
                    if tiles_[0] == 0 and not Rfirst:
                        dve.wait_ge(S["pe_table"], b_)
                    for t in tiles_:
                        nc.vector.tensor_tensor(onehot_lo[:, t], lo_h[:, t:t + 1, :].to_broadcast([P, LO, E]), iota_lo[:, :, :], ALU.is_equal)
                        last = nc.vector.tensor_tensor(onehot_hi[:, t], hi_h[:, t].rearrange("p (g o e) -> p g o e", g=G, o=1).to_broadcast([P, G, HI, GE]), iota_hi[:, :, :, :], ALU.is_equal)
                    ch.link(last)
                    code_b = at(token_code, b_)
                    for t in tiles_:
                        last = nc.vector.tensor_scalar(onehot_lo[:, t], onehot_lo[:, t], code_b[:, t:t + 1], None, ALU.mult)
                    if tiles_[-1] == T - 1:
                        last.then_inc(S["dve_onehot"], 1)

                if flush:
                    residual_stats(i - 1)
                    output()
                    onehots(b - 1, (0, 1))
                    output_lo()
                    onehots(b - 1, (2, 3))
                    output_stats()
                if R and not final:
                    rows_lo()
                if Nx:
                    if isinstance(i, int):
                        for b_ in range(i + 1, B if i == PEEL - 1 else i + 2):
                            dve.wait_ge(dma_x[b_], 16)
                    xb = at(resid, i + 1)
                    norm_stats([xb[:, t, :] for t in range(T)], stats1, mv1, ve1, nm1, ch, "dve_mv1", ("pool_r1", i + 1))
                if Q and R and not flush:
                    output()
                if R:
                    dve.wait_ge(S["pe_gate"], b + 1)
                    lg = bank[gate_bank][:, 0:T * E].rearrange("p (t e) -> p t e", t=T)
                    ch.link(nc.vector.tensor_reduce(top, lg, AX.X, ALU.max))
                    nc.vector.tensor_tensor(logit, lg, top.rearrange("p (t o) -> p t o", o=1).to_broadcast([P, T, E]), ALU.subtract).then_inc(S["dve_logit"], 1)
                if final:
                    hidden(2, b - 1)
                elif R and not Rfirst:
                    add_table(i - 3, 6)
                if R:
                    dve.wait_ge(S["act_exp"], b + 1)
                    ch.link(nc.vector.tensor_reduce(expsum, logit, AX.X, ALU.add))
                    ch.link(nc.vector.reciprocal(expinv, expsum))
                    ch.link(nc.vector.tensor_tensor(padded[:, :, 0:E], logit, expinv.rearrange("p (t o) -> p t o", o=1).to_broadcast([P, T, E]), ALU.mult))
                    if not Rfirst:
                        dve.wait_ge(S["dma_rows"], 16 * b)
                    nc.vector.tensor_copy(xg[:, :, D:ROW], padded[:, :, 0:E]).then_inc(S["dve_scores"], 1)
                    if flush:
                        residual_stats(i)
                    for t in range(T):
                        last = nc.vector.max(top8[:, t, :], padded[:, t, :])
                    ch.link_apart(last)
                    for t in range(T):
                        last = nc.vector.match_replace(replaced[:, t, :], top8[:, t, :], padded[:, t, :], -1.0)
                    ch.link(last)
                    if not Rfirst:
                        dve.wait_ge(S["pe_pos"], b)
                    nc.vector.tensor_scalar(sel[:, :, :], replaced[:, :, 0:E], 0.0, None, ALU.is_lt).then_inc(S["dve_sel"], 1)
                    ch.link(nc.vector.tensor_scalar(penalty, replaced[:, :, 0:E], 0.0, float(N), ALU.is_ge, ALU.mult))
                if Pfirst:
                    late_weights()
                    token_codes()
                if Q and not R:
                    output()
                if Pr:
                    for c_ in range(2):
                        dve.wait_ge(S["act_th"], 2 * i + c_ + 1)
                        if not Pfirst:
                            dve.wait_ge(S["pool_un"], i)
                        nc.vector.scalar_tensor_tensor(tiles(u_sb, c_), tiles(th, c_), 1.0, bank[c_][:, :], ALU.add, ALU.mult).then_inc(S["dve_u"], 1)

                def slot_operands():
                    dve.wait_ge(S["dve_table"], B)
                    masked = y_sb.rearrange("p t d -> p (t d)")[:, 0:E * LO].rearrange("p (n e) -> p n e", e=GE)
                    ch.link(nc.vector.tensor_tensor(masked, table[:, :, :, :].rearrange("p g l e -> p (g l) e"),
                                                    own[:, :].rearrange("p (o e) -> p o e", o=1).to_broadcast([P, G * LO, GE]), ALU.mult))
                    own_codes = y_sb.rearrange("p t d -> p (t d)")[:, E * LO:E * LO + G * LO]
                    ch.link(nc.vector.tensor_reduce(own_codes, masked, AX.X, ALU.add))
                    nc.vector.tensor_tensor(slot_codes, own_codes.rearrange("p (g o l) -> p g o l", g=G, o=1).to_broadcast([P, G, HI, LO]),
                                            own_hi[:, :].rearrange("p (o h q) -> p o h q", o=1, q=1).to_broadcast([P, G, HI, LO]), ALU.mult).then_inc(S["dve_slots"], 1)

                if R and not final:
                    hidden(0)
                def own_blocks():
                    dve.wait_ge(S["pe_kv"], i + 1)
                    if not Pfirst:
                        dve.wait_ge(S["pe_out"], 2 * i)
                    else:
                        dve.wait_ge(S["pool_const2"], 1)
                    nc.vector.tensor_tensor(kv_sb, bank[3][:, 0:K * P].rearrange("p (k n) -> p k n", k=K),
                                            block_mask[:, :].rearrange("p (o n) -> p o n", o=1).to_broadcast([P, K, P]), ALU.mult).then_inc(S["dve_kv"], 1)

                if Pfirst:
                    own_blocks()
                if final:
                    add_table(b - 1, 1)
                if R:
                    dve.wait_ge(S["pe_pos"], b + 1)
                    nc.vector.tensor_tensor(posi[:, :, :], bank[2][:, 0:T * E].rearrange("p (t e) -> p t e", t=T), penalty, ALU.add).then_inc(S["dve_pos"], 1)
                def chosen_before():
                    ch.link(nc.vector.tensor_reduce(taken_now, sel[:, :, :].rearrange("p t e -> p e t"), AX.X, ALU.add))
                    dve.wait_ge(S["dve_pos"], 2 * b + 1)
                    nc.vector.tensor_tensor(taken[:, :], taken[:, :], taken_now, ALU.add).then_inc(S["dve_pos"], 1)

                if flush:
                    chosen_before()
                if R and not final:
                    hidden(1)
                if Q and not flush:
                    output_lo()
                if deferred(i):
                    own_blocks()
                if Nx:
                    dve.wait_ge(S["pe_u"], 2 * i + 2)
                    transposed_lo(xT_lo, xT_hi, (2, 3), "act_xT", 2 * (i + 1), "dve_xT")
                if R:
                    if not flush and not final:
                        hidden(2)
                    if not flush:
                        chosen_before()
                    nc.vector.tensor_scalar(lo_i[:, :, :], posi[:, :, :], LO - 1, None, ALU.bitwise_and)
                    ch.link(nc.vector.tensor_scalar(hi_i[:, :, :], posi[:, :, :], LO.bit_length() - 1, None, ALU.logical_shift_right))
                    nc.vector.tensor_copy(lo_h[:, :, :], lo_i[:, :, :])
                    ch.link(nc.vector.tensor_copy(hi_h[:, :, :], hi_i[:, :, :]))
                    if final:
                        onehots(b)
                        hidden(0)
                        add_table(b, 0)
                        slot_operands()
                        index(ch)
                        dve.wait_ge(S["dve_index"], 1)
                        for e in range(AHEAD):
                            rows_list(0, e, True)
                        hidden(1)
                        hidden(2)
                if Q and not flush:
                    output_stats()
                if Pr and not Pfirst and not deferred(i):
                    own_blocks()
                if deferred(i):
                    heads_norm(i + 1)
                if R and Q and not deferred(i):
                    onehots(b, range(T))
                if Q and not flush and not deferred(i):
                    residual_stats(i)
                assert ch.n == PER_N * Nx + PER_Q * Q + PER_R * R + SLOTS * final + (MOVED.get(i, 0) if isinstance(i, int) else 0)

            steps(dve, body)
            tail = Chain(links_before(B + 2) + SLOTS)

            def dest_list(j, k, first):
                e = j * BODY + k
                if not first:
                    dve.wait_ge(S[f"dma_scatter{k % 2}"], 16 * (share(j, k, 2) - 1))
                nc.vector.tensor_copy(dest_now[:, k % 4:k % 4 + 1], scatter_rows[:, bass.ds(e, 1)]).then_inc(S["dve_dest_now"], 1)

            def hidden_rows(j, k, first):
                e = j * BODY + k
                dve.wait_ge(S["act_silu"], e + 1)
                if not first:
                    dve.wait_ge(S["pe_hidT"], e - 1)
                nc.vector.tensor_tensor(hid[:, k % 2], silu_a[:, k % 2], bank[2 + k % 2][:, F:2 * F], ALU.mult).then_inc(S["dve_hid"], 1)

            dve.wait_ge(S["dma_rows"], 16 * B)
            dve.wait_ge(S["dve_index"], 1)

            def experts(j, k):
                known = isinstance(j, int)
                if not known or k + AHEAD < E:
                    rows_list(j, k + AHEAD, known and k + AHEAD < XS)
                if not known or k < E:
                    dest_list(j, k, known and k < 4)
                hidden_rows(j, k, known and k < 2)

            expert_steps(dve, experts, after=0)

            LAG = 3
            for n in range(CN + LAG):
                room, r_ = n % CS, (n - 1) % 2
                if n < CN:
                    dve.wait_ge(dma_s[room], 32 * (n // CS + 1))
                    if n >= CS:
                        dve.wait_ge(S["pool_fin"], n - CS + 1)
                    nc.vector.tensor_tensor(total[:, room], s0[:, room], s1[:, room], ALU.add).then_inc(S["dve_total"], 1)
                if 1 <= n <= CN:
                    used = [("pool_rc", n - 2)] if n >= 3 else []
                    wait_apart(dve, ("dve_link", tail.base + 2 * n - 1), *used)
                    for t in range(CT):
                        last = nc.vector.bn_aggr(mvc[:, t, :], statsc[:, t, :])
                    last.then_inc(S["dve_link"], 1)
                    dve.wait_ge(S["dve_link"], tail.base + 2 * n)
                    nc.vector.tensor_scalar(vec[:, r_, 0:CT], mvc[:, 0:CT, 1], EPS, None, ALU.add)
                    nc.vector.tensor_scalar(nmc[:, r_, 0:CT], mvc[:, 0:CT, 0], -1.0, None, ALU.mult).then_inc(S["dve_mvc"], 1)
                if n < CN:
                    wait_apart(dve, ("dve_total", n + 1))
                    for t in range(CT):
                        last = nc.vector.bn_stats(statsc[:, t, :], total[:, room, t, :])
                    last.then_inc(S["dve_link"], 1)
                if n >= LAG:
                    m_ = n - LAG
                    dve.wait_ge(S["act_cn"], m_ + 1)
                    if m_ >= CS:
                        dve.wait_ge(dma_out[m_ % CS], 16 * (m_ // CS))
                    nc.vector.tensor_tensor(fin[:, m_ % CS, 1], resid[:, m_ * CT // T, m_ * CT % T + 1], total[:, m_ % CS, 1], ALU.add).then_inc(S["dve_fin"], 1)

        @block.tensor
        def _(pe):
            def product(out_, pairs, start=True, stop=True):
                for n, ((ah, al), (bh, bl)) in enumerate(pairs):
                    first, last_ = start and n == 0, stop and n == len(pairs) - 1
                    nc.tensor.matmul(out_, ah, bh, start=first, stop=False)
                    nc.tensor.matmul(out_, ah, bl, start=False, stop=False)
                    last = nc.tensor.matmul(out_, al, bh, start=False, stop=last_)
                return last

            def transposes(src, banks, done):
                for c_ in range(K):
                    for t in range(T):
                        last = nc.tensor.transpose(bank[banks[c_]][:, tile_of(t)], src[:, t, c_ * P:(c_ + 1) * P], ident[:, :])
                    last.then_inc(S[done], 1)

            def parts(hi, lo, *index):
                return hi[index], lo[index]

            pe.wait_ge(S["pool_const"], 3)
            pe.wait_ge(S["pool_const2"], 1)
            pe.wait_ge(S["act_xn"], 1)
            transposes(xn, (2, 3), "pe_trx")
            ALL = slice(None)

            def down(b):
                pe.wait_ge(S["dve_h"], 3 * b + 3)
                pe.wait_ge(S["act_hT"], 3 * b + 3)
                pe.wait_ge(S["pool_hT"], 3 * b + 3)
                for t in range(T):
                    last = product(bank[4 + t // 2][:, (t % 2) * D:(t % 2 + 1) * D],
                                   [((hT_hi[0:w, j, tile_of(t)], hT_lo[0:w, j, tile_of(t)]), (s2_hi[0:w, j, :], s2_lo[0:w, j, :]))
                                    for j, (_, w) in enumerate(CHUNKS)])
                    if t % 2:
                        last.then_inc(S["pe_down"], 1)

            def body(i):
                Nx, _ = live(i, -1)
                Pr, Pfirst = live(i, 0)
                Q, Qfirst = live(i, 1)
                R, Rfirst = live(i, 2)
                flush, final = ending(i)
                Tb = R and not Rfirst
                b = i - 2
                y_banks = (0, 1) if flush else (6, 7)
                gate_bank = 7 if flush else 0 if final else 2

                def queue_table(b_, bank_):
                    pe.wait_ge(S["dve_onehot"], b_ + 1)
                    for g in range(G):
                        for t in range(T):
                            last = nc.tensor.matmul(bank[bank_][:, g * LO * GE:(g + 1) * LO * GE],
                                                    onehot_hi[:, t, g].rearrange("p h e -> p (h e)"), onehot_lo[:, t, :, g * GE:(g + 1) * GE],
                                                    start=(t == 0), stop=(t == T - 1))
                    last.then_inc(S["pe_table"], 1)

                def last_table():
                    if not final:
                        pe.wait_ge(S["act_yn"], 2 * (i - 1))
                    queue_table(i - 3, 1 if final else 6)

                def rows_T():
                    pe.wait_ge(S["act_xn2"], b + 1)
                    if Pr:
                        pe.wait_ge(S["act_q"], 2 * i + 2)
                    else:
                        pe.wait_ge(S["dve_pos"], 2 * b)
                        pe.wait_ge(S["dve_kv"], B)
                    transposes(xg, (2, 3), "pe_trx2")

                def up(j, b=b):
                    o, w = CHUNKS[j]
                    for half, bk in enumerate(up_banks(j, b)):
                        cols = slice(half * FS + o, half * FS + o + w)
                        last = product(bank[bk][0:w, :], [(parts(s13_hi, s13_lo, ALL, k, cols), parts(x2T_hi, x2T_lo, ALL, k, ALL)) for k in range(K)])
                    last.then_inc(S["pe_up"], 1)

                def logits():
                    if Rfirst:
                        pe.wait_ge(S["dma_wg"], 16)
                    pe.wait_ge(S["act_x2"], 2 * b + 2)
                    if not flush and not final:
                        pe.wait_ge(S["act_x2T"], 2 * b + 2)
                        pe.wait_ge(S["dve_x2T"], 2 * b + 2)
                    for t in range(T):
                        for k in range(K):
                            last = nc.tensor.matmul(bank[gate_bank][:, t * E:(t + 1) * E], x2T[:, k, tile_of(t)], gate[:, k, :], start=(k == 0), stop=(k == K - 1))
                    last.then_inc(S["pe_gate"], 1)

                def output_T():
                    pe.wait_ge(S["dve_on"], i)
                    if Pr:
                        pe.wait_ge(S["dve_u"], 2 * (i + 1))
                    else:
                        pe.wait_ge(S["act_o"], 2 * i)
                    transposes(on, (0, 1), "pe_tro")

                def output_product():
                    pe.wait_ge(S["act_oT"], 2 * i)
                    pe.wait_ge(S["dve_oT"], 2 * i)
                    if Qfirst:
                        pe.wait_ge(S["dve_w"], 5)
                    if R and not flush:
                        pe.wait_ge(S["dve_h"], 3 * b + 2)
                    for t in range(T):
                        last = product(bank[y_banks[t // 2]][:, (t % 2) * D:(t % 2 + 1) * D],
                                       [(parts(oT_hi, oT_lo, ALL, k, tile_of(t)), parts(w_hi, w_lo, ALL, k, slice(4 * D, 5 * D))) for k in range(K)])
                        if t % 2:
                            last.then_inc(S["pe_wo"], 1)

                def output_heads(i):
                    pe.wait_ge(S["act_q"], 2 * i)
                    pe.wait_ge(S["dve_kv"], i)
                    pe.wait_ge(S["dve_u"], 2 * i)
                    if not live(i, 1)[1]:
                        pe.wait_ge(S["act_oT"], 2 * (i - 1))
                        pe.wait_ge(S["dve_oT"], 2 * (i - 1))
                    for t in range(T):
                        for c_ in range(K):
                            at_ = (t % 2) * D + c_ * P
                            last = nc.tensor.matmul(bank[t // 2][:, at_:at_ + P], q_sb[:, c_, tile_of(t)], kv_sb[:, c_, :], start=True, stop=True)
                        if t % 2:
                            last.then_inc(S["pe_out"], 1)

                if Q and not flush:
                    output_heads(i)
                if Pr:
                    pe.wait_ge(S["act_xT"], 2 * i + 2)
                    pe.wait_ge(S["dve_xT"], 2 * i + 2)
                    if Pfirst:
                        pe.wait_ge(S["dve_w"], 1)
                    for c_ in range(K):
                        last = product(bank[2 + c_][:, :], [(parts(w_hi, w_lo, ALL, k, slice(c_ * P, (c_ + 1) * P)), parts(xT_hi, xT_lo, ALL, k, ALL)) for k in range(K)])
                        last.then_inc(S["pe_q"], 1)

                def keys_values(t):
                    if t < 2:
                        if Q:
                            pe.wait_ge(S["act_o"], 2 * (i - 1) + t + 1)
                    else:
                        pe.wait_ge(S["act_kv"], 4 * i + t - 1)
                    if Pfirst:
                        pe.wait_ge(S["dve_w"], 3)
                    last = product(bank[t % 2][:, :], [(parts(xT_hi, xT_lo, ALL, k, tile_of(t)), parts(w_hi, w_lo, ALL, k, slice(D, 3 * D))) for k in range(K)])
                    last.then_inc(S["pe_kvp"], 1)

                if Pr:
                    keys_values(0)
                    keys_values(1)
                def gates(half):
                    if Pfirst:
                        pe.wait_ge(S["dve_w"], 4)
                    pe.wait_ge(S["act_kv"], 4 * i + 3 + half)
                    for t in (2 * half, 2 * half + 1):
                        last = product(bank[half][:, (t % 2) * D:(t % 2 + 1) * D],
                                       [(parts(xT_hi, xT_lo, ALL, k, tile_of(t)), parts(w_hi, w_lo, ALL, k, slice(3 * D, 4 * D))) for k in range(K)])
                    last.then_inc(S["pe_u"], 1)

                if Pr:
                    keys_values(2)
                    keys_values(3)
                if flush:
                    output_T()
                    output_product()
                if R:
                    rows_T()
                if final:
                    pe.wait_ge(S["dve_h"], 3 * (b - 1) + 1)
                    up(2, b - 1)
                if Tb and Pr:
                    last_table()
                if Pr:
                    gates(0)
                if R:
                    logits()
                if flush:
                    last_table()
                    pe.wait_ge(S["act_x2T"], 2 * b + 2)
                    pe.wait_ge(S["dve_x2T"], 2 * b + 2)
                if Pr:
                    gates(1)
                def positions():
                    pe.wait_ge(S["dve_logit"], b + 1)
                    pe.wait_ge(S["dve_sel"], b + 1)
                    if not Rfirst:
                        pe.wait_ge(S["dve_pos"], 2 * b)
                    for t in range(T):
                        at_ = bank[2][:, t * E:(t + 1) * E]
                        nc.tensor.matmul(at_, before[:, :], sel[:, t, :], start=True, stop=False)
                        for t_ in range(t):
                            nc.tensor.matmul(at_, ones[:, :], sel[:, t_, :], start=False, stop=False)
                        last = nc.tensor.matmul(at_, ones[:, :], taken[:, :], start=False, stop=True)
                    last.then_inc(S["pe_pos"], 1)

                if final:
                    last_table()
                    pe.wait_ge(S["act_x2T"], 2 * b + 2)
                    pe.wait_ge(S["pool_x2T"], 2)
                    pe.wait_ge(S["dve_h"], 3 * (b - 1) + 2)
                    up(0)
                    positions()
                    down(b - 1)
                    pe.wait_ge(S["act_z"], 2 * b)
                    up(1)
                    queue_table(b, 0)
                if R and not final:
                    if not Rfirst:
                        pe.wait_ge(S["act_z"], 2 * b)
                    up(0)
                    if Tb:
                        pe.wait_ge(S["dve_table"], i - 2)
                    else:
                        pe.wait_ge(S["act_yn"], 2 * (i - 1))
                    if flush:
                        pe.wait_ge(S["dve_logit"], b + 1)
                    up(1)
                def blocks_kv():
                    pe.wait_ge(S["act_kv"], 4 * i + 4)
                    for c_ in range(K):
                        for t in range(T):
                            last = nc.tensor.matmul(bank[3][:, c_ * P:(c_ + 1) * P], k_sb[:, t, c_ * P:(c_ + 1) * P], v_sb[:, t, c_ * P:(c_ + 1) * P],
                                                    start=(t == 0), stop=(t == T - 1))
                    last.then_inc(S["pe_kv"], 1)

                if Pfirst:
                    blocks_kv()
                if R and not final:
                    positions()
                if deferred(i):
                    blocks_kv()
                if Q and not flush:
                    output_T()
                if Nx:
                    pe.wait_ge(S["act_xn"], i + 2)
                    if not R:
                        pe.wait_ge(S["act_q"], 2 * i + 2)
                    if Pfirst:
                        pe.wait_ge(S["dve_kv"], 1)
                    if R:
                        pe.wait_ge(S["dve_pos"], 2 * b + 1)
                    transposes(xn, (2, 3), "pe_trx")
                if R and not final:
                    if not flush:
                        pe.wait_ge(S["dve_h"], 3 * b + 1)
                        up(2)
                if Q and not flush:
                    output_product()
                if deferred(i):
                    output_heads(i + 1)
                elif Pr and not Pfirst:
                    if Nx:
                        pe.wait_ge(S["act_xT"], 2 * i + 4)
                        pe.wait_ge(S["dve_xT"], 2 * i + 4)
                    blocks_kv()
                if final:
                    pe.wait_ge(S["dve_h"], 3 * b + 1)
                    up(2)
                    pe.wait_ge(S["dve_slots"], 1)
                    for g in range(G):
                        last = nc.tensor.matmul(bank[0][:, g * GE:(g + 1) * GE], slot_codes[:, g].rearrange("p h l -> p (h l)"), own[:, :], start=True, stop=True)
                    last.then_inc(S["pe_code"], 1)
                if R and not flush and not final:
                    down(b)

            steps(pe, body)

            def tokens_T(j, k, first):
                e = j * BODY + k
                pe.wait_ge(dma_xe[k % XS], 16 * (share(j, k, XS) + 1))
                if not first:
                    pe.wait_ge(S["act_xeT"], e - 1)
                for c_ in range(K):
                    last = nc.tensor.transpose(bank[k % 2][:, c_ * P:(c_ + 1) * P], xe[:, k % XS, c_ * P:(c_ + 1) * P], ident[:, :])
                last.then_inc(S["pe_xeT"], 1)

            def expert_up(j, k, first):
                e = j * BODY + k
                slot = (k // 2) % WB
                pe.wait_ge(dma_w13[slot], 16 * (share(j, k, BODY) + 1))
                pe.wait_ge(S["act_xeT"], e + 1)
                if not first:
                    pe.wait_ge(S["dve_hid"], e - 1)
                for c_ in range(K):
                    last = nc.tensor.matmul(bank[2 + k % 2][:, 0:2 * F], xeT[:, k % 2, c_, :], w13_sb[slot][:, k % 2, c_, :], start=(c_ == 0), stop=(c_ == K - 1))
                last.then_inc(S["pe_eup"], 1)

            def hidden_T(j, k, first):
                e = j * BODY + k
                pe.wait_ge(S["dve_hid"], e + 1)
                if not first:
                    pe.wait_ge(S["act_hidT"], e - 1)
                for c_ in range(2):
                    last = nc.tensor.transpose(bank[4 + k % 2][0:FH, c_ * P:(c_ + 1) * P], hid[:, k % 2, c_ * FH:(c_ + 1) * FH], ident[:, :])
                last.then_inc(S["pe_hidT"], 1)

            def expert_down(j, k, first):
                e = j * BODY + k
                slot = (k // 2) % WB
                pe.wait_ge(dma_w2[slot], 16 * (share(j, k, BODY) + 1))
                pe.wait_ge(S["act_hidT"], e + 1)
                if not first:
                    pe.wait_ge(S["act_ye"], e - 1)
                for c_ in range(2):
                    last = nc.tensor.matmul(bank[6 + k % 2][:, 0:D], hidT[0:FH, k % 2, c_, :], w2_sb[slot][0:FH, k % 2, c_, :], start=(c_ == 0), stop=(c_ == 1))
                last.then_inc(S["pe_edown"], 1)

            pe.wait_ge(S["dve_index"], 1)
            tokens_T(0, 0, True)

            def experts(j, k):
                known = isinstance(j, int)
                if not known or k + 1 < E:
                    tokens_T(j, k + 1, known and k < 1)
                if not known or k < E:
                    expert_up(j, k, known and k < 2)
                if known and k == 0:
                    down(B - 1)
                if known and k == 1:
                    pe.wait_ge(S["act_z"], 2 * B)
                if not known or 1 <= k <= E:
                    hidden_T(j, k - 1, known and k < 3)
                if not known or k >= 2:
                    expert_down(j, k - 2, known and k < 4)

            expert_steps(pe, experts)


def kernel(L0_attn_x, L0_attn_Wq, L0_attn_Wk, L0_attn_Wv, L0_attn_Wu, L0_attn_Wo, L0_ffn_gate_w, L0_ffn_w1, L0_ffn_w2,
           L0_ffn_w3, L0_ffn_sw1, L0_ffn_sw2, L0_ffn_sw3):
    import concourse.bacc as bacc
    from concourse.bass_utils import run_bass_kernel_spmd

    def features_first(w):
        return np.asarray(w).T.reshape(K, P, -1).transpose(1, 0, 2)

    w1, w2, w3 = (np.asarray(w) for w in (L0_ffn_w1, L0_ffn_w2, L0_ffn_w3))
    both = np.concatenate([w1, w3], axis=1)
    arrays = {
        "x": L0_attn_x, "wq": L0_attn_Wq, "wk": L0_attn_Wk, "wv": L0_attn_Wv, "wu": L0_attn_Wu, "wo": L0_attn_Wo,
        "gate_w": features_first(L0_ffn_gate_w),
        "w13": both.transpose(2, 0, 1).reshape(K, P, E, 2 * F).transpose(1, 2, 0, 3),
        "w2": w2.transpose(2, 0, 1).reshape(2, FH, E, D).transpose(1, 2, 0, 3),
        "sw13": features_first(np.concatenate([np.asarray(L0_ffn_sw1), np.asarray(L0_ffn_sw3)], axis=0)),
        "sw2": np.asarray(L0_ffn_sw2).T,
    }
    arrays = {n: np.ascontiguousarray(a) for n, a in arrays.items()}
    nc = bacc.Bacc("TRN2", target_bir_lowering=False, num_devices=1)
    aps = [nc.dram_tensor(n, a.shape, mybir.dt.from_np(a.dtype), kind="ExternalInput").ap() for n, a in arrays.items()]
    result = nc.dram_tensor("result", (B, L, D), F32, kind="ExternalOutput").ap()
    build(nc, *aps, result)
    r = run_bass_kernel_spmd(nc, [arrays], core_ids=[0])
    return r.results[0]["result"]
```
